# Optimizing a Trainium2 kernel written in Bass

```python
import numpy as np
import jax
import jax.numpy as jnp

def _softmax(x, axis=-1):
    return jax.nn.softmax(x, axis=axis)

def _gelu(x):
    return jax.nn.gelu(x, approximate=True)

def _silu(x):
    return jax.nn.silu(x)

def _sigmoid(x):
    return jax.nn.sigmoid(x)

def _layernorm(x, axis=-1, eps=1e-05):
    m = jnp.mean(x, axis=axis, keepdims=True)
    v = jnp.var(x, axis=axis, keepdims=True)
    return (x - m) / jnp.sqrt(v + eps)

def _scatter_add(tgt, idx, src, axis=0):
    return tgt.at[idx].add(src)

def _segment_sum(src, seg, n):
    return jax.ops.segment_sum(src, seg, n)
kernel_name = 'mk_decoder_preln_d2_seqx_r4_88870f'

def setup_inputs(seed: int=0):
    np.random.seed(seed)
    _w = jnp.asarray

    def _rec_inputs():
        import jax
        import jax.numpy as jnp
        _rk = jax.random.key(seed)
        x = -0.0003929 + 0.9999 * jax.random.normal(jax.random.fold_in(_rk, 1), (16, 100, 256), jnp.float32)
        _lenS = 100 - jax.random.randint(jax.random.fold_in(_rk, 7), (16,), 0, max(1, 100 // 4) + 1, jnp.int32)
        _lenS2 = 361 - jax.random.randint(jax.random.fold_in(_rk, 8), (16,), 0, max(1, 361 // 4) + 1, jnp.int32)
        _ctx_512P = jax.random.normal(jax.random.fold_in(_rk, 11), (16, 16, 128), jnp.float32)
        _ctx_512c = jax.random.dirichlet(jax.random.fold_in(_rk, 511), 0.3 * jnp.ones((16,), jnp.float32), (16, 361))
        _ctx_512t = jnp.einsum('bsk,bkd->bsd', _ctx_512c, _ctx_512P)
        _ctx_512t = _ctx_512t * jax.lax.rsqrt(jnp.mean(jnp.square(_ctx_512t)) + 1e-12) * 0.953939
        ctx_512 = 4.13588e-05 + 0.999923 * (_ctx_512t + 0.3 * jax.random.normal(jax.random.fold_in(_rk, 611), (16, 361, 128), jnp.float32))
        return (x, ctx_512)
    x, ctx_512 = _rec_inputs()

    def _L0_attn_setup():
        import jax, jax.numpy as jnp
        import numpy as np
        import math
        B, N, D = (64, 128, 256)
        SHELL_DIM, RFF_DIM, ORDER = (64, 32, 4)
        CHARGE_COUPLING, SHELL_COUPLING = (1.0, 0.5)
        DIST_COUPLING, DIST_SCALE = (0.3, 10.0)
        COMBINED_DIM = 64

        def _forward(x, W_charge, b_charge, W_shell, b_shell, omega, rff_bias, W_combine, W_v, b_v, W_out, b_out, log_temp):
            b, n, d = x.shape
            q = jnp.tanh(x @ W_charge.T + b_charge)[..., 0]
            coeffs = jnp.asarray([(-CHARGE_COUPLING) ** m / math.factorial(m) for m in range(ORDER + 1)], dtype=x.dtype)
            mags = jnp.sqrt(jnp.abs(coeffs) + 1e-10)
            phi_c = mags * q[..., None] ** jnp.arange(ORDER + 1)
            shell = x @ W_shell.T + b_shell
            shell = shell / jnp.maximum(jnp.linalg.norm(shell, axis=-1, keepdims=True), 1e-12)
            proj = shell @ omega.T + rff_bias
            rff_scale = math.sqrt(2.0 / (2 * RFF_DIM)) * math.sqrt(math.exp(-SHELL_COUPLING))
            phi_s = jnp.concatenate([jnp.cos(proj), jnp.sin(proj)], axis=-1) * rff_scale
            tp = (phi_c[..., :, None] * phi_s[..., None, :]).reshape(b, n, -1)
            phi = tp @ W_combine.T
            idx = jnp.arange(n)
            T = jnp.exp(-DIST_COUPLING * jnp.abs(idx[:, None] - idx[None, :]).astype(x.dtype) / DIST_SCALE)
            temp = jax.nn.softplus(log_temp) + 0.1
            logits = jnp.einsum('bnd,bmd->bnm', phi, phi) * T / temp
            causal = idx[:, None] >= idx[None, :]
            logits = jnp.where(causal, logits, -jnp.inf)
            attn = jax.nn.softmax(logits, axis=-1)
            V = x @ W_v.T + b_v
            out = jnp.einsum('bnm,bmd->bnd', attn, V)
            return out @ W_out.T + b_out
        key = jax.random.key(seed)
        ks = jax.random.split(key, 12)
        s = 0.02
        inp = {'x': jax.random.normal(ks[0], (B, N, D), dtype=jnp.float32), 'W_charge': jax.random.normal(ks[1], (1, D), dtype=jnp.float32) * s, 'b_charge': jnp.zeros((1,), dtype=jnp.float32), 'W_shell': jax.random.normal(ks[2], (SHELL_DIM, D), dtype=jnp.float32) * s, 'b_shell': jnp.zeros((SHELL_DIM,), dtype=jnp.float32), 'omega': jax.random.normal(ks[3], (RFF_DIM, SHELL_DIM), dtype=jnp.float32) * math.sqrt(SHELL_COUPLING), 'rff_bias': jax.random.uniform(ks[4], (RFF_DIM,), dtype=jnp.float32) * (2.0 * math.pi), 'W_combine': jax.random.normal(ks[5], (COMBINED_DIM, (ORDER + 1) * 2 * RFF_DIM), dtype=jnp.float32) * s, 'W_v': jax.random.normal(ks[6], (D, D), dtype=jnp.float32) * s, 'b_v': jnp.zeros((D,), dtype=jnp.float32), 'W_out': jax.random.normal(ks[7], (D, D), dtype=jnp.float32) * s, 'b_out': jnp.zeros((D,), dtype=jnp.float32), 'log_temp': jnp.zeros((), dtype=jnp.float32)}
        return inp
    _L0_attn_all = _L0_attn_setup()
    _L0_attn_in = {k: v for k, v in _L0_attn_all.items() if k in ('W_charge', 'b_charge', 'W_shell', 'b_shell', 'omega', 'rff_bias', 'W_combine', 'W_v', 'b_v', 'W_out', 'b_out', 'log_temp')}
    del _L0_attn_all

    def _L0_xattn_setup():
        import jax, jax.numpy as jnp
        import numpy as np
        B, LQ, LK = (8, 512, 512)
        QD, KD, VD = (256, 128, 128)
        key = jax.random.key(seed)
        ks = jax.random.split(key, 9)
        s = 0.02
        return {'query': jax.random.normal(ks[0], (B, LQ, QD), jnp.float32), 'key': jax.random.normal(ks[1], (B, LK, KD), jnp.float32), 'value': jax.random.normal(ks[2], (B, LK, VD), jnp.float32), 'Wq': jax.random.normal(ks[3], (QD, QD), jnp.float32) * s, 'bq': jnp.zeros((QD,), jnp.float32), 'Wk': jax.random.normal(ks[4], (KD, QD), jnp.float32) * s, 'bk': jnp.zeros((QD,), jnp.float32), 'Wv': jax.random.normal(ks[5], (VD, QD), jnp.float32) * s, 'bv': jnp.zeros((QD,), jnp.float32)}
    _L0_xattn_all = _L0_xattn_setup()
    _L0_xattn_in = {k: v for k, v in _L0_xattn_all.items() if k in ('Wq', 'bq', 'Wk', 'bk', 'Wv', 'bv')}
    del _L0_xattn_all

    def _L0_ffn_setup():
        import jax, jax.numpy as jnp
        import numpy as np
        EMB = 256
        HID = 512
        HEADS = 16
        HEAD_DIM = EMB // HEADS
        EXPERTS = 8
        TOPK = 2
        EPS = 1e-05

        def layernorm(x, scale, shift):
            mean = jnp.mean(x, axis=-1, keepdims=True)
            var = jnp.mean((x - mean) ** 2, axis=-1, keepdims=True)
            return scale * (x - mean) / jnp.sqrt(var + EPS) + shift

        def attention(x, wq, wk, wv, wo, bo):
            b, t, _ = x.shape
            q = (x @ wq).reshape(b, t, HEADS, HEAD_DIM)
            k = (x @ wk).reshape(b, t, HEADS, HEAD_DIM)
            v = (x @ wv).reshape(b, t, HEADS, HEAD_DIM)
            scores = jnp.einsum('bqhd,bkhd->bhqk', q, k)
            mask = jnp.arange(t)[:, None] < jnp.arange(t)[None, :]
            scores = jnp.where(mask, -jnp.inf, scores)
            attn = jax.nn.softmax(scores / np.sqrt(HEAD_DIM), axis=-1)
            ctx = jnp.einsum('bhqk,bkhd->bqhd', attn, v).reshape(b, t, EMB)
            return ctx @ wo + bo

        def moe_ff(x, gate_w, w1, w2, w3):
            b, t, d = x.shape
            xf = x.reshape(b * t, d)
            scores = xf @ gate_w
            topk_scores, topk_idx = jax.lax.top_k(scores, TOPK)
            topk_probs = jax.nn.softmax(topk_scores, axis=-1)
            weight = jnp.sum(jax.nn.one_hot(topk_idx, EXPERTS, dtype=xf.dtype) * topk_probs[..., None], axis=1)
            h = jax.nn.silu(jnp.einsum('td,edh->eth', xf, w1)) * jnp.einsum('td,edh->eth', xf, w2)
            out_e = jnp.einsum('eth,ehd->etd', h, w3)
            out = jnp.einsum('etd,te->td', out_e, weight)
            return out.reshape(b, t, d)
        key = jax.random.key(seed)
        ks = jax.random.split(key, 12)
        s = lambda k, shape, fan: jax.random.normal(k, shape, jnp.float32) / np.sqrt(fan)
        return {'x': jax.random.normal(ks[0], (2, 512, EMB), jnp.float32), 'ln1_scale': jnp.ones((EMB,), jnp.float32), 'ln1_shift': jnp.zeros((EMB,), jnp.float32), 'wq': s(ks[1], (EMB, EMB), EMB), 'wk': s(ks[2], (EMB, EMB), EMB), 'wv': s(ks[3], (EMB, EMB), EMB), 'wo': s(ks[4], (EMB, EMB), EMB), 'bo': jnp.zeros((EMB,), jnp.float32), 'ln2_scale': jnp.ones((EMB,), jnp.float32), 'ln2_shift': jnp.zeros((EMB,), jnp.float32), 'gate_w': s(ks[5], (EMB, EXPERTS), EMB), 'w1': s(ks[6], (EXPERTS, EMB, HID), EMB), 'w2': s(ks[7], (EXPERTS, EMB, HID), EMB), 'w3': s(ks[8], (EXPERTS, HID, EMB), HID)}
    _L0_ffn_all = _L0_ffn_setup()
    _L0_ffn_in = {k: v for k, v in _L0_ffn_all.items() if k in ('ln1_scale', 'ln1_shift', 'wq', 'wk', 'wv', 'wo', 'bo', 'ln2_scale', 'ln2_shift', 'gate_w', 'w1', 'w2', 'w3')}
    del _L0_ffn_all

    def _L1_attn_setup():
        import jax, jax.numpy as jnp
        import numpy as np
        EPS_RMS = 1e-06
        EPS_Q = 1e-05

        def rmsnorm(x, g):
            var = jnp.mean(x * x, axis=-1, keepdims=True)
            return g * (x * jax.lax.rsqrt(var + EPS_RMS))

        def activation_quant(x):
            scale = 127.0 / jnp.clip(jnp.max(jnp.abs(x), axis=-1, keepdims=True), EPS_Q)
            y = jnp.clip(jnp.round(x * scale), -128, 127) / scale
            return x + jax.lax.stop_gradient(y - x)

        def weight_quant(w):
            s = jnp.clip(jnp.mean(jnp.abs(w)), EPS_Q)
            y = jnp.clip(jnp.round(w / s), -1, 1) * s
            return w + jax.lax.stop_gradient(y - w)

        def bitlinear(x, w, g):
            xq = activation_quant(rmsnorm(x, g))
            wq = weight_quant(w)
            return jnp.einsum('btc,oc->bto', xq, wq)
        key = jax.random.key(seed)
        ks = jax.random.split(key, 5)
        B, T, C = (2, 512, 256)
        std = 1.0 / np.sqrt(C)
        inp = {'x': jax.random.normal(ks[0], (B, T, C), jnp.float32), 'wq': jax.random.normal(ks[1], (C, C), jnp.float32) * std, 'wk': jax.random.normal(ks[2], (C, C), jnp.float32) * std, 'wv': jax.random.normal(ks[3], (C, C), jnp.float32) * std, 'wo': jax.random.normal(ks[4], (C, C), jnp.float32) * std, 'gq': jnp.ones((C,), jnp.float32), 'gk': jnp.ones((C,), jnp.float32), 'gv': jnp.ones((C,), jnp.float32), 'go': jnp.ones((C,), jnp.float32)}
        return inp
    _L1_attn_all = _L1_attn_setup()
    _L1_attn_in = {k: v for k, v in _L1_attn_all.items() if k in ('wq', 'wk', 'wv', 'wo', 'gq', 'gk', 'gv', 'go')}
    del _L1_attn_all

    def _L1_xattn_setup():
        import jax, jax.numpy as jnp
        import numpy as np
        HEADS = 16
        D_MODEL = 256
        IMG_MODEL = 128
        D_K = D_MODEL // HEADS
        key = jax.random.key(seed)
        ks = jax.random.split(key, 12)
        B, LQ, LKV = (8, 512, 256)
        s_dm = 1.0 / np.sqrt(D_MODEL)
        s_im = 1.0 / np.sqrt(IMG_MODEL)
        return {'q': jax.random.normal(ks[0], (B, LQ, D_MODEL), jnp.float32), 'k': jax.random.normal(ks[1], (B, LKV, IMG_MODEL), jnp.float32), 'v': jax.random.normal(ks[2], (B, LKV, IMG_MODEL), jnp.float32), 'Wq': jax.random.normal(ks[3], (D_MODEL, D_MODEL), jnp.float32) * s_dm, 'bq': jnp.zeros((D_MODEL,), jnp.float32), 'Wk': jax.random.normal(ks[4], (IMG_MODEL, D_MODEL), jnp.float32) * s_im, 'bk': jnp.zeros((D_MODEL,), jnp.float32), 'Wv': jax.random.normal(ks[5], (IMG_MODEL, D_MODEL), jnp.float32) * s_im, 'bv': jnp.zeros((D_MODEL,), jnp.float32), 'Wo': jax.random.normal(ks[6], (D_MODEL, D_MODEL), jnp.float32) * s_dm, 'bo': jnp.zeros((D_MODEL,), jnp.float32)}
    _L1_xattn_all = _L1_xattn_setup()
    _L1_xattn_in = {k: v for k, v in _L1_xattn_all.items() if k in ('Wq', 'bq', 'Wk', 'bk', 'Wv', 'bv', 'Wo', 'bo')}
    del _L1_xattn_all

    def _L1_ffn_setup():
        import jax, jax.numpy as jnp
        import numpy as np
        E = 8
        TOP_K = 2
        H = 256
        I = 128
        SI = 128
        B, S = (4, 1024)
        key = jax.random.key(seed)
        ks = jax.random.split(key, 8)
        sc_h = 1.0 / np.sqrt(H)
        sc_i = 1.0 / np.sqrt(I)
        return {'hidden_states': jax.random.normal(ks[0], (B, S, H), jnp.float32), 'gate_w': jax.random.normal(ks[1], (E, H), jnp.float32) * sc_h, 'Wg': jax.random.normal(ks[2], (E, H, I), jnp.float32) * sc_h, 'Wu': jax.random.normal(ks[3], (E, H, I), jnp.float32) * sc_h, 'Wd': jax.random.normal(ks[4], (E, I, H), jnp.float32) * sc_i, 'sWg': jax.random.normal(ks[5], (H, SI), jnp.float32) * sc_h, 'sWu': jax.random.normal(ks[6], (H, SI), jnp.float32) * sc_h, 'sWd': jax.random.normal(ks[7], (SI, H), jnp.float32) * sc_i}
    _L1_ffn_all = _L1_ffn_setup()
    _L1_ffn_in = {k: v for k, v in _L1_ffn_all.items() if k in ('gate_w', 'Wg', 'Wu', 'Wd', 'sWg', 'sWu', 'sWd')}
    del _L1_ffn_all
    return {'x': x, 'ctx_512': ctx_512, 'L0_attn_W_charge': _L0_attn_in['W_charge'], 'L0_attn_b_charge': _L0_attn_in['b_charge'], 'L0_attn_W_shell': _L0_attn_in['W_shell'], 'L0_attn_b_shell': _L0_attn_in['b_shell'], 'L0_attn_omega': _L0_attn_in['omega'], 'L0_attn_rff_bias': _L0_attn_in['rff_bias'], 'L0_attn_W_combine': _L0_attn_in['W_combine'], 'L0_attn_W_v': _L0_attn_in['W_v'], 'L0_attn_b_v': _L0_attn_in['b_v'], 'L0_attn_W_out': _L0_attn_in['W_out'], 'L0_attn_b_out': _L0_attn_in['b_out'], 'L0_attn_log_temp': _L0_attn_in['log_temp'], 'L0_xattn_Wq': _L0_xattn_in['Wq'], 'L0_xattn_bq': _L0_xattn_in['bq'], 'L0_xattn_Wk': _L0_xattn_in['Wk'], 'L0_xattn_bk': _L0_xattn_in['bk'], 'L0_xattn_Wv': _L0_xattn_in['Wv'], 'L0_xattn_bv': _L0_xattn_in['bv'], 'L0_ffn_ln1_scale': _L0_ffn_in['ln1_scale'], 'L0_ffn_ln1_shift': _L0_ffn_in['ln1_shift'], 'L0_ffn_wq': _L0_ffn_in['wq'], 'L0_ffn_wk': _L0_ffn_in['wk'], 'L0_ffn_wv': _L0_ffn_in['wv'], 'L0_ffn_wo': _L0_ffn_in['wo'], 'L0_ffn_bo': _L0_ffn_in['bo'], 'L0_ffn_ln2_scale': _L0_ffn_in['ln2_scale'], 'L0_ffn_ln2_shift': _L0_ffn_in['ln2_shift'], 'L0_ffn_gate_w': _L0_ffn_in['gate_w'], 'L0_ffn_w1': _L0_ffn_in['w1'], 'L0_ffn_w2': _L0_ffn_in['w2'], 'L0_ffn_w3': _L0_ffn_in['w3'], 'L1_attn_wq': _L1_attn_in['wq'], 'L1_attn_wk': _L1_attn_in['wk'], 'L1_attn_wv': _L1_attn_in['wv'], 'L1_attn_wo': _L1_attn_in['wo'], 'L1_attn_gq': _L1_attn_in['gq'], 'L1_attn_gk': _L1_attn_in['gk'], 'L1_attn_gv': _L1_attn_in['gv'], 'L1_attn_go': _L1_attn_in['go'], 'L1_xattn_Wq': _L1_xattn_in['Wq'], 'L1_xattn_bq': _L1_xattn_in['bq'], 'L1_xattn_Wk': _L1_xattn_in['Wk'], 'L1_xattn_bk': _L1_xattn_in['bk'], 'L1_xattn_Wv': _L1_xattn_in['Wv'], 'L1_xattn_bv': _L1_xattn_in['bv'], 'L1_xattn_Wo': _L1_xattn_in['Wo'], 'L1_xattn_bo': _L1_xattn_in['bo'], 'L1_ffn_gate_w': _L1_ffn_in['gate_w'], 'L1_ffn_Wg': _L1_ffn_in['Wg'], 'L1_ffn_Wu': _L1_ffn_in['Wu'], 'L1_ffn_Wd': _L1_ffn_in['Wd'], 'L1_ffn_sWg': _L1_ffn_in['sWg'], 'L1_ffn_sWu': _L1_ffn_in['sWu'], 'L1_ffn_sWd': _L1_ffn_in['sWd']}

def reference(x, ctx_512, L0_attn_W_charge, L0_attn_b_charge, L0_attn_W_shell, L0_attn_b_shell, L0_attn_omega, L0_attn_rff_bias, L0_attn_W_combine, L0_attn_W_v, L0_attn_b_v, L0_attn_W_out, L0_attn_b_out, L0_attn_log_temp, L0_xattn_Wq, L0_xattn_bq, L0_xattn_Wk, L0_xattn_bk, L0_xattn_Wv, L0_xattn_bv, L0_ffn_ln1_scale, L0_ffn_ln1_shift, L0_ffn_wq, L0_ffn_wk, L0_ffn_wv, L0_ffn_wo, L0_ffn_bo, L0_ffn_ln2_scale, L0_ffn_ln2_shift, L0_ffn_gate_w, L0_ffn_w1, L0_ffn_w2, L0_ffn_w3, L1_attn_wq, L1_attn_wk, L1_attn_wv, L1_attn_wo, L1_attn_gq, L1_attn_gk, L1_attn_gv, L1_attn_go, L1_xattn_Wq, L1_xattn_bq, L1_xattn_Wk, L1_xattn_bk, L1_xattn_Wv, L1_xattn_bv, L1_xattn_Wo, L1_xattn_bo, L1_ffn_gate_w, L1_ffn_Wg, L1_ffn_Wu, L1_ffn_Wd, L1_ffn_sWg, L1_ffn_sWu, L1_ffn_sWd):
    import jax
    import jax.numpy as jnp

    def _L0_attn_ref(x, W_charge, b_charge, W_shell, b_shell, omega, rff_bias, W_combine, W_v, b_v, W_out, b_out, log_temp):
        import jax, jax.numpy as jnp
        import numpy as np
        import math
        B, N, D = (64, 128, 256)
        SHELL_DIM, RFF_DIM, ORDER = (64, 32, 4)
        CHARGE_COUPLING, SHELL_COUPLING = (1.0, 0.5)
        DIST_COUPLING, DIST_SCALE = (0.3, 10.0)
        COMBINED_DIM = 64

        def _forward(x, W_charge, b_charge, W_shell, b_shell, omega, rff_bias, W_combine, W_v, b_v, W_out, b_out, log_temp):
            b, n, d = x.shape
            q = jnp.tanh(x @ W_charge.T + b_charge)[..., 0]
            coeffs = jnp.asarray([(-CHARGE_COUPLING) ** m / math.factorial(m) for m in range(ORDER + 1)], dtype=x.dtype)
            mags = jnp.sqrt(jnp.abs(coeffs) + 1e-10)
            phi_c = mags * q[..., None] ** jnp.arange(ORDER + 1)
            shell = x @ W_shell.T + b_shell
            shell = shell / jnp.maximum(jnp.linalg.norm(shell, axis=-1, keepdims=True), 1e-12)
            proj = shell @ omega.T + rff_bias
            rff_scale = math.sqrt(2.0 / (2 * RFF_DIM)) * math.sqrt(math.exp(-SHELL_COUPLING))
            phi_s = jnp.concatenate([jnp.cos(proj), jnp.sin(proj)], axis=-1) * rff_scale
            tp = (phi_c[..., :, None] * phi_s[..., None, :]).reshape(b, n, -1)
            phi = tp @ W_combine.T
            idx = jnp.arange(n)
            T = jnp.exp(-DIST_COUPLING * jnp.abs(idx[:, None] - idx[None, :]).astype(x.dtype) / DIST_SCALE)
            temp = jax.nn.softplus(log_temp) + 0.1
            logits = jnp.einsum('bnd,bmd->bnm', phi, phi) * T / temp
            causal = idx[:, None] >= idx[None, :]
            logits = jnp.where(causal, logits, -jnp.inf)
            attn = jax.nn.softmax(logits, axis=-1)
            V = x @ W_v.T + b_v
            out = jnp.einsum('bnm,bmd->bnd', attn, V)
            return out @ W_out.T + b_out
        return _forward(x, W_charge, b_charge, W_shell, b_shell, omega, rff_bias, W_combine, W_v, b_v, W_out, b_out, log_temp)

    def _L0_xattn_ref(query, key, value, Wq, bq, Wk, bk, Wv, bv):
        import jax, jax.numpy as jnp
        import numpy as np
        B, LQ, LK = (8, 512, 512)
        QD, KD, VD = (256, 128, 128)
        q = jnp.einsum('bld,de->ble', query, Wq) + bq
        k = jnp.einsum('bld,de->ble', key, Wk) + bk
        v = jnp.einsum('bld,de->ble', value, Wv) + bv
        scores = jnp.einsum('bqe,bke->bqk', q, k)
        attn = jax.nn.softmax(scores, axis=-1)
        out = jnp.einsum('bqk,bke->bqe', attn, v)
        return out

    def _L0_ffn_ref(x, ln1_scale, ln1_shift, wq, wk, wv, wo, bo, ln2_scale, ln2_shift, gate_w, w1, w2, w3):
        import jax, jax.numpy as jnp
        import numpy as np
        EMB = 256
        HID = 512
        HEADS = 16
        HEAD_DIM = EMB // HEADS
        EXPERTS = 8
        TOPK = 2
        EPS = 1e-05

        def layernorm(x, scale, shift):
            mean = jnp.mean(x, axis=-1, keepdims=True)
            var = jnp.mean((x - mean) ** 2, axis=-1, keepdims=True)
            return scale * (x - mean) / jnp.sqrt(var + EPS) + shift

        def attention(x, wq, wk, wv, wo, bo):
            b, t, _ = x.shape
            q = (x @ wq).reshape(b, t, HEADS, HEAD_DIM)
            k = (x @ wk).reshape(b, t, HEADS, HEAD_DIM)
            v = (x @ wv).reshape(b, t, HEADS, HEAD_DIM)
            scores = jnp.einsum('bqhd,bkhd->bhqk', q, k)
            mask = jnp.arange(t)[:, None] < jnp.arange(t)[None, :]
            scores = jnp.where(mask, -jnp.inf, scores)
            attn = jax.nn.softmax(scores / np.sqrt(HEAD_DIM), axis=-1)
            ctx = jnp.einsum('bhqk,bkhd->bqhd', attn, v).reshape(b, t, EMB)
            return ctx @ wo + bo

        def moe_ff(x, gate_w, w1, w2, w3):
            b, t, d = x.shape
            xf = x.reshape(b * t, d)
            scores = xf @ gate_w
            topk_scores, topk_idx = jax.lax.top_k(scores, TOPK)
            topk_probs = jax.nn.softmax(topk_scores, axis=-1)
            weight = jnp.sum(jax.nn.one_hot(topk_idx, EXPERTS, dtype=xf.dtype) * topk_probs[..., None], axis=1)
            h = jax.nn.silu(jnp.einsum('td,edh->eth', xf, w1)) * jnp.einsum('td,edh->eth', xf, w2)
            out_e = jnp.einsum('eth,ehd->etd', h, w3)
            out = jnp.einsum('etd,te->td', out_e, weight)
            return out.reshape(b, t, d)
        h = layernorm(x, ln1_scale, ln1_shift)
        x = x + attention(h, wq, wk, wv, wo, bo)
        h = layernorm(x, ln2_scale, ln2_shift)
        x = x + moe_ff(h, gate_w, w1, w2, w3)
        return x

    def _L1_attn_ref(x, wq, wk, wv, wo, gq, gk, gv, go):
        import jax, jax.numpy as jnp
        import numpy as np
        EPS_RMS = 1e-06
        EPS_Q = 1e-05

        def rmsnorm(x, g):
            var = jnp.mean(x * x, axis=-1, keepdims=True)
            return g * (x * jax.lax.rsqrt(var + EPS_RMS))

        def activation_quant(x):
            scale = 127.0 / jnp.clip(jnp.max(jnp.abs(x), axis=-1, keepdims=True), EPS_Q)
            y = jnp.clip(jnp.round(x * scale), -128, 127) / scale
            return x + jax.lax.stop_gradient(y - x)

        def weight_quant(w):
            s = jnp.clip(jnp.mean(jnp.abs(w)), EPS_Q)
            y = jnp.clip(jnp.round(w / s), -1, 1) * s
            return w + jax.lax.stop_gradient(y - w)

        def bitlinear(x, w, g):
            xq = activation_quant(rmsnorm(x, g))
            wq = weight_quant(w)
            return jnp.einsum('btc,oc->bto', xq, wq)
        B, T, C = x.shape
        n_head = 16
        head_dim = C // n_head
        q = bitlinear(x, wq, gq).reshape(B, T, n_head, head_dim).transpose(0, 2, 1, 3)
        k = bitlinear(x, wk, gk).reshape(B, T, n_head, head_dim).transpose(0, 2, 1, 3)
        v = bitlinear(x, wv, gv).reshape(B, T, n_head, head_dim).transpose(0, 2, 1, 3)
        att = jnp.einsum('bhqd,bhkd->bhqk', q, k) * (1.0 / np.sqrt(head_dim))
        causal = jnp.tril(jnp.ones((T, T), dtype=bool))
        att = jnp.where(causal[None, None], att, -jnp.inf)
        att = jax.nn.softmax(att, axis=-1)
        y = jnp.einsum('bhqk,bhkd->bhqd', att, v)
        y = y.transpose(0, 2, 1, 3).reshape(B, T, C)
        return bitlinear(y, wo, go)

    def _L1_xattn_ref(q, k, v, Wq, bq, Wk, bk, Wv, bv, Wo, bo):
        import jax, jax.numpy as jnp
        import numpy as np
        HEADS = 16
        D_MODEL = 256
        IMG_MODEL = 128
        D_K = D_MODEL // HEADS
        B, LQ, _ = q.shape
        LKV = k.shape[1]
        qh = (q @ Wq + bq).reshape(B, LQ, HEADS, D_K).transpose(0, 2, 1, 3)
        kh = (k @ Wk + bk).reshape(B, LKV, HEADS, D_K).transpose(0, 2, 1, 3)
        vh = (v @ Wv + bv).reshape(B, LKV, HEADS, D_K).transpose(0, 2, 1, 3)
        scale = 1.0 / np.sqrt(D_K)
        scores = jnp.einsum('bhqd,bhkd->bhqk', qh, kh) * scale
        attn = jax.nn.softmax(scores, axis=-1)
        out = jnp.einsum('bhqk,bhkd->bhqd', attn, vh)
        concat = out.transpose(0, 2, 1, 3).reshape(B, LQ, D_MODEL)
        return concat @ Wo + bo

    def _L1_ffn_ref(hidden_states, gate_w, Wg, Wu, Wd, sWg, sWu, sWd):
        import jax, jax.numpy as jnp
        import numpy as np
        E = 8
        TOP_K = 2
        H = 256
        I = 128
        SI = 128
        B, S = (4, 1024)
        b, s, h = hidden_states.shape
        x = hidden_states.reshape(-1, h)
        logits = x.astype(jnp.float32) @ gate_w.T
        scores = jax.nn.softmax(logits, axis=-1)
        topk_w, topk_idx = jax.lax.top_k(scores, TOP_K)
        topk_w = topk_w / (topk_w.sum(-1, keepdims=True) + 1e-20)
        cw = (jax.nn.one_hot(topk_idx, E, dtype=topk_w.dtype) * topk_w[..., None]).sum(1)
        g = jnp.einsum('th,ehi->tei', x, Wg)
        u = jnp.einsum('th,ehi->tei', x, Wu)
        inter = jax.nn.gelu(g, approximate=False) * u
        y = jnp.einsum('tei,te,eih->th', inter, cw.astype(x.dtype), Wd)
        sh = jax.nn.gelu(x @ sWg, approximate=False) * (x @ sWu) @ sWd
        return (y + sh).reshape(b, s, h)
    x = x + _L0_attn_ref(_layernorm(x, axis=-1), L0_attn_W_charge, L0_attn_b_charge, L0_attn_W_shell, L0_attn_b_shell, L0_attn_omega, L0_attn_rff_bias, L0_attn_W_combine, L0_attn_W_v, L0_attn_b_v, L0_attn_W_out, L0_attn_b_out, L0_attn_log_temp)
    x = x + _L0_xattn_ref(_layernorm(x, axis=-1), ctx_512, ctx_512, L0_xattn_Wq, L0_xattn_bq, L0_xattn_Wk, L0_xattn_bk, L0_xattn_Wv, L0_xattn_bv)
    x = x + _L0_ffn_ref(_layernorm(x, axis=-1), L0_ffn_ln1_scale, L0_ffn_ln1_shift, L0_ffn_wq, L0_ffn_wk, L0_ffn_wv, L0_ffn_wo, L0_ffn_bo, L0_ffn_ln2_scale, L0_ffn_ln2_shift, L0_ffn_gate_w, L0_ffn_w1, L0_ffn_w2, L0_ffn_w3)
    x = x + _L1_attn_ref(_layernorm(x, axis=-1), L1_attn_wq, L1_attn_wk, L1_attn_wv, L1_attn_wo, L1_attn_gq, L1_attn_gk, L1_attn_gv, L1_attn_go)
    x = x + _L1_xattn_ref(_layernorm(x, axis=-1), ctx_512, ctx_512, L1_xattn_Wq, L1_xattn_bq, L1_xattn_Wk, L1_xattn_bk, L1_xattn_Wv, L1_xattn_bv, L1_xattn_Wo, L1_xattn_bo)
    x = x + _L1_ffn_ref(_layernorm(x, axis=-1), L1_ffn_gate_w, L1_ffn_Wg, L1_ffn_Wu, L1_ffn_Wd, L1_ffn_sWg, L1_ffn_sWu, L1_ffn_sWd)
    return x

_drawn_inputs = setup_inputs


def setup_inputs(seed=0):
    import zlib

    import numpy as np

    out = dict(_drawn_inputs(seed))
    spreads = {'L0_attn_b_shell': (0.0, 2.0),
     'L0_attn_b_v': (0.0, 0.1),
     'L0_attn_b_out': (0.0, 0.1),
     'L0_xattn_bq': (0.0, 0.1),
     'L0_xattn_bk': (0.0, 2.0),
     'L0_xattn_bv': (0.0, 0.1),
     'L0_ffn_ln1_scale': (1.0, 0.2),
     'L0_ffn_ln1_shift': (0.0, 0.1),
     'L0_ffn_bo': (0.0, 0.1),
     'L0_ffn_ln2_scale': (1.0, 0.2),
     'L0_ffn_ln2_shift': (0.0, 0.1),
     'L1_attn_gq': (1.0, 0.559),
     'L1_attn_gk': (1.0, 0.2),
     'L1_attn_gv': (1.0, 0.2),
     'L1_attn_go': (1.0, 0.2),
     'L1_xattn_bq': (0.0, 0.49),
     'L1_xattn_bk': (0.0, 2.0),
     'L1_xattn_bv': (0.0, 0.1),
     'L1_xattn_bo': (0.0, 0.1)}
    factors = {'L0_attn_W_charge': 8.0,
     'L0_attn_W_shell': 8.0,
     'L0_attn_omega': 8.0,
     'L0_attn_rff_bias': 8.0,
     'L0_attn_W_combine': 8.0}
    for name, (base, spread) in spreads.items():
        noise = np.random.default_rng([zlib.crc32(name.encode()), seed]).standard_normal(out[name].shape)
        drawn = base * np.exp(spread * noise) if base else spread * noise
        out[name] = jnp.asarray(drawn.astype(out[name].dtype))
    for name, factor in factors.items():
        out[name] = (out[name] * factor).astype(out[name].dtype)
    return out
```

```python
import math
from contextlib import ExitStack

import numpy as np

import concourse.bass as bass
from concourse import mybir

ACT = mybir.ActivationFunctionType
ALU = mybir.AluOpType
F32 = mybir.dt.float32
BF16 = mybir.dt.bfloat16
AX = mybir.AxisListType.X

NSEQ, S, D = 16, 100, 256
NB = 4
NG = NSEQ // NB
NT = NB * S
P = 128
DC = D // P
LC, DX = 361, 128
KC = 3
KW = 121
LP = KC * KW
NH, HD = 16, 16
HC = NH // DC
SH, RF, ORD = 64, 32, 5
E0, HID0 = 8, 512
E1, HID1 = 9, 128
MC0 = HID0 // P
W0 = DC * HID0 * 2 + MC0 * D
EPS = 1e-5
EPS_RMS = 1e-6
MAGIC = 12582912.0
TWO_PI_HI = 6.28125
TWO_PI_LO = 2 * math.pi - TWO_PI_HI
NEG = -1e30
MAGS = [math.sqrt(abs((-1.0) ** m / math.factorial(m)) + 1e-10) for m in range(ORD)]
RFF_SCALE = math.sqrt(2.0 / (2 * RF)) * math.sqrt(math.exp(-0.5))
PHI_SCALE2 = (MAGS[0] * RFF_SCALE) ** 2

WCOLS = [("A_in", DC * 321), ("A_omega", P), ("A_comb", 320), ("A_out", DC * D),
         ("B_q", DC * D), ("B_kT", DC * DX), ("B_bk", DC), ("B_v", D),
         ("C_q", DC * D), ("C_k", DC * D), ("C_v", DC * D), ("C_o", DC * D), ("D_gate", DC * 8),
         ("F_q", DC * D), ("F_k", D), ("F_v", D), ("F_o", DC * D), ("G_gate", DC * 8),
         ("cols", 24)]
WOFF, _o = {}, 0
for _n, _w in WCOLS:
    WOFF[_n] = (_o, _w)
    _o += _w
NW = _o
COLS = {"rb": 0, "half_pi": 1, "B_bq": 2, "C_s": 4, "C_b": 6, "D_s": 8, "D_b": 10, "F_bq": 12, "F_bk": 14,
        "log_temp": 16}
RCOLS = [("A_in", 321), ("A_out", D), ("B_v", D), ("C_o", D), ("F_v", D), ("F_o", D),
         ("gq", D), ("gk", D), ("gv", D), ("go", D)]
ROFF, _o = {}, 0
for _n, _w in RCOLS:
    ROFF[_n] = (_o, _w)
    _o += _w
NR = _o
CCOLS = [("ident", P), ("ones", P), ("decay", S), ("causal", S), ("head", HC), ("before", 64), ("mhalf", 8), ("eps", 4)]
COFF, _o = {}, 0
for _n, _w in CCOLS:
    COFF[_n] = (_o, _w)
    _o += _w
NCST = _o
VU = 2 * HC * P
NVU = 6


class Signal:

    def __init__(self, sem, per, credit=0):
        self.sem, self.per, self.credit = sem, per, credit

    def at(self, it, k=1):
        return it * self.per + (k + self.credit)

    def free(self, it, k=1):
        return it * self.per + k


def decoder(nc, x_d, ctxT_d, ctx_d, w_d, r_d, c_d, wq_d, e0_d, e1_d, out_d):
    with ExitStack() as ctx:
        def sb(name, shape, dt=F32):
            return ctx.enter_context(nc.sbuf_tensor(name, shape, dt))

        def sig(name, per=1, credit=0):
            return Signal(ctx.enter_context(nc.semaphore(name)), per, credit)

        ps = ctx.enter_context(nc.psum_tensor("ps", [P, 8, 512], F32))

        wt = sb("wt", [P, NW])
        rows = sb("rows", [P, NR])
        cst = sb("cst", [P, NCST])
        wtern = sb("wtern", [P, 4, DC, D], BF16)
        experts = sb("experts", [P, 2 * W0 + 768])
        xall = sb("xall", [S, NSEQ, D])
        hT_all = sb("hT_all", [P, DC, NG * NT])
        gates_all = sb("gates_all", [S, NSEQ, 8])
        spread = sb("spread", [P, NVU, VU])
        probs = sb("probs", [S, 2, 800])
        probsT = sb("probsT", [P, 2, 800])
        headbd = sb("headbd", [P, 2, HC, S])
        xin = sb("xin", [S, NB, D])
        x = sb("x", [S, NB, D])
        y = sb("y", [S, NB, D])
        xn = sb("xn", [S, NB, D])
        hT = sb("hT", [P, DC, NT])
        qT = sb("qT", [P, DC, NT])
        kT = sb("kT", [P, 2, DC * LC + 80])
        ctxT = sb("ctxT", [P, NB, LP])
        identb = sb("identb", [P, P], BF16)
        causalb = sb("causalb", [S, NB, S], BF16)
        small = sb("small", [P, 512])
        xqT = sb("xqT", [P, DC, NT], BF16)
        xq = sb("xq", [S, NB, D], BF16)

        def wv(name, chunks=None, rows_=P):
            o, n = WOFF[name]
            v = wt[0:rows_, o:o + n]
            return v.rearrange("p (c n) -> p c n", c=chunks) if chunks else v

        def col(name, c=0, p=P):
            o = WOFF["cols"][0] + COLS[name] + c
            return wt[0:p, o:o + 1]

        def row(name, p=S):
            o, n = ROFF[name]
            return rows[0:p, o:o + n]

        def cs(name, p=P):
            o, n = COFF[name]
            return cst[0:p, o:o + n]

        ident = cs("ident")
        identS = ident[0:S, 0:S]
        scr = spread[:, 2:6, :].rearrange("p u n -> p (u n)")
        a_in = scr[0:S, 0:NB * 321].rearrange("p (b n) -> p b n", b=NB)
        a_sqw = scr[0:S, 1300:1300 + NB * P].rearrange("p (b n) -> p b n", b=NB)
        a_sq = a_sqw[:, :, 0:SH]
        a_shT = scr[0:SH, 1900:2300]
        a_ang = scr[0:SH, 2300:2700]
        a_lg = scr[0:S, 2300:2700].rearrange("p (b n) -> p b n", b=NB)
        a_k = scr[0:SH, 2700:3100]
        a_trig = scr[0:SH, 3100:3500]
        a_phiw = scr[0:S, 3500:3500 + NB * P].rearrange("p (b n) -> p b n", b=NB)
        a_phi = a_phiw[:, :, 0:SH]
        a_phiT = scr[0:SH, 7460:7860]
        ctxk = scr[0:KW, 4300:4300 + NB * KC * DX].rearrange("p (b c n) -> p b c n", b=NB, c=KC)
        b_e = scr[0:S, 5900:5900 + NB * LP].rearrange("p (b n) -> p b n", b=NB)
        b_eT = scr[0:KW, 0:NB * KC * S].rearrange("p (b n) -> p b n", b=NB)
        decay = scr[0:S, 7360:7460]
        c_v = scr[0:S, 0:NB * D].rearrange("p (b n) -> p b n", b=NB)
        hid = spread[:, 0:2, :].rearrange("p u n -> p (u n)")[:, 0:2 * MC0 * NT].rearrange(
            "p (s c n) -> p s c n", s=2, c=MC0)
        silu = spread[:, 4, 0:2 * NT].rearrange("p (s n) -> p s n", s=2)
        f_e = probs[:].rearrange("p s n -> p (s n)")[:, 0:4 * LP].rearrange("p (s i n) -> p s i n", s=2, i=2)
        f_eT = probsT[0:KW].rearrange("p s n -> p (s n)")[:, 0:4 * KC * S].rearrange(
            "p (s i n) -> p s i n", s=2, i=2)
        g_hid, g_act = probsT[:, :, 0:NT], probsT[:, :, NT:2 * NT]
        sm_o = [0]

        def smt(n, p=S, shape=None):
            v = small[0:p, sm_o[0]:sm_o[0] + n]
            sm_o[0] += n
            return v.rearrange("p (b n) -> p b n", b=shape) if shape else v

        stats = smt(NB * 6, shape=NB)
        mv = smt(NB * 2, shape=NB)
        var_e, r1, r2, t1 = smt(4), smt(4), smt(4), smt(4)
        a_ss, a_rn, a_q, a_nm, a_sum, a_rs = smt(4), smt(4), smt(4), smt(4), smt(4), smt(4)
        b_qbk, b_mx, b_nm, b_sum, b_rs = smt(4), smt(4), smt(4), smt(4), smt(4)
        h_nm = smt(32, shape=2)
        h_sum = smt(64, shape=NB)
        h_rs = smt(64, shape=NB)
        g_s, g_e, g_rank = smt(32, shape=NB), smt(32, shape=NB), smt(32, shape=NB)
        g_m, g_r = smt(4), smt(4)
        wsum, wscale, wrecip = smt(4, P), smt(4, P), smt(4, P)
        tempc = smt(4, P)
        q_am, q_sc, q_isc = smt(4), smt(4), smt(12, shape=3)
        bq4 = smt(2, P)
        assert sm_o[0] <= 512

        ld = {n: sig("ld_" + n) for n in ("wt", "rows", "cst", "wq", "x", "ctxT", "ctxk", "ctxT3", "e1", "out")}
        ld_e0 = [sig(f"ld_e0_{i}") for i in range(2)]
        prep_abs = sig("prep_abs")
        prep_sum = sig("prep_sum")
        prep_b = sig("prep_b")
        prep_t = sig("prep_t")
        prep_e = sig("prep_e")
        x_free = sig("x_free")
        tern_go = sig("tern_go")
        names = {}

        def stage(prefix, table):
            for n, per in table.items():
                names[prefix + n] = sig(prefix + n, per)

        def shared(name, per, phase1, phase3):
            sem = ctx.enter_context(nc.semaphore(name))
            for i, p in enumerate(phase1):
                names[f"{p}_{name}"] = Signal(sem, per * len(phase1), per * i)
            for i, p in enumerate(phase3):
                names[f"{p}_{name}"] = Signal(sem, per * len(phase3), per * (NG * len(phase1) + i))

        for n, per, stages3 in (("mv", 1, "EFG"), ("rstd", 1, "EFG"), ("xn", 1, "FG"), ("hTp", 2, "FG"),
                                ("hT", 2, "FG")):
            shared(n, per, "ABCD", stages3)
        shared("out", 1, "ABC", "EF")
        shared("x", 1, "ABC", "F")
        shared("xb", 1, "ABC", "F")
        for n, per in {"qTp": 2, "qT": 2, "kTp": 2, "kT": 2, "vp": 1, "v": 1, "bd": 8, "vs": 4, "s": 8, "sub": 8,
                       "e": 8, "pTp": 8, "pT": 8, "av": 8, "rs": 1, "rx": 1, "rTp": 2, "rT": 2,
                       "yT": 1}.items():
            shared(n, per, "C", "E")
        for n in ("gs", "gm", "ge", "g"):
            shared(n, 1, "D", "G")
        stage("A_", {n: 1 for n in ("in_p", "in", "ss", "rn", "q", "shn", "shTp", "shT", "angp", "ang", "trig",
                                    "comb", "phi", "phiTp", "phiT", "lg", "nm", "e", "p", "pTp", "pT", "oTp", "oT")})
        stage("B_", {"qTp": 2, "qT": 2, "kqTp": 1, "kqT": 1, "qbkp": 1, "s": 1, "nm": 1, "e": 1,
                     "p": 1, "pTp": 1, "pT": 1, "pT2": 1, "oTp": 1, "oT": 1})
        stage("E_", {"xq": 4, "xqTp": 4, "xqT": 4, "bc": 2, "bcp": 2, "sc": 2, "ytp": 1, "ssr": 1, "sso": 1})
        stage("F_", {"qTp": 2, "qT": 2, "kvp": 20, "kv": 20, "bd": 8, "s": 32, "nm": 32, "e": 32, "pTp": 32,
                     "pT": 32, "av": 32, "o": 4, "rs": 1, "rx": 1, "rTp": 2, "rT": 2, "yT": 1})
        stage("G_", {"h": 9, "act": 9, "hid": 9, "o": 9, "acc": 9})
        m_h = sig("m_h", 4 * 8)
        m_act = sig("m_act", 4 * 8)
        m_hid = sig("m_hid", 4 * 8, credit=2)
        m_out = sig("m_out", 8, credit=8)
        m_acc = sig("m_acc", 8, credit=2)

        def W(e, name, it, k=1):
            s = names[name]
            e.wait_ge(s.sem, s.at(it, k))

        def inc(ins, name):
            ins.then_inc(names[name].sem, 1)

        def bank(b, p=P, n=512, lo=0):
            return ps[0:p, b, lo:lo + n]

        def norm_dve(e, pre, it, src, xn_out, second=False):
            for b in range(NB):
                e.bn_stats(stats[:, b, :], src[:, b, :])
            e.drain()
            for b in range(NB):
                ins = e.bn_aggr(mv[:, b, :], stats[:, b, :])
            inc(ins, pre + "mv")
            e.drain()
            W(e, pre + "rstd", it)
            for b in range(NB):
                ins = e.tensor_scalar(xn_out[:, b, :], src[:, b, :], mv[:, b, 0:1], r1[:, b:b + 1],
                                      ALU.subtract, ALU.mult)
            return ins

        def norm_pool(e, pre, it, eps2=None, fold=False):
            W(e, pre + "mv", it)
            e.tensor_tensor(var_e, mv[:, :, 1], cs("eps", S), ALU.add)
            e.drain()
            ins = e.tensor_tensor(r1, var_e, cs("mhalf", S)[:, 0:4], ALU.pow)
            if eps2 is not None:
                e.drain()
                e.tensor_tensor(t1, r1, r1, ALU.mult)
                e.drain()
                e.tensor_tensor(t1, t1, mv[:, :, 1], ALU.mult)
                e.drain()
                e.tensor_scalar(t1, t1, eps2, None, ALU.add)
                e.drain()
                ins = e.tensor_tensor(r2, t1, cs("mhalf", S)[:, 0:4], ALU.pow)
                if fold:
                    e.drain()
                    ins = e.tensor_tensor(r1, r1, r2, ALU.mult)
            inc(ins, pre + "rstd")

        def toT_pe(e, src, name, b0=0):
            for c in range(DC):
                for b in range(NB):
                    ins = e.transpose(ps[:, b0 + c, b * S:(b + 1) * S], src[:, b, c * P:(c + 1) * P], identS)
                inc(ins, name)

        def toT_act(e, dst, pname, name, it, b0=0, scale=None, bias=None):
            for c in range(DC):
                W(e, pname, it, c + 1)
                if scale:
                    ins = e.activation(dst[:, c, :], bank(b0 + c, n=NT), ACT.Identity,
                                       scale=col(scale, c), bias=col(bias, c))
                else:
                    ins = e.activation(dst[:, c, :], bank(b0 + c, n=NT), ACT.Copy)
                inc(ins, name)

        def projT_pe(e, w, src, m, b):
            for c in range(DC):
                ins = e.matmul(bank(b, n=NT), w[:, c, m * P:(m + 1) * P], src[:, c, :],
                               start=(c == 0), stop=(c == DC - 1))
            return ins

        def proj_pe(e, w, srcT, b0, name, n=D):
            for b in range(NB):
                for c in range(DC):
                    ins = e.matmul(ps[0:S, b0 + b // 2, (b % 2) * D:(b % 2) * D + n],
                                   srcT[:, c, b * S:(b + 1) * S], w[:, c, 0:n],
                                   start=(c == 0), stop=(c == DC - 1))
            inc(ins, name)

        def pair(b0, p=S):
            return ps[0:p, b0:b0 + 2, :].rearrange("p a (b n) -> p (a b) n", b=2)

        def diag(unit, p):
            base = spread[0:p, unit, :]
            return bass.AP(tensor=base.tensor, offset=base.offset,
                           ap=[list(base.ap[0]), [HC * P, DC], [P + HD, HC], [1, HD]])

        def window(unit, p, c, h):
            return spread[0:p, unit, (c * HC + h) * P:(c * HC + h + 1) * P]

        def self_pe(e, pre, it, vready):
            def scores(u):
                b, c = divmod(u, 2)
                W(e, pre + "bd", it, u + 1)
                if u >= 2:
                    W(e, pre + "sub", it, u - 1)
                for i in range(2):
                    o = bank(2 * (u % 2) + i, S, 4 * S)
                    e.matmul(o, qT[:, c, b * S:(b + 1) * S],
                             headbd[:, u % 2, 4 * i:4 * i + 4, :].rearrange("p h n -> p (h n)"),
                             start=True, stop=False)
                    ins = e.matmul(o, identb[0:S, 0:S], causalb[:].rearrange("p h n -> p (h n)"),
                                   start=False, stop=True)
                inc(ins, pre + "s")

            def turn(u):
                W(e, pre + "e", it, u + 1)
                if u >= 1:
                    W(e, pre + "pT", it, u)
                for h in range(HC):
                    ins = e.transpose(ps[0:S, 4 + h // 4, (h % 4) * S:(h % 4 + 1) * S],
                                      probs[:, u % 2, h * S:(h + 1) * S], identS)
                inc(ins, pre + "pTp")

            def values(u):
                b, c = divmod(u, 2)
                W(e, pre + "pT", it, u + 1)
                W(e, pre + "vs", it, b + 1)
                for h in range(HC):
                    ins = e.matmul(ps[:, 6 + c, b * S:(b + 1) * S], window(b % 2, S, c, h),
                                   probsT[0:S, u % 2, h * S:(h + 1) * S], start=(h == 0), stop=(h == HC - 1))
                inc(ins, pre + "av")

            for u in range(2 * NB + 2):
                if u < 2 * NB:
                    scores(u)
                if 1 <= u <= 2 * NB:
                    turn(u - 1)
                if u >= 2:
                    values(u - 2)
            W(e, pre + "rx", it)
            toT_pe(e, xn, pre + "rTp", 0)

        def self_dve(e, pre, it):
            def shift(u):
                W(e, pre + "s", it, u + 1)
                sc = ps[0:S, 2 * (u % 2):2 * (u % 2) + 2, 0:4 * S].rearrange("p a (h n) -> p a h n", h=4)
                nm = h_nm[:, u % 2, 0:HC].rearrange("p (a h) -> p a h", a=2)
                e.tensor_reduce(nm, sc, AX, ALU.max)
                e.drain()
                if u >= 2:
                    W(e, pre + "pTp", it, u - 1)
                for i in range(2):
                    ins = e.tensor_tensor(
                        probs[:, u % 2, i * 4 * S:(i + 1) * 4 * S].rearrange("p (h n) -> p h n", h=4),
                        sc[:, i, :, :], nm[:, i, :].unsqueeze(2).broadcast_to([S, 4, S]), ALU.subtract)
                inc(ins, pre + "sub")

            def total(u):
                b, c = divmod(u, 2)
                W(e, pre + "e", it, u + 1)
                e.tensor_reduce(h_sum[:, b, c * HC:(c + 1) * HC],
                                probs[:, u % 2, :].rearrange("p (h n) -> p h n", h=HC), AX, ALU.add)

            for u in range(2 * NB + 1):
                if u < 2 * NB:
                    shift(u)
                if u >= 1:
                    total(u - 1)
            e.drain()
            inc(e.reciprocal(h_rs, h_sum), pre + "rs")

        def self_act(e, pre, it):
            def expo(u):
                W(e, pre + "sub", it, u + 1)
                inc(e.activation(probs[:, u % 2, :], probs[:, u % 2, :], ACT.Exp), pre + "e")

            def evac(u):
                W(e, pre + "pTp", it, u + 1)
                if u >= 2:
                    W(e, pre + "av", it, u - 1)
                ins = e.activation(probsT[0:S, u % 2, :].rearrange("p (a n) -> p a n", a=2),
                                   ps[0:S, 4:6, 0:4 * S], ACT.Copy)
                inc(ins, pre + "pT")

            for u in range(2 * NB + 1):
                if u < 2 * NB:
                    expo(u)
                if u >= 1:
                    evac(u - 1)

        def self_pool(e, pre, it, vsrc):
            for u in range(2 * NB):
                b, c = divmod(u, 2)
                if u == 0:
                    W(e, pre + "kT", it, 2)
                if u >= 2:
                    W(e, pre + "s", it, u - 1)
                inc(e.tensor_tensor(headbd[:, u % 2],
                                    kT[:, 0, c * NT + b * S:c * NT + (b + 1) * S].unsqueeze(1).broadcast_to([P, HC, S]),
                                    cs("head").unsqueeze(2).broadcast_to([P, HC, S]), ALU.mult), pre + "bd")
                if c == 0:
                    if b == 0:
                        W(e, pre + "v", it)
                    if b >= 2:
                        W(e, pre + "av", it, 2 * (b - 1))
                    inc(e.tensor_tensor(diag(b % 2, S), vsrc[:, b, :].rearrange("p (c h d) -> p c h d", c=DC, h=HC),
                                        cs("ones", S)[:, 0:1].unsqueeze(2).unsqueeze(3).broadcast_to([S, DC, HC, HD]),
                                        ALU.mult), pre + "vs")
            W(e, pre + "rs", it)
            inc(e.tensor_tensor(xn[:].rearrange("p b (h d) -> p b h d", d=HD),
                                  h_rs.unsqueeze(3).broadcast_to([S, NB, NH, HD]),
                                  cs("ones", S)[:, 0:1].unsqueeze(2).unsqueeze(3).broadcast_to([S, NB, NH, HD]),
                                  ALU.mult), pre + "rx")

        def recipT_act(e, pre, it):
            toT_act(e, hT, pre + "rTp", pre + "rT", it, 0)

        def gate_pe(e, pre, it, w, srcT):
            for b in range(NB):
                for c in range(DC):
                    ins = e.matmul(ps[0:S, 3, b * 8:(b + 1) * 8], srcT(c, b), w[:, c, :],
                                   start=(c == 0), stop=(c == DC - 1))
            inc(ins, pre + "gs")

        def gate_act(e, pre, it):
            W(e, pre + "gm", it)
            inc(e.activation(g_e, g_e, ACT.Exp), pre + "ge")

        def gate_dve(e, pre, it, probs_first, out_gates):
            W(e, pre + "gs", it)
            e.tensor_scalar(g_s, ps[0:S, 3, 0:32].rearrange("p (b n) -> p b n", b=NB), 1.0, None, ALU.mult)
            e.drain()
            e.tensor_reduce(g_m, g_s, AX, ALU.max)
            e.drain()
            bc = lambda v: v.unsqueeze(2).broadcast_to([S, NB, 8])
            inc(e.tensor_tensor(g_e, g_s, bc(g_m), ALU.subtract), pre + "gm")
            W(e, pre + "ge", it)
            if probs_first:
                e.tensor_reduce(g_m, g_e, AX, ALU.add)
                e.drain()
                e.reciprocal(g_r, g_m)
                e.drain()
                e.tensor_tensor(g_e, g_e, bc(g_r), ALU.mult)
                e.drain()
            key = g_e if probs_first else g_s
            sh = [S, NB, 8, 8]
            mine = key.unsqueeze(3).broadcast_to(sh)
            other = key.unsqueeze(2).broadcast_to(sh)
            cmp = y[:, 0, 0:256].rearrange("p (b e f) -> p b e f", b=NB, e=8)
            eq = y[:, 1, 0:256].rearrange("p (b e f) -> p b e f", b=NB, e=8)
            before = cs("before", S).rearrange("p (e f) -> p e f", e=8).unsqueeze(1).broadcast_to(sh)
            e.tensor_tensor(cmp, other, mine, ALU.is_gt)
            e.tensor_tensor(eq, other, mine, ALU.is_equal)
            e.drain()
            e.tensor_tensor(eq, eq, before, ALU.mult)
            e.drain()
            e.tensor_tensor(cmp, cmp, eq, ALU.add)
            e.drain()
            e.tensor_reduce(g_rank, cmp, AX, ALU.add)
            e.drain()
            e.scalar_tensor_tensor(g_e, g_rank, 1.5, g_e, ALU.is_lt, ALU.mult)
            e.drain()
            e.tensor_reduce(g_m, g_e, AX, ALU.add)
            e.drain()
            if probs_first:
                e.tensor_scalar(g_m, g_m, 1e-20, None, ALU.add)
                e.drain()
            e.reciprocal(g_r, g_m)
            e.drain()
            inc(e.tensor_tensor(out_gates, g_e, bc(g_r), ALU.mult), pre + "g")

        block = ctx.enter_context(nc.Block())

        @block.sync
        def _(e):
            def load_group(g):
                e.dma_start(xin[:], x_d[g]).then_inc(ld["x"].sem, 16)
                e.dma_start(ctxT[:], ctxT_d[g]).then_inc(ld["ctxT"].sem, 16)
                e.dma_start(ctxk, ctx_d[g]).then_inc(ld["ctxk"].sem, 16)

            e.dma_start(xin[:], x_d[0]).then_inc(ld["x"].sem, 16)
            e.dma_start(cst[:], c_d).then_inc(ld["cst"].sem, 16)
            e.dma_start(wt[:], w_d).then_inc(ld["wt"].sem, 16)
            e.dma_start(rows[:], r_d).then_inc(ld["rows"].sem, 16)
            e.dma_start(ctxT[:], ctxT_d[0]).then_inc(ld["ctxT"].sem, 16)
            e.dma_start(ctxk, ctx_d[0]).then_inc(ld["ctxk"].sem, 16)
            e.dma_start(experts[:, 0:4 * DC * D], wq_d).then_inc(ld["wq"].sem, 16)
            with e.Fori(0, NG - 1) as g:
                W(e, "B_oTp", g)
                load_group(g + 1)
            e.wait_ge(tern_go.sem, 1)
            with e.Fori(0, E0 // 2) as ep:
                for s in range(2):
                    e.wait_ge(m_out.sem, m_out.free(ep, NG * (s + 1)))
                    e.dma_start(experts[:, s * W0:(s + 1) * W0], e0_d[2 * ep + s]).then_inc(ld_e0[s].sem, 16)
            W(e, "B_oTp", NG - 1)
            e.dma_start(ctxT[:], ctxT_d[0]).then_inc(ld["ctxT3"].sem, 16)
            e.wait_ge(m_out.sem, m_out.at(E0 // 2 - 1, 2 * NG))
            e.dma_start(experts[:, 0:E1 * 768], e1_d).then_inc(ld["e1"].sem, 16)
            e.sem_inc(x_free.sem, 1)
            with e.Fori(0, NG - 1) as g:
                W(e, "F_kvp", g, 5 * NB)
                e.dma_start(ctxT[:], ctxT_d[g + 1]).then_inc(ld["ctxT3"].sem, 16)
                W(e, "G_acc", g, E1)
                e.dma_start(out_d[g], x[:]).then_inc(ld["out"].sem, 16)
                e.wait_ge(ld["out"].sem, g * 16 + 16)
                e.sem_inc(x_free.sem, 1)
            W(e, "G_acc", NG - 1, E1)
            e.dma_start(out_d[NG - 1], x[:]).then_inc(ld["out"].sem, 16)
            e.wait_ge(ld["out"].sem, NG * 16)

        @block.tensor
        def _(e):
            e.wait_ge(ld["cst"].sem, 16)
            e.wait_ge(prep_abs.sem, 1)
            inc_ = e.matmul(bank(0, n=4), cs("ones"), wsum, start=True, stop=True)
            inc_.then_inc(prep_sum.sem, 1)
            e.wait_ge(ld["wt"].sem, 16)
            e.wait_ge(prep_b.sem, 1)
            with e.Fori(0, NG) as g:
                W(e, "A_xn", g)
                toT_pe(e, xn, "A_hTp")
                W(e, "A_hT", g, 2)
                w = wv("A_in", DC)
                for b in range(NB):
                    for c in range(DC):
                        ins = e.matmul(bank(2 + b, S, 321), hT[:, c, b * S:(b + 1) * S], w[:, c, :],
                                       start=(c == 0), stop=(c == DC - 1))
                inc(ins, "A_in_p")
                W(e, "A_shn", g)
                for b in range(NB):
                    ins = e.transpose(ps[:, 0, b * S:(b + 1) * S], a_sqw[:, b, :], identS)
                inc(ins, "A_shTp")
                W(e, "A_shT", g)
                inc(e.matmul(bank(1, n=NT), wv("A_omega", rows_=SH), a_shT, start=True, stop=True), "A_angp")
                W(e, "A_trig", g)
                for b in range(NB):
                    ins = e.matmul(bank(2 + b, S, 320), a_trig[:, b * S:(b + 1) * S], wv("A_comb", rows_=SH),
                                   start=True, stop=True)
                inc(ins, "A_comb")
                W(e, "A_phi", g)
                for b in range(NB):
                    ins = e.transpose(ps[:, 0, b * S:(b + 1) * S], a_phiw[:, b, :], identS)
                inc(ins, "A_phiTp")
                W(e, "A_phiT", g)
                for b in range(NB):
                    pb = a_phiT[:, b * S:(b + 1) * S]
                    ins = e.matmul(ps[0:S, 1, b * S:(b + 1) * S], pb, pb, start=True, stop=True)
                inc(ins, "A_lg")
                W(e, "A_p", g)
                for b in range(NB):
                    ins = e.transpose(ps[0:S, 0, b * S:(b + 1) * S], a_lg[:, b, :], identS)
                inc(ins, "A_pTp")
                W(e, "A_pT", g)
                for c in range(DC):
                    for b in range(NB):
                        ins = e.matmul(ps[:, 2 + c, b * S:(b + 1) * S], a_in[:, b, 65 + c * P:65 + (c + 1) * P],
                                       probsT[0:S, 0, b * S:(b + 1) * S], start=True, stop=True)
                inc(ins, "A_oTp")
                W(e, "A_oT", g)
                proj_pe(e, wv("A_out", DC), qT, 4, "A_out")
                W(e, "B_xn", g)
                toT_pe(e, xn, "B_hTp")
                W(e, "B_hT", g, 2)
                for m in range(DC):
                    inc(projT_pe(e, wv("B_q", DC), hT, m, 2 + m), "B_qTp")
                W(e, "B_qT", g, 2)
                for c in range(DC):
                    ins = e.matmul(bank(0, n=NT), wv("B_kT", DC)[:, c, :], qT[:, c, :], start=(c == 0), stop=(c == DC - 1))
                inc(ins, "B_kqTp")
                for b in range(NB):
                    for c in range(DC):
                        ins = e.matmul(ps[0:S, 1, b:b + 1], qT[:, c, b * S:(b + 1) * S], wv("B_bk", DC)[:, c, :],
                                       start=(c == 0), stop=(c == DC - 1))
                inc(ins, "B_qbkp")
                W(e, "B_kqT", g)
                e.wait_ge(ld["ctxT"].sem, g * 16 + 16)
                for b in range(NB):
                    ins = e.matmul(bank(4 + b, S, LC), hT[:, 0, b * S:(b + 1) * S], ctxT[:, b, 0:LC],
                                   start=True, stop=True)
                inc(ins, "B_s")
                W(e, "B_p", g)
                for b in range(NB):
                    for k in range(KC):
                        ins = e.transpose(ps[0:KW, b, k * S:(k + 1) * S], b_e[:, b, k * KW:(k + 1) * KW], identS)
                inc(ins, "B_pTp")
                W(e, "B_pT", g)
                W(e, "B_pT2", g)
                e.wait_ge(ld["ctxk"].sem, g * 16 + 16)
                for b in range(NB):
                    for k in range(KC):
                        ins = e.matmul(ps[:, 4, b * S:(b + 1) * S], ctxk[:, b, k, :], b_eT[:, b, k * S:(k + 1) * S],
                                       start=(k == 0), stop=(k == KC - 1))
                inc(ins, "B_oTp")
                W(e, "B_oT", g)
                for b in range(NB):
                    ins = e.matmul(ps[0:S, 6 + b // 2, (b % 2) * D:(b % 2 + 1) * D], hT[:, 1, b * S:(b + 1) * S],
                                   wv("B_v"), start=True, stop=True)
                inc(ins, "B_out")
                W(e, "C_xn", g)
                toT_pe(e, xn, "C_hTp")
                W(e, "C_hT", g, 2)
                proj_pe(e, wv("C_v", DC), hT, 2, "C_vp")
                for m in range(DC):
                    inc(projT_pe(e, wv("C_k", DC), hT, m, 4 + m), "C_kTp")
                for m in range(DC):
                    inc(projT_pe(e, wv("C_q", DC), hT, m, 6 + m), "C_qTp")
                W(e, "C_qT", g, 2)
                W(e, "C_v", g)
                self_pe(e, "C_", g, None)
                W(e, "C_yT", g)
                proj_pe(e, wv("C_o", DC), qT, 2, "C_out")
                W(e, "D_xn", g)
                toT_pe(e, xn, "D_hTp")
                W(e, "D_hT", g, 2)
                gate_pe(e, "D_", g, wv("D_gate", DC), lambda c, b: hT[:, c, b * S:(b + 1) * S])
            W(e, "D_g", NG - 1)
            with e.Fori(0, E0 // 2) as ep:
                def up(s, m):
                    slot, gi = divmod(s, NG)
                    n = s * MC0 + m
                    if gi == 0 and m == 0:
                        e.wait_ge(ld_e0[slot].sem, ep * 16 + 16)
                    e.wait_ge(m_hid.sem, m_hid.free(ep, n + 1))
                    for i in range(2):
                        w = experts[:, slot * W0 + i * DC * HID0:slot * W0 + (i + 1) * DC * HID0].rearrange(
                            "p (c n) -> p c n", c=DC)
                        for c in range(DC):
                            ins = e.matmul(bank(2 * i + m % 2, n=NT), w[:, c, m * P:(m + 1) * P],
                                           hT_all[:, c, gi * NT:(gi + 1) * NT], start=(c == 0), stop=(c == DC - 1))
                    ins.then_inc(m_h.sem, 1)

                def down(s):
                    slot, gi = divmod(s, NG)
                    e.wait_ge(m_hid.sem, m_hid.at(ep, MC0 * (s + 1)))
                    e.wait_ge(m_acc.sem, m_acc.free(ep, s + 1))
                    w = experts[:, slot * W0 + 2 * DC * HID0:(slot + 1) * W0].rearrange("p (c n) -> p c n", c=MC0)
                    for b in range(NB):
                        for c in range(MC0):
                            ins = e.matmul(ps[0:S, 4 + 2 * (s % 2) + b // 2, (b % 2) * D:(b % 2 + 1) * D],
                                           hid[:, s % 2, c, b * S:(b + 1) * S], w[:, c, :],
                                           start=(c == 0), stop=(c == MC0 - 1))
                    ins.then_inc(m_out.sem, 1)

                for s in range(2 * NG):
                    up(s, 0)
                    up(s, 1)
                    if s >= 1:
                        down(s - 1)
                    up(s, 2)
                    up(s, 3)
                down(2 * NG - 1)
            e.wait_ge(m_acc.sem, m_acc.at(E0 // 2 - 1, 8))
            with e.Fori(0, NG) as g:
                for j in range(3):
                    W(e, "E_xq", g, j + 1)
                    for c in range(DC):
                        pb = ps[:, c, :].bitcast(BF16)
                        for b in range(NB):
                            ins = e.transpose(pb[:, b * S:(b + 1) * S], xq[:, b, c * P:(c + 1) * P], identb[0:S, 0:S])
                    inc(ins, "E_xqTp")
                    W(e, "E_xqT", g, j + 1)
                    if j < 2:
                        for m in range(DC):
                            inc(projT_pe(e, wtern[:, j], xqT, m, 4 + m), "E_qTp" if j == 0 else "E_kTp")
                        W(e, "E_bc", g, j + 1)
                        for b in range(NB):
                            ins = e.matmul(ps[:, 6, b * S:(b + 1) * S], cs("ones", S), y[:, b, 0:S],
                                           start=True, stop=True)
                        inc(ins, "E_bcp")
                        W(e, "E_qT" if j == 0 else "E_kT", g, 2)
                    else:
                        proj_pe(e, wtern[:, j], xqT, 2, "E_vp")
                W(e, "E_v", g)
                self_pe(e, "E_", g, None)
                W(e, "E_yT", g)
                for b in range(NB):
                    for c in range(DC):
                        ins = e.transpose(ps[0:S, 2 + b // 2, (b % 2) * D + c * P:(b % 2) * D + (c + 1) * P],
                                          qT[:, c, b * S:(b + 1) * S], ident)
                inc(ins, "E_ytp")
                W(e, "E_xq", g, 4)
                for c in range(DC):
                    pb = ps[:, c, :].bitcast(BF16)
                    for b in range(NB):
                        ins = e.transpose(pb[:, b * S:(b + 1) * S], xq[:, b, c * P:(c + 1) * P], identb[0:S, 0:S])
                inc(ins, "E_xqTp")
                W(e, "E_xqT", g, 4)
                proj_pe(e, wtern[:, 3], xqT, 4, "E_out")
                W(e, "F_xn", g)
                toT_pe(e, xn, "F_hTp")
                W(e, "F_hT", g, 2)
                for m in range(DC):
                    inc(projT_pe(e, wv("F_q", DC), hT, m, 2 + m), "F_qTp")
                e.wait_ge(ld["ctxT3"].sem, g * 16 + 16)

                def kv(b, i):
                    n = 5 * b + i
                    if n >= 1:
                        W(e, "F_kv", g, n)
                    if i < DC:
                        ins = e.matmul(bank(7, n=LC), wv("F_k")[:, i * P:(i + 1) * P], ctxT[:, b, 0:LC],
                                       start=True, stop=True)
                    else:
                        k = i - DC
                        ins = e.matmul(bank(7, KW, D), ctxT[:, b, k * KW:(k + 1) * KW], wv("F_v"),
                                       start=True, stop=True)
                    inc(ins, "F_kvp")

                def f_scores(b, v):
                    n, c = 8 * b + v, v // 4
                    W(e, "F_bd", g, 2 * b + c + 1)
                    if v == 0:
                        W(e, "F_kv", g, 5 * b + 2)
                    if n >= 2:
                        W(e, "F_e", g, n - 1)
                    for i in range(2):
                        ins = e.matmul(bank(2 * (n % 2) + i, S, LC), headbd[:, c, 2 * (v % 4) + i, :],
                                       kT[:, b % 2, c * LC:(c + 1) * LC], start=True, stop=True)
                    inc(ins, "F_s")

                def f_turn(b, v):
                    n = 8 * b + v
                    W(e, "F_e", g, n + 1)
                    if n >= 1:
                        W(e, "F_pT", g, n)
                    for i in range(2):
                        for k in range(KC):
                            ins = e.transpose(ps[0:KW, 4 + i, k * S:(k + 1) * S],
                                              f_e[:, n % 2, i, k * KW:(k + 1) * KW], identS)
                    inc(ins, "F_pTp")

                def f_values(b, v):
                    n, c = 8 * b + v, v // 4
                    W(e, "F_pT", g, n + 1)
                    if v == 0:
                        W(e, "F_kv", g, 5 * b + 5)
                        if b >= 1:
                            W(e, "F_o", g, b)
                    for i in range(2):
                        h = 2 * (v % 4) + i
                        for k in range(KC):
                            ins = e.matmul(ps[:, 6, (2 * (b % 2) + c) * S:(2 * (b % 2) + c + 1) * S],
                                           window(3 * (b % 2) + k, KW, c, h), f_eT[:, n % 2, i, k * S:(k + 1) * S],
                                           start=(h == 0 and k == 0), stop=(h == HC - 1 and k == KC - 1))
                    inc(ins, "F_av")

                W(e, "F_qT", g, 2)
                for i in range(5):
                    kv(0, i)
                units = [(b, v) for b in range(NB) for v in range(8)]
                for n in range(len(units) + 2):
                    if n < len(units):
                        b, v = units[n]
                        f_scores(b, v)
                    if 1 <= n <= len(units):
                        f_turn(*units[n - 1])
                    if n >= 2:
                        f_values(*units[n - 2])
                    if n < len(units) and b + 1 < NB and 3 <= v < 8:
                        kv(b + 1, v - 3)
                W(e, "F_rx", g)
                toT_pe(e, xn, "F_rTp", 0)
                W(e, "F_yT", g)
                proj_pe(e, wv("F_o", DC), qT, 2, "F_out")
                W(e, "G_xn", g)
                toT_pe(e, xn, "G_hTp")
                W(e, "G_hT", g, 2)
                gate_pe(e, "G_", g, wv("G_gate", DC), lambda c, b: hT[:, c, b * S:(b + 1) * S])
                e.wait_ge(ld["e1"].sem, 16)
                W(e, "G_gm", g)

                def up1(j):
                    if j >= 2:
                        W(e, "G_hid", g, j - 1)
                    for i in range(2):
                        w = experts[:, j * 768 + i * 256:j * 768 + (i + 1) * 256].rearrange("p (c n) -> p c n", c=DC)
                        for c in range(DC):
                            ins = e.matmul(bank(2 * i + j % 2, n=NT), w[:, c, :], hT[:, c, :],
                                           start=(c == 0), stop=(c == DC - 1))
                    inc(ins, "G_h")

                def down1(j):
                    W(e, "G_hid", g, j + 1)
                    if j >= 2:
                        W(e, "G_acc", g, j - 1)
                    for b in range(NB):
                        ins = e.matmul(ps[0:S, 4 + 2 * (j % 2) + b // 2, (b % 2) * D:(b % 2 + 1) * D],
                                       g_hid[:, j % 2, b * S:(b + 1) * S], experts[:, j * 768 + 512:(j + 1) * 768],
                                       start=True, stop=True)
                    inc(ins, "G_o")

                for j in range(E1 + 1):
                    if j < E1:
                        up1(j)
                    if j >= 1:
                        down1(j - 1)


        @block.scalar
        def _(e):
            e.wait_ge(ld["cst"].sem, 16)
            e.activation(identb[:], ident, ACT.Copy)
            for b in range(NB):
                ins = e.activation(causalb[:, b, :], cs("causal", S), ACT.Copy)
            ins.then_inc(prep_b.sem, 1)
            e.wait_ge(prep_t.sem, 1)
            e.activation(tempc[:, 1:2], tempc[:, 0:1], ACT.Exp, scale=-1.0)
            e.drain()
            e.activation(tempc[:, 1:2], tempc[:, 1:2], ACT.Ln, bias=1.0).then_inc(prep_e.sem, 1)
            with e.Fori(0, NG) as g:
                toT_act(e, hT, "A_hTp", "A_hT", g)
                W(e, "A_in", g)
                inc(e.activation(a_q, a_in[:, :, SH], ACT.Tanh), "A_q")
                W(e, "A_shTp", g)
                inc(e.activation(a_shT, bank(0, SH, NT), ACT.Copy), "A_shT")
                W(e, "A_ang", g)
                inc(e.activation(a_trig, a_ang, ACT.Sin), "A_trig")
                W(e, "A_phiTp", g)
                inc(e.activation(a_phiT, bank(0, SH, NT), ACT.Copy), "A_phiT")
                W(e, "A_nm", g)
                for b in range(NB):
                    ins = e.activation(a_lg[:, b, :], a_lg[:, b, :], ACT.Exp, bias=a_nm[:, b:b + 1],
                                       accum_out=a_sum[:, b:b + 1])
                inc(ins, "A_e")
                W(e, "A_pTp", g)
                inc(e.activation(probsT[0:S, 0, 0:NT], bank(0, S, NT), ACT.Copy), "A_pT")
                W(e, "A_oTp", g)
                inc(e.activation(qT[:], ps[:, 2:4, 0:NT], ACT.Copy), "A_oT")
                toT_act(e, hT, "B_hTp", "B_hT", g)
                for m in range(DC):
                    W(e, "B_qTp", g, m + 1)
                    inc(e.activation(qT[:, m, :], bank(2 + m, n=NT), ACT.Identity, bias=col("B_bq", m)), "B_qT")
                W(e, "B_kqTp", g)
                inc(e.activation(hT[:, 0, :], bank(0, n=NT), ACT.Copy), "B_kqT")
                W(e, "B_nm", g)
                for b in range(NB):
                    ins = e.activation(b_e[:, b, 0:LC], bank(4 + b, S, LC), ACT.Exp, bias=b_nm[:, b:b + 1],
                                       accum_out=b_sum[:, b:b + 1])
                inc(ins, "B_e")
                W(e, "B_pTp", g)
                inc(e.activation(b_eT[:, 0:2, :], ps[0:KW, 0:2, 0:KC * S], ACT.Copy), "B_pT")
                W(e, "B_oTp", g)
                inc(e.activation(hT[:, 1, :], bank(4, n=NT), ACT.Copy), "B_oT")
                toT_act(e, hT, "C_hTp", "C_hT", g, scale="C_s", bias="C_b")
                for m in range(DC):
                    W(e, "C_kTp", g, m + 1)
                    inc(e.activation(kT[:, 0, m * NT:(m + 1) * NT], bank(4 + m, n=NT), ACT.Copy), "C_kT")
                for m in range(DC):
                    W(e, "C_qTp", g, m + 1)
                    inc(e.activation(qT[:, m, :], bank(6 + m, n=NT), ACT.Copy, scale=HD ** -0.5), "C_qT")
                self_act(e, "C_", g)
                recipT_act(e, "C_", g)
                toT_act(e, hT, "D_hTp", "D_hT", g, scale="D_s", bias="D_b")
                gate_act(e, "D_", g)
            with e.Fori(0, E0 // 2) as ep:
                for n in range(2 * NG * MC0):
                    e.wait_ge(m_h.sem, m_h.at(ep, n + 1))
                    e.wait_ge(m_hid.sem, m_hid.free(ep, n + 1))
                    e.activation(silu[:, n % 2, :], bank(n % 2, n=NT), ACT.Silu).then_inc(m_act.sem, 1)
            with e.Fori(0, NG) as g:
                for j in range(4):
                    W(e, "E_xqTp", g, j + 1)
                    inc(e.activation(xqT[:], ps[:, 0:DC, :].bitcast(BF16)[:, :, 0:NT], ACT.Copy), "E_xqT")
                    if j < 2:
                        W(e, "E_bcp", g, j + 1)
                        inc(e.activation(hT[:, j, :], bank(6, n=NT), ACT.Copy, scale=wscale[:, j:j + 1]), "E_sc")
                    if j == 2:
                        self_act(e, "E_", g)
                        recipT_act(e, "E_", g)
                toT_act(e, hT, "F_hTp", "F_hT", g)
                for m in range(DC):
                    W(e, "F_qTp", g, m + 1)
                    inc(e.activation(qT[:, m, :], bank(2 + m, n=NT), ACT.Identity, scale=HD ** -0.5,
                                     bias=bq4[:, m:m + 1]), "F_qT")

                def key_evac(b, i):
                    W(e, "F_kvp", g, 5 * b + i + 1)
                    inc(e.activation(kT[:, b % 2, i * LC:(i + 1) * LC], bank(7, n=LC), ACT.Identity,
                                     bias=col("F_bk", i)), "F_kv")

                for i in range(DC):
                    key_evac(0, i)
                for n in range(8 * NB):
                    b, v = divmod(n, 8)
                    W(e, "F_nm", g, n + 1)
                    if n >= 2:
                        W(e, "F_pTp", g, n - 1)
                    for i in range(2):
                        h = 2 * v + i
                        ins = e.activation(f_e[:, n % 2, i, 0:LC], bank(2 * (n % 2) + i, S, LC), ACT.Exp,
                                           bias=h_nm[:, n % 2, i:i + 1], accum_out=h_sum[:, b, h:h + 1])
                    inc(ins, "F_e")
                    if v == 1 and b >= 1:
                        W(e, "F_av", g, 8 * b)
                        inc(e.activation(hT[:, :, (b - 1) * S:b * S],
                                         ps[:, 6, 2 * ((b - 1) % 2) * S:2 * ((b - 1) % 2) * S + 2 * S].rearrange(
                                             "p (c n) -> p c n", c=DC), ACT.Copy), "F_o")
                    if b + 1 < NB and v in (3, 4):
                        key_evac(b + 1, v - 3)
                W(e, "F_av", g, 8 * NB)
                inc(e.activation(hT[:, :, (NB - 1) * S:NB * S],
                                 ps[:, 6, 2 * S:4 * S].rearrange("p (c n) -> p c n", c=DC), ACT.Copy), "F_o")
                for c in range(DC):
                    W(e, "F_rTp", g, c + 1)
                    inc(e.activation(kT[:, c, 0:NT], bank(c, n=NT), ACT.Copy), "F_rT")
                toT_act(e, hT, "G_hTp", "G_hT", g)
                gate_act(e, "G_", g)
                for j in range(E1):
                    W(e, "G_h", g, j + 1)
                    if j >= 2:
                        W(e, "G_hid", g, j - 1)
                    inc(e.activation(g_act[:, j % 2, :], bank(j % 2, n=NT), ACT.Gelu), "G_act")

        @block.gpsimd
        def _(e):
            e.memset(spread[:, 0:2, :], 0.0)
            e.wait_ge(ld["cst"].sem, 16)
            e.wait_ge(ld["rows"].sem, 16)
            e.drain()
            bcast = lambda name: row(name).unsqueeze(1).broadcast_to([S, NB, D])
            with e.Fori(0, NG) as g:
                norm_pool(e, "A_", g)
                inc(e.tensor_tensor(x[:], xin[:], bcast("A_out"), ALU.add), "A_xb")
                W(e, "A_ss", g)
                inc(e.tensor_tensor(a_rn, a_ss, cs("mhalf", S)[:, 0:4], ALU.pow), "A_rn")
                norm_pool(e, "B_", g)
                W(e, "B_xn", g)
                inc(e.tensor_tensor(x[:], x[:], bcast("B_v"), ALU.add), "B_xb")
                norm_pool(e, "C_", g, eps2=EPS)
                W(e, "C_xn", g)
                inc(e.tensor_tensor(y[:], y[:], bcast("C_o"), ALU.add), "C_xb")
                self_pool(e, "C_", g, c_v)
                norm_pool(e, "D_", g)
            e.wait_ge(m_acc.sem, m_acc.at(E0 // 2 - 1, 2 * NG))
            for u in range(NVU):
                e.memset(spread[:, u, :], 0.0)
            e.drain()
            with e.Fori(0, NG) as g:
                norm_pool(e, "E_", g, eps2=EPS_RMS, fold=True)
                self_pool(e, "E_", g, y)
                W(e, "E_ssr", g)
                inc(e.tensor_tensor(r2, t1, cs("mhalf", S)[:, 0:4], ALU.pow), "E_sso")
                norm_pool(e, "F_", g)
                e.memset(f_e[:, :, :, LC:LP], 0.0)
                W(e, "F_xn", g)
                inc(e.tensor_tensor(x[:], x[:], bcast("F_o"), ALU.add), "F_xb")
                e.drain()
                W(e, "F_qT", g, 2)
                for b in range(NB):
                    for c in range(DC):
                        if b >= 1:
                            W(e, "F_s", g, 8 * (b - 1) + 4 * (c + 1))
                        inc(e.tensor_tensor(headbd[:, c],
                                            qT[:, c, b * S:(b + 1) * S].unsqueeze(1).broadcast_to([P, HC, S]),
                                            cs("head").unsqueeze(2).broadcast_to([P, HC, S]), ALU.mult), "F_bd")
                W(e, "F_rs", g)
                inc(e.tensor_tensor(xn[:].rearrange("p b (h d) -> p b h d", d=HD),
                                    h_rs.unsqueeze(3).broadcast_to([S, NB, NH, HD]),
                                    cs("ones", S)[:, 0:1].unsqueeze(2).unsqueeze(3).broadcast_to([S, NB, NH, HD]),
                                    ALU.mult), "F_rx")
                norm_pool(e, "G_", g)

        @block.vector
        def _(e):
            e.sem_inc(m_hid.sem, m_hid.credit)
            e.sem_inc(m_acc.sem, m_acc.credit)
            e.sem_inc(m_out.sem, m_out.credit)
            e.wait_ge(ld["wq"].sem, 16)
            e.wait_ge(ld["wt"].sem, 16)
            e.wait_ge(ld["cst"].sem, 16)
            e.wait_ge(ld["rows"].sem, 16)
            wq4 = experts[:, 0:4 * DC * D].rearrange("p (j n) -> p j n", j=4)
            e.tensor_reduce(wsum, wq4, AX, ALU.add, apply_absolute_value=True).then_inc(prep_abs.sem, 1)
            lt = col("log_temp")
            e.tensor_scalar(tempc[:, 0:1], lt, -1.0, None, ALU.mult)
            e.drain()
            e.tensor_tensor(tempc[:, 0:1], tempc[:, 0:1], lt, ALU.max).then_inc(prep_t.sem, 1)
            e.tensor_scalar(bq4, wt[:, WOFF["cols"][0] + COLS["F_bq"]:WOFF["cols"][0] + COLS["F_bq"] + 2],
                            HD ** -0.5, None, ALU.mult)
            e.memset(b_e[:, :, LC:LP], 0.0)
            e.memset(a_sqw[:, :, SH:P], 0.0)
            e.memset(a_phiw[:, :, SH:P], 0.0)
            e.wait_ge(prep_sum.sem, 1)
            e.tensor_scalar(wscale, bank(0, n=4), 1.0 / (D * D), 1e-5, ALU.mult, ALU.max)
            e.drain()
            e.reciprocal(wrecip, wscale)
            e.drain()
            for j in range(4):
                e.tensor_scalar(wq4[:, j, :], wq4[:, j, :], wrecip[:, j:j + 1], MAGIC, ALU.mult, ALU.add)
            e.tensor_scalar(wscale[:, 0:1], wscale[:, 0:1], HD ** -0.5, None, ALU.mult)
            e.drain()
            e.tensor_scalar(wq4, wq4, MAGIC, 1.0, ALU.subtract, ALU.min)
            e.drain()
            e.tensor_scalar(wtern[:].rearrange("p j c n -> p j (c n)"), wq4, -1.0, None, ALU.max
                            ).then_inc(tern_go.sem, 1)
            e.wait_ge(prep_e.sem, 1)
            e.tensor_scalar(tempc[:, 2:3], lt, 0.0, None, ALU.max)
            e.drain()
            e.tensor_tensor(tempc[:, 2:3], tempc[:, 2:3], tempc[:, 1:2], ALU.add)
            e.drain()
            e.tensor_scalar(tempc[:, 2:3], tempc[:, 2:3], 0.1, None, ALU.add)
            e.drain()
            e.reciprocal(tempc[:, 3:4], tempc[:, 2:3])
            e.drain()
            e.tensor_scalar(decay, cs("decay", S), tempc[0:S, 3:4], None, ALU.mult)

            def add_pair(dst, b0, src, name):
                inc(e.tensor_tensor(dst[:], pair(b0), src[:], ALU.add), name)

            with e.Fori(0, NG) as g:
                e.wait_ge(ld["x"].sem, g * 16 + 16)
                inc(norm_dve(e, "A_", g, xin, xn), "A_xn")
                W(e, "A_in_p", g)
                inc(e.tensor_tensor(a_in, ps[0:S, 2:6, 0:321], row("A_in").unsqueeze(1).broadcast_to([S, NB, 321]),
                                    ALU.add), "A_in")
                e.drain()
                e.tensor_tensor(a_sq, a_in[:, :, 0:SH], a_in[:, :, 0:SH], ALU.mult)
                e.drain()
                e.tensor_reduce(a_ss, a_sq, AX, ALU.add)
                e.drain()
                inc(e.tensor_scalar(a_ss, a_ss, 1e-24, None, ALU.max), "A_ss")
                W(e, "A_rn", g)
                inc(e.tensor_tensor(a_sq, a_in[:, :, 0:SH], a_rn.unsqueeze(2).broadcast_to([S, NB, SH]), ALU.mult),
                    "A_shn")
                W(e, "A_angp", g)
                e.tensor_scalar(a_ang, bank(1, SH, NT), col("rb", 0, SH), col("half_pi", 0, SH), ALU.add, ALU.add)
                e.drain()
                e.tensor_scalar(a_k, a_ang, 1.0 / (2 * math.pi), MAGIC, ALU.mult, ALU.add)
                e.drain()
                e.tensor_scalar(a_k, a_k, MAGIC, -1.0, ALU.subtract, ALU.mult)
                e.drain()
                e.scalar_tensor_tensor(a_ang, a_k, TWO_PI_HI, a_ang, ALU.mult, ALU.add)
                e.drain()
                e.scalar_tensor_tensor(a_ang, a_k, TWO_PI_LO, a_ang, ALU.mult, ALU.add)
                e.drain()
                inc(e.tensor_scalar(a_ang, a_ang, 3.1415925, -3.1415925, ALU.min, ALU.max), "A_ang")
                W(e, "A_comb", g)
                W(e, "A_q", g)
                qb = a_q.unsqueeze(2).broadcast_to([S, NB, SH])
                pm = lambda m: ps[0:S, 2:6, m * SH:(m + 1) * SH]
                e.tensor_scalar(a_phi, pm(ORD - 1), MAGS[ORD - 1] / MAGS[ORD - 2], None, ALU.mult)
                e.drain()
                for m in range(ORD - 2, -1, -1):
                    e.tensor_tensor(a_phi, a_phi, qb, ALU.mult)
                    e.drain()
                    ins = e.tensor_tensor(a_phi, a_phi, pm(m), ALU.add)
                    if m:
                        e.drain()
                        e.tensor_scalar(a_phi, a_phi, MAGS[m] / MAGS[m - 1], None, ALU.mult)
                        e.drain()
                inc(ins, "A_phi")
                W(e, "A_lg", g)
                e.tensor_tensor(a_lg, bank(1, S, NT).rearrange("p (b n) -> p b n", b=NB),
                                decay.unsqueeze(1).broadcast_to([S, NB, S]), ALU.mult)
                e.drain()
                e.tensor_tensor(a_lg, a_lg, cs("causal", S).unsqueeze(1).broadcast_to([S, NB, S]), ALU.add)
                e.drain()
                inc(e.tensor_reduce(a_nm, a_lg, AX, ALU.max, negate=True), "A_nm")
                W(e, "A_e", g)
                e.reciprocal(a_rs, a_sum)
                e.drain()
                inc(e.tensor_tensor(a_lg, a_lg, a_rs.unsqueeze(2).broadcast_to([S, NB, S]), ALU.mult), "A_p")
                W(e, "A_out", g)
                W(e, "A_xb", g)
                add_pair(x, 4, x, "A_x")
                e.drain()
                inc(norm_dve(e, "B_", g, x, xn), "B_xn")
                W(e, "B_qbkp", g)
                e.tensor_scalar(b_qbk, bank(1, S, NB), 1.0, None, ALU.mult)
                W(e, "B_s", g)
                e.tensor_reduce(b_mx, ps[0:S, 4:8, 0:LC], AX, ALU.max)
                e.drain()
                e.tensor_tensor(b_mx, b_mx, b_qbk, ALU.add)
                e.drain()
                inc(e.tensor_tensor(b_nm, b_qbk, b_mx, ALU.subtract), "B_nm")
                W(e, "B_e", g)
                e.reciprocal(b_rs, b_sum)
                e.drain()
                for b in range(NB):
                    ins = e.tensor_scalar(b_e[:, b, 0:LC], b_e[:, b, 0:LC], b_rs[:, b:b + 1], None, ALU.mult)
                inc(ins, "B_p")
                W(e, "B_pTp", g)
                inc(e.tensor_scalar(b_eT[:, 2:4, :], ps[0:KW, 2:4, 0:KC * S], 1.0, None, ALU.mult), "B_pT2")
                W(e, "B_out", g)
                W(e, "B_xb", g)
                add_pair(x, 6, x, "B_x")
                e.drain()
                norm_dve(e, "C_", g, x, y)
                e.drain()
                for b in range(NB):
                    ins = e.tensor_scalar(xn[:, b, :], y[:, b, :], r2[:, b:b + 1], None, ALU.mult)
                inc(ins, "C_xn")
                W(e, "C_vp", g)
                inc(e.tensor_scalar(c_v, pair(2), 1.0, None, ALU.mult), "C_v")
                self_dve(e, "C_", g)
                W(e, "C_rT", g, 2)
                inc(e.tensor_tensor(qT[:], ps[:, 6:8, 0:NT], hT[:], ALU.mult), "C_yT")
                W(e, "C_out", g)
                W(e, "C_xb", g)
                add_pair(y, 2, y, "C_x")
                e.drain()
                inc(norm_dve(e, "D_", g, y, xn), "D_xn")
                e.tensor_tensor(xall[:, bass.ds(g * NB, NB), :], x[:], y[:], ALU.add)
                e.drain()
                W(e, "D_hT", g, 2)
                for c in range(DC):
                    e.tensor_scalar(hT_all[:, c, bass.ds(g * NT, NT)], hT[:, c, :], 1.0, None, ALU.mult)
                gate_dve(e, "D_", g, False, gates_all[:, bass.ds(g * NB, NB), :])
                e.drain()
            gpair = g_rank.rearrange("p b n -> p (b n)").rearrange("p (q s) -> p q s", s=2)
            with e.Fori(0, E0 // 2) as ep:
                e.tensor_scalar(gpair, gates_all[:, :, bass.ds(2 * ep, 2)], 1.0, None, ALU.mult)
                e.drain()

                def acc(s):
                    slot, gi = divmod(s, NG)
                    e.wait_ge(m_out.sem, m_out.at(ep, s + 1))
                    for b in range(NB):
                        q = gi * NB + b
                        ins = e.scalar_tensor_tensor(
                            xall[:, q, :], ps[0:S, 4 + 2 * (s % 2) + b // 2, (b % 2) * D:(b % 2 + 1) * D],
                            gpair[:, q, slot:slot + 1], xall[:, q, :], ALU.mult, ALU.add)
                    ins.then_inc(m_acc.sem, 1)

                for s in range(2 * NG):
                    for m in range(MC0):
                        n = s * MC0 + m
                        e.wait_ge(m_act.sem, m_act.at(ep, n + 1))
                        if m == 0:
                            e.wait_ge(m_out.sem, m_out.at(ep, s - 1))
                        e.tensor_tensor(hid[:, s % 2, m, :], bank(2 + n % 2, n=NT), silu[:, n % 2, :],
                                        ALU.mult).then_inc(m_hid.sem, 1)
                        if m == 1 and s >= 1:
                            acc(s - 1)
                acc(2 * NG - 1)
                e.drain()
            tq = xin

            def quantise(j, g):
                e.drain()
                e.tensor_reduce(q_am, tq[:], AX, ALU.max, apply_absolute_value=True)
                e.drain()
                e.tensor_scalar(q_am, q_am, 1e-5, None, ALU.max)
                e.drain()
                e.reciprocal(q_sc, q_am)
                e.tensor_scalar(q_isc[:, min(j, 2), :], q_am, 1.0 / 127.0, None, ALU.mult)
                e.drain()
                e.tensor_scalar(q_sc, q_sc, 127.0, None, ALU.mult)
                e.drain()
                for b in range(NB):
                    e.tensor_scalar(tq[:, b, :], tq[:, b, :], q_sc[:, b:b + 1], MAGIC, ALU.mult, ALU.add)
                e.drain()
                if j >= 1:
                    W(e, "E_xqTp", g, j)
                inc(e.tensor_scalar(xq[:], tq[:], MAGIC, 127.0, ALU.subtract, ALU.min), "E_xq")

            with e.Fori(0, NG) as g:
                e.wait_ge(x_free.sem, g + 1)
                e.tensor_scalar(x[:], xall[:, bass.ds(g * NB, NB), :], 1.0, None, ALU.mult)
                e.drain()
                norm_dve(e, "E_", g, x, xn)
                e.drain()
                for j, gain in enumerate(("gq", "gk", "gv")):
                    e.tensor_tensor(tq[:], xn[:], row(gain).unsqueeze(1).broadcast_to([S, NB, D]), ALU.mult)
                    quantise(j, g)
                    if j < 2:
                        if j == 1:
                            W(e, "E_bcp", g, 1)
                        for b in range(NB):
                            ins = e.tensor_scalar(y[:, b, 0:S], identS, q_isc[:, j, b:b + 1], None, ALU.mult)
                        inc(ins, "E_bc")
                        W(e, "E_sc", g, j + 1)
                        W(e, "E_qTp" if j == 0 else "E_kTp", g, 2)
                        for m in range(DC):
                            dst = qT[:, m, :] if j == 0 else kT[:, 0, m * NT:(m + 1) * NT]
                            inc(e.tensor_tensor(dst, bank(4 + m, n=NT), hT[:, j, :], ALU.mult),
                                "E_qT" if j == 0 else "E_kT")
                W(e, "E_vp", g)
                for b in range(NB):
                    ins = e.tensor_scalar(y[:, b, :], ps[0:S, 2 + b // 2, (b % 2) * D:(b % 2 + 1) * D],
                                          q_isc[:, 2, b:b + 1], wscale[0:S, 2:3], ALU.mult, ALU.mult)
                inc(ins, "E_v")
                self_dve(e, "E_", g)
                W(e, "E_rT", g, 2)
                inc(e.tensor_tensor(qT[:], ps[:, 6:8, 0:NT], hT[:], ALU.mult), "E_yT")
                W(e, "E_ytp", g)
                e.tensor_scalar(y[:], pair(2), 1.0, None, ALU.mult)
                e.drain()
                e.tensor_tensor(tq[:], y[:], y[:], ALU.mult)
                e.drain()
                e.tensor_reduce(q_am, tq[:], AX, ALU.add)
                e.drain()
                inc(e.tensor_scalar(t1, q_am, 1.0 / D, EPS_RMS, ALU.mult, ALU.add), "E_ssr")
                W(e, "E_sso", g)
                for b in range(NB):
                    e.scalar_tensor_tensor(tq[:, b, :], y[:, b, :], r2[:, b:b + 1], row("go"), ALU.mult, ALU.mult)
                quantise(3, g)
                e.tensor_scalar(q_isc[:, 2, :], q_isc[:, 2, :], wscale[0:S, 3:4], None, ALU.mult)
                e.drain()
                W(e, "E_out", g)
                for b in range(NB):
                    e.scalar_tensor_tensor(x[:, b, :], ps[0:S, 4 + b // 2, (b % 2) * D:(b % 2 + 1) * D],
                                           q_isc[:, 2, b:b + 1], x[:, b, :], ALU.mult, ALU.add)
                e.drain()
                inc(norm_dve(e, "F_", g, x, xn), "F_xn")

                def value_evac(b, k):
                    W(e, "F_kvp", g, 5 * b + DC + k + 1)
                    inc(e.tensor_tensor(diag(3 * (b % 2) + k, KW),
                                        bank(7, KW, D).rearrange("p (c h d) -> p c h d", c=DC, h=HC),
                                        row("F_v", KW).rearrange("p (c h d) -> p c h d", c=DC, h=HC), ALU.add), "F_kv")

                for k in range(KC):
                    value_evac(0, k)
                for n in range(8 * NB + 1):
                    b, v = divmod(n, 8)
                    if n < 8 * NB:
                        W(e, "F_s", g, n + 1)
                        if n >= 2:
                            W(e, "F_e", g, n - 1)
                        inc(e.tensor_reduce(h_nm[:, n % 2, 0:2], ps[0:S, 2 * (n % 2):2 * (n % 2) + 2, 0:LC], AX,
                                            ALU.max, negate=True), "F_nm")
                    if n >= 1:
                        W(e, "F_pTp", g, n)
                        if n >= 3:
                            W(e, "F_av", g, n - 2)
                        inc(e.tensor_scalar(f_eT[:, (n - 1) % 2], ps[0:KW, 4:6, 0:KC * S], 1.0, None, ALU.mult), "F_pT")
                    if n < 8 * NB and b + 1 < NB and v >= 5:
                        value_evac(b + 1, v - 5)
                W(e, "F_e", g, 8 * NB)
                inc(e.reciprocal(h_rs, h_sum), "F_rs")
                W(e, "F_rT", g, 2)
                W(e, "F_o", g, NB)
                inc(e.tensor_tensor(qT[:], hT[:], kT[:, :, 0:NT], ALU.mult), "F_yT")
                W(e, "F_out", g)
                W(e, "F_xb", g)
                add_pair(x, 2, x, "F_x")
                e.drain()
                inc(norm_dve(e, "G_", g, x, xn), "G_xn")
                gate_dve(e, "G_", g, True, gates_all[:, 0:NB, :])
                e.drain()

                def acc1(j):
                    W(e, "G_o", g, j + 1)
                    b0 = 4 + 2 * (j % 2)
                    if j == E1 - 1:
                        ins = e.tensor_tensor(x[:], pair(b0), x[:], ALU.add)
                    else:
                        for b in range(NB):
                            ins = e.scalar_tensor_tensor(
                                x[:, b, :], ps[0:S, b0 + b // 2, (b % 2) * D:(b % 2 + 1) * D],
                                gates_all[:, b, j:j + 1], x[:, b, :], ALU.mult, ALU.add)
                    e.drain()
                    inc(ins, "G_acc") if False else e.sem_inc(names["G_acc"].sem, 1)

                for j in range(E1 + 1):
                    if j < E1:
                        W(e, "G_act", g, j + 1)
                        if j >= 2:
                            W(e, "G_o", g, j - 1)
                        inc(e.tensor_tensor(g_hid[:, j % 2, :], bank(2 + j % 2, n=NT), g_act[:, j % 2, :],
                                            ALU.mult), "G_hid")
                    if j >= 1:
                        acc1(j - 1)


def kernel(**inputs):
    import concourse.bacc as bacc
    from concourse.bass_utils import run_bass_kernel_spmd

    a = {k: np.asarray(v) for k, v in inputs.items()}
    f32 = np.float32

    def chunks(w):
        return np.ascontiguousarray(w.reshape(-1, P, w.shape[1]).transpose(1, 0, 2)).reshape(P, -1)

    wt = np.zeros((P, NW), f32)

    def put(name, v):
        o, n = WOFF[name]
        wt[:v.shape[0], o:o + n] = v

    put("A_in", chunks(np.concatenate([a["L0_attn_W_shell"].T, a["L0_attn_W_charge"].T, a["L0_attn_W_v"].T], 1)))
    put("A_omega", np.concatenate([a["L0_attn_omega"].T] * 2 + [np.zeros((SH, 2 * RF), f32)], 1))
    put("A_comb", a["L0_attn_W_combine"].reshape(SH, ORD, 2 * RF).transpose(2, 1, 0).reshape(2 * RF, ORD * SH))
    put("A_out", chunks(a["L0_attn_W_out"].T))
    put("B_q", chunks(a["L0_xattn_Wq"]))
    put("B_kT", chunks(a["L0_xattn_Wk"].T))
    put("B_bk", chunks(a["L0_xattn_bk"][:, None]))
    put("B_v", a["L0_xattn_Wv"])
    put("C_q", chunks(a["L0_ffn_wq"]))
    put("C_k", chunks(a["L0_ffn_wk"]))
    put("C_v", chunks(a["L0_ffn_wv"]))
    put("C_o", chunks(a["L0_ffn_wo"]))
    put("D_gate", chunks(a["L0_ffn_gate_w"]))
    put("F_q", chunks(a["L1_xattn_Wq"]))
    put("F_k", a["L1_xattn_Wk"])
    put("F_v", a["L1_xattn_Wv"])
    put("F_o", chunks(a["L1_xattn_Wo"]))
    put("G_gate", chunks(a["L1_ffn_gate_w"].T))

    def putcol(name, v):
        o = WOFF["cols"][0] + COLS[name]
        wt[:v.shape[0], o:o + v.shape[1]] = v

    putcol("rb", np.concatenate([a["L0_attn_rff_bias"]] * 2)[:, None])
    putcol("half_pi", np.full((RF, 1), math.pi / 2, f32))
    for name, key in (("B_bq", "L0_xattn_bq"), ("C_s", "L0_ffn_ln1_scale"), ("C_b", "L0_ffn_ln1_shift"),
                      ("D_s", "L0_ffn_ln2_scale"), ("D_b", "L0_ffn_ln2_shift"), ("F_bq", "L1_xattn_bq"),
                      ("F_bk", "L1_xattn_bk")):
        putcol(name, a[key].reshape(DC, P).T)
    putcol("log_temp", np.broadcast_to(a["L0_attn_log_temp"].reshape(1, 1), (P, 1)))

    rv = {"A_in": np.concatenate([a["L0_attn_b_shell"], a["L0_attn_b_charge"], a["L0_attn_b_v"]]),
          "A_out": a["L0_attn_b_out"], "B_v": a["L0_xattn_bv"], "C_o": a["L0_ffn_bo"], "F_v": a["L1_xattn_bv"],
          "F_o": a["L1_xattn_bo"], "gq": a["L1_attn_gq"], "gk": a["L1_attn_gk"], "gv": a["L1_attn_gv"],
          "go": a["L1_attn_go"]}
    rows = np.ascontiguousarray(np.broadcast_to(np.concatenate([rv[n] for n, _ in RCOLS])[None], (P, NR)))

    cst = np.zeros((P, NCST), f32)

    def putc(name, v):
        o, n = COFF[name]
        cst[:v.shape[0], o:o + n] = v

    i = np.arange(S)
    putc("ident", np.eye(P, dtype=f32))
    putc("ones", np.ones((P, P), f32))
    putc("decay", (np.exp(-0.03 * np.abs(i[:, None] - i[None, :])) * PHI_SCALE2).astype(f32))
    putc("causal", np.where(i[:, None] >= i[None, :], 0.0, NEG).astype(f32))
    putc("head", (np.arange(P)[:, None] // HD == np.arange(HC)[None, :]).astype(f32))
    putc("before", np.broadcast_to((np.arange(8)[None, :] < np.arange(8)[:, None]).astype(f32).reshape(1, 64), (P, 64)))
    putc("mhalf", np.full((P, 8), -0.5, f32))
    putc("eps", np.full((P, 4), EPS, f32))

    c = a["ctx_512"].reshape(NG, NB, LC, DX)
    cpad = np.concatenate([c, np.zeros((NG, NB, LP - LC, DX), f32)], 2)
    arrays = {
        "x_d": np.ascontiguousarray(a["x"].reshape(NG, NB, S, D).transpose(0, 2, 1, 3)),
        "ctxT_d": np.ascontiguousarray(cpad.transpose(0, 3, 1, 2)),
        "ctx_d": np.ascontiguousarray(cpad.reshape(NG, NB, KC, KW, DX).transpose(0, 3, 1, 2, 4)),
        "w_d": wt, "r_d": rows, "c_d": cst,
        "wq_d": np.concatenate([chunks(a["L1_attn_" + n].T) for n in ("wq", "wk", "wv", "wo")], 1),
        "e0_d": np.stack([np.concatenate([chunks(a["L0_ffn_w1"][e]), chunks(a["L0_ffn_w2"][e]),
                                          chunks(a["L0_ffn_w3"][e])], 1) for e in range(E0)]),
        "e1_d": np.concatenate(
            [np.concatenate([chunks(a["L1_ffn_Wg"][e]), chunks(a["L1_ffn_Wu"][e]), a["L1_ffn_Wd"][e]], 1)
             for e in range(E1 - 1)]
            + [chunks(a["L1_ffn_sWg"]), chunks(a["L1_ffn_sWu"]), a["L1_ffn_sWd"]], 1),
    }
    nc = bacc.Bacc("TRN2", target_bir_lowering=False, num_devices=1)
    aps = [nc.dram_tensor(n, v.shape, F32, kind="ExternalInput").ap() for n, v in arrays.items()]
    out = nc.dram_tensor("out_0", (NG, S, NB, D), F32, kind="ExternalOutput").ap()
    decoder(nc, *aps, out)
    r = run_bass_kernel_spmd(nc, [arrays], core_ids=[0])
    return np.ascontiguousarray(r.results[0]["out_0"].reshape(NG, S, NB, D).transpose(0, 2, 1, 3)).reshape(NSEQ, S, D)
```

```python
import math
from contextlib import ExitStack

import numpy as np

import concourse.bass as bass
from concourse import mybir

ACT = mybir.ActivationFunctionType
ALU = mybir.AluOpType
F32 = mybir.dt.float32
F32R = mybir.dt.float32r
BF16 = mybir.dt.bfloat16
AX = mybir.AxisListType.X

NSEQ, S, D = 16, 100, 256
NB = 4
NG = NSEQ // NB
NT = NB * S
HB, HT = NB // 2, NB * S // 2
P = 128
DC = D // P
LC, DX = 361, 128
KC = 3
KW = 121
LP = KC * KW
NH, HD = 16, 16
HC = NH // DC
SH, RF, ORD = 64, 32, 5
E0, HID0 = 8, 512
E1, HID1 = 9, 128
MC0 = HID0 // P
W0 = DC * HID0 * 2 + MC0 * D
NPIECE = 3 * MC0
WP = W0 // NPIECE
EPS = 1e-5
EPS_RMS = 1e-6
MAGIC = 12582912.0
TWO_PI_HI = 6.28125
TWO_PI_LO = 2 * math.pi - TWO_PI_HI
NEG = -1e30
MAGS = [math.sqrt(abs((-1.0) ** m / math.factorial(m)) + 1e-10) for m in range(ORD)]
RFF_SCALE = math.sqrt(2.0 / (2 * RF)) * math.sqrt(math.exp(-0.5))
PHI_SCALE2 = (MAGS[0] * RFF_SCALE) ** 2

WCOLS = [("A_in", DC * 321), ("A_omega", P), ("A_comb", 320), ("A_out", DC * D),
         ("B_q", DC * D), ("B_kT", DC * DX), ("B_bk", DC), ("B_v", D),
         ("C_q", DC * D), ("C_k", DC * D), ("C_v", DC * D), ("C_o", DC * D), ("D_gate", DC * 8),
         ("F_q", DC * D), ("F_k", D), ("F_v", D), ("F_o", DC * D), ("G_gate", DC * 8),
         ("cols", 24)]
WOFF, _o = {}, 0
for _n, _w in WCOLS:
    WOFF[_n] = (_o, _w)
    _o += _w
NW = _o
COLS = {"rb": 0, "half_pi": 1, "B_bq": 2, "C_s": 4, "C_b": 6, "D_s": 8, "D_b": 10, "F_bq": 12, "F_bk": 14,
        "log_temp": 16}
RCOLS = [("A_in", 321), ("A_out", D), ("B_v", D), ("C_o", D), ("F_v", D), ("F_o", D),
         ("gq", D), ("gk", D), ("gv", D), ("go", D)]
ROFF, _o = {}, 0
for _n, _w in RCOLS:
    ROFF[_n] = (_o, _w)
    _o += _w
NR = _o
CCOLS = [("ident", P), ("ones", P), ("decay", S), ("causal", S), ("head", HC), ("before", 64), ("mhalf", 8), ("eps", 4)]
COFF, _o = {}, 0
for _n, _w in CCOLS:
    COFF[_n] = (_o, _w)
    _o += _w
NCST = _o
VU = 2 * HC * P
NVU = 6


class Signal:

    def __init__(self, sem, stride, base=0, turns=1):
        self.sem, self.stride, self.base, self.turns = sem, stride, base, turns

    def at(self, it, k=1, half=0):
        return it * self.stride + (self.base + self.turns * (k - 1) + half + 1)

    def free(self, it, k=1):
        return it * self.stride + k


def in_turn(*streams):
    streams = list(streams)
    while streams:
        for st in list(streams):
            if next(st, "over") == "over":
                streams.remove(st)


def decoder(nc, x_d, ctxT_d, ctx_d, w_d, r_d, c_d, wq_d, e0_d, e1_d, out_d):
    with ExitStack() as ctx:
        def sb(name, shape, dt=F32):
            return ctx.enter_context(nc.sbuf_tensor(name, shape, dt))

        def sig(name, stride=1, base=0):
            return Signal(ctx.enter_context(nc.semaphore(name)), stride, base)

        ps = ctx.enter_context(nc.psum_tensor("ps", [P, 8, 512], F32))

        wt = sb("wt", [P, NW])
        rows = sb("rows", [P, NR])
        cst = sb("cst", [P, NCST])
        wtern = sb("wtern", [P, 4, DC, D], BF16)
        experts_start = -(-nc.sbuf_base // 32) * 32
        experts = sb("experts", [P, 2 * W0 + 768])
        xall = sb("xall", [S, NSEQ, D])
        hT_all = sb("hT_all", [P, DC, NG * NT])
        gates_all = sb("gates_all", [S, NSEQ, 8])
        identb = sb("identb", [P, P], BF16)
        causalb = sb("causalb", [S, NB, S], BF16)
        small = sb("small", [P, 512])
        ctxT = sb("ctxT", [P, NB, LP])
        work_start = -(-nc.sbuf_base // 32) * 32
        spread = sb("spread", [P, NVU, VU])
        probs = sb("probs", [S, 2, 800])
        probsT = sb("probsT", [P, 2, 800])
        headbd = sb("headbd", [P, 2, HC, S])
        xin = sb("xin", [S, NB, D])
        x = sb("x", [S, NB, D])
        y = sb("y", [S, NB, D])
        xn = sb("xn", [S, NB, D])
        hT = sb("hT", [P, DC, NT])
        qT = sb("qT", [P, DC, NT])
        kT = sb("kT", [P, 2, DC * LC + 80])
        xqT = sb("xqT", [P, DC, NT], BF16)
        xq = sb("xq", [S, NB, D], BF16)
        place = [work_start]

        def over(name, shape, dt):
            t = nc.alloc_sbuf_tensor_at(name, shape, dt, offset=place[0])
            place[0] += 4 * int(np.prod(shape[1:]))
            assert place[0] <= nc.sbuf_base
            return t

        x_hi = over("x_hi", [P, DC, NG * NT], F32R)
        x_lo = over("x_lo", [P, DC, NG * NT], F32R)
        w_hi = over("w_hi", [P, 2, W0], F32R)
        hid_hi = over("hid_hi", [P, 2, MC0, NT], F32R)
        hid_lo = over("hid_lo", [P, 2, MC0, NT], F32R)
        hid = over("hid", [P, 2, NT], F32)
        silu = over("silu", [P, 2, NT], F32)
        gate_b = over("gate_b", [P, 2, NG, NT], F32)
        gated = over("gated", [P, DC, NT], F32)
        w_lo = nc.alloc_sbuf_tensor_at("w_lo", [P, 2, W0], F32R, offset=experts_start)

        keysT = kT[:].rearrange("p s n -> p (s n)")[:, 0:DC * NT].rearrange("p (c n) -> p c n", c=DC)
        def wv(name, chunks=None, rows_=P):
            o, n = WOFF[name]
            v = wt[0:rows_, o:o + n]
            return v.rearrange("p (c n) -> p c n", c=chunks) if chunks else v

        def col(name, c=0, p=P):
            o = WOFF["cols"][0] + COLS[name] + c
            return wt[0:p, o:o + 1]

        def row(name, p=S):
            o, n = ROFF[name]
            return rows[0:p, o:o + n]

        def cs(name, p=P):
            o, n = COFF[name]
            return cst[0:p, o:o + n]

        ident = cs("ident")
        identS = ident[0:S, 0:S]
        scr = spread[:, 2:6, :].rearrange("p u n -> p (u n)")
        a_in = scr[0:S, 0:NB * 321].rearrange("p (b n) -> p b n", b=NB)
        a_sqw = scr[0:S, 1300:1300 + NB * P].rearrange("p (b n) -> p b n", b=NB)
        a_sq = a_sqw[:, :, 0:SH]
        a_shT = scr[0:SH, 1900:2300]
        a_ang = scr[0:SH, 2300:2700]
        a_lg = scr[0:S, 2300:2700].rearrange("p (b n) -> p b n", b=NB)
        a_k = scr[0:SH, 2700:3100]
        a_trig = scr[0:SH, 3100:3500]
        a_phiw = scr[0:S, 3500:3500 + NB * P].rearrange("p (b n) -> p b n", b=NB)
        a_phi = a_phiw[:, :, 0:SH]
        a_phiT = scr[0:SH, 7460:7860]
        ctxk = scr[0:KW, 4300:4300 + NB * KC * DX].rearrange("p (b c n) -> p b c n", b=NB, c=KC)
        b_e = scr[0:S, 5900:5900 + NB * LP].rearrange("p (b n) -> p b n", b=NB)
        b_eT = scr[0:KW, 0:NB * KC * S].rearrange("p (b n) -> p b n", b=NB)
        decay = scr[0:S, 7360:7460]
        c_v = scr[0:S, 0:NB * D].rearrange("p (b n) -> p b n", b=NB)
        f_e = probs[:].rearrange("p s n -> p (s n)")[:, 0:4 * LP].rearrange("p (s i n) -> p s i n", s=2, i=2)
        f_eT = probsT[0:KW].rearrange("p s n -> p (s n)")[:, 0:4 * KC * S].rearrange(
            "p (s i n) -> p s i n", s=2, i=2)
        g_hid, g_act = probsT[:, :, 0:NT], probsT[:, :, NT:2 * NT]
        sm_o = [0]

        def smt(n, p=S, shape=None):
            v = small[0:p, sm_o[0]:sm_o[0] + n]
            sm_o[0] += n
            return v.rearrange("p (b n) -> p b n", b=shape) if shape else v

        stats = smt(NB * 6, shape=NB)
        mv = smt(NB * 2, shape=NB)
        var_e, r1, r2, t1 = smt(4), smt(4), smt(4), smt(4)
        a_ss, a_rn, a_q, a_nm, a_sum, a_rs = smt(4), smt(4), smt(4), smt(4), smt(4), smt(4)
        b_qbk, b_mx, b_nm, b_sum, b_rs = smt(4), smt(4), smt(4), smt(4), smt(4)
        h_nm = smt(32, shape=2)
        h_sum = smt(64, shape=NB)
        h_rs = smt(64, shape=NB)
        g_s, g_e, g_rank = smt(32, shape=NB), smt(32, shape=NB), smt(32, shape=NB)
        g_m, g_r = smt(4), smt(4)
        wsum, wscale, wrecip = smt(4, P), smt(4, P), smt(4, P)
        tempc = smt(4, P)
        q_am, q_sc, q_isc = smt(4), smt(4), smt(12, shape=3)
        bq4 = smt(2, P)
        assert sm_o[0] <= 512
        gpair = g_rank.rearrange("p b n -> p (b n)").rearrange("p (s q) -> p s q", s=2)

        ld = {n: sig("ld_" + n) for n in ("wt", "rows", "cst", "wq", "x", "ctxT", "ctxk", "ctxT3", "e1", "out")}
        ld_e0 = [sig(f"ld_e0_{i}") for i in range(2)]
        prep_abs = sig("prep_abs")
        prep_sum = sig("prep_sum")
        prep_b = sig("prep_b")
        prep_t = sig("prep_t")
        prep_e = sig("prep_e")
        x_free = sig("x_free")
        tern_go = sig("tern_go")
        names = {}

        def stage(prefix, table):
            for n, per in table.items():
                names[prefix + n] = sig(prefix + n, per)

        def halves(name, per, phase1, phase3=""):
            sem = ctx.enter_context(nc.semaphore(name))
            base = 0
            for stages in (phase1, phase3):
                for i, p in enumerate(stages):
                    names[f"{p}_{name}"] = Signal(sem, 2 * per * len(stages), base + 2 * per * i, 2)
                base += 2 * per * NG * len(stages)

        def shared(name, per, phase1, phase3):
            sem = ctx.enter_context(nc.semaphore(name))
            names[f"{phase1}_{name}"] = Signal(sem, per)
            names[f"{phase3}_{name}"] = Signal(sem, per, per * NG)

        for n, stages1, stages3 in (("mv", "ABCD", "EFG"), ("rstd", "ABCD", "EFG"), ("xn", "ABCD", "FG"),
                                    ("hTp", "ABCD", "FG"), ("hT", "ABCD", "FG"),
                                    ("out", "ABC", "EF"), ("xb", "ABC", "F"),
                                    ("qTp", "BC", "EF"), ("qT", "BC", "EF"),
                                    ("kTp", "C", "E"), ("kT", "C", "E"), ("vp", "C", "E"), ("v", "C", "E"),
                                    ("rx", "C", "EF"), ("rTp", "C", "EF"), ("rT", "C", "EF"), ("yT", "C", "EF"),
                                    ("gs", "D", "G"), ("gm", "D", "G"), ("ge", "D", "G"), ("g", "D", "G")):
            halves(n, 1, stages1, stages3)
        for n in ("in_p", "in", "ss", "rn", "q", "shn", "shTp", "shT", "angp", "ang", "trig", "comb", "phi",
                  "phiTp", "phiT", "lg", "nm", "e", "p", "pTp", "pT", "oTp", "oT"):
            sem_name = "A" + n
            halves(sem_name, 1, "A")
            names["A_" + n] = names.pop("A_" + sem_name)
        for n in ("kqTp", "kqT", "qbkp", "s", "nm", "e", "p", "pTp", "pT", "oTp", "oT"):
            sem_name = "B" + n
            halves(sem_name, 1, "B")
            names["B_" + n] = names.pop("B_" + sem_name)
        for n, per in (("xq", 4), ("xqTp", 4), ("xqT", 4), ("bc", 2), ("bcp", 2), ("sc", 2), ("ytp", 1), ("ssr", 1),
                       ("sso", 1)):
            halves(n, per, "", "E")
        for n, per in {"bd": 8, "vs": 4, "s": 8, "sub": 8, "e": 8, "pTp": 8, "pT": 8, "av": 8, "rs": 1}.items():
            shared(n, per, "C", "E")
        stage("F_", {"kvp": 20, "kv": 20, "bd": 8, "s": 32, "nm": 32, "e": 32, "pTp": 32,
                     "pT": 32, "av": 32, "o": 4, "rs": 1})
        stage("G_", {"h": 9, "act": 9, "hid": 9, "o": 9, "acc": 9})
        m_x = sig("m_x")
        m_whi = sig("m_whi", 2 * NPIECE)
        m_wlo = sig("m_wlo", 2 * NPIECE)
        m_gr = sig("m_gr")
        m_gp = sig("m_gp", 2)
        m_gb = sig("m_gb", 2)
        m_h = sig("m_h", 2 * NG * MC0)
        m_act = sig("m_act", 2 * NG * MC0)
        m_hid = sig("m_hid", 2 * NG * MC0, 2)
        m_lo = sig("m_lo", 2 * NG * MC0)
        m_out = sig("m_out", 2 * NG, 2 * NG)
        m_acc = sig("m_acc", 2 * NG, 2)
        m_sum = sig("m_sum")
        m_back = sig("m_back")

        def W(e, name, it, k=1, half=0):
            e.wait_ge(names[name].sem, names[name].at(it, k, half))

        def inc(ins, name):
            ins.then_inc(names[name].sem, 1)

        def bank(b, p=P, n=512, lo=0):
            return ps[0:p, b, lo:lo + n]

        def seqs(h):
            return range(HB * h, HB * (h + 1))

        def own(h):
            return slice(HB * h, HB * (h + 1))

        def tok(h):
            return slice(HT * h, HT * (h + 1))

        def norm_dve(e, pre, g, h, src, xn_out):
            for b in seqs(h):
                e.bn_stats(stats[:, b, :], src[:, b, :])
            e.drain()
            for b in seqs(h):
                ins = e.bn_aggr(mv[:, b, :], stats[:, b, :])
            inc(ins, pre + "mv")
            e.drain()
            yield
            W(e, pre + "rstd", g, 1, h)
            for b in seqs(h):
                ins = e.tensor_scalar(xn_out[:, b, :], src[:, b, :], mv[:, b, 0:1], r1[:, b:b + 1],
                                      ALU.subtract, ALU.mult)
            return ins

        def norm_pool(e, pre, g, h, eps2=None, fold=False):
            o = own(h)
            yield
            W(e, pre + "mv", g, 1, h)
            e.tensor_tensor(var_e[:, o], mv[:, o, 1], cs("eps", S)[:, 0:HB], ALU.add)
            e.drain()
            ins = e.tensor_tensor(r1[:, o], var_e[:, o], cs("mhalf", S)[:, 0:HB], ALU.pow)
            if eps2 is not None:
                e.drain()
                e.tensor_tensor(t1[:, o], r1[:, o], r1[:, o], ALU.mult)
                e.drain()
                e.tensor_tensor(t1[:, o], t1[:, o], mv[:, o, 1], ALU.mult)
                e.drain()
                e.tensor_scalar(t1[:, o], t1[:, o], eps2, None, ALU.add)
                e.drain()
                ins = e.tensor_tensor(r2[:, o], t1[:, o], cs("mhalf", S)[:, 0:HB], ALU.pow)
                if fold:
                    e.drain()
                    ins = e.tensor_tensor(r1[:, o], r1[:, o], r2[:, o], ALU.mult)
            inc(ins, pre + "rstd")

        def part(b0, n=HT, p=P, chunks=DC):
            return ps[0:p, b0, 0:chunks * n].rearrange("p (c n) -> p c n", c=chunks)

        def toT_pe(e, pre, g, h, name, b0, src, ready):
            yield
            W(e, ready[0], g, ready[1], h)
            for c in range(DC):
                for i, b in enumerate(seqs(h)):
                    ins = e.transpose(part(b0)[:, c, i * S:(i + 1) * S], src[:, b, c * P:(c + 1) * P], identS)
            inc(ins, pre + name)

        def toT_act(e, pre, g, h, pname, name, b0, dst, scale=None, bias=None):
            yield
            W(e, pre + pname, g, 1, h)
            if scale:
                for c in range(DC):
                    ins = e.activation(dst[:, c, tok(h)], part(b0)[:, c, :], ACT.Identity,
                                       scale=col(scale, c), bias=col(bias, c))
            else:
                ins = e.activation(dst[:, :, tok(h)], part(b0), ACT.Copy)
            inc(ins, pre + name)

        def projT_pe(e, h, w, src, b0, name):
            for m in range(DC):
                for c in range(DC):
                    ins = e.matmul(part(b0)[:, m, :], w[:, c, m * P:(m + 1) * P], src[:, c, tok(h)],
                                   start=(c == 0), stop=(c == DC - 1))
            inc(ins, name)

        def proj_pe(e, h, w, srcT, b0, name):
            for i, b in enumerate(seqs(h)):
                for c in range(DC):
                    ins = e.matmul(ps[0:S, b0, i * D:(i + 1) * D], srcT[:, c, b * S:(b + 1) * S], w[:, c, :],
                                   start=(c == 0), stop=(c == DC - 1))
            inc(ins, name)

        def tokens(b0, p=S):
            return ps[0:p, b0, 0:HB * D].rearrange("p (b n) -> p b n", b=HB)

        def pair(b0, p=S):
            return ps[0:p, b0:b0 + 2, :].rearrange("p a (b n) -> p (a b) n", b=2)

        def diag(unit, p):
            base = spread[0:p, unit, :]
            return bass.AP(tensor=base.tensor, offset=base.offset,
                           ap=[list(base.ap[0]), [HC * P, DC], [P + HD, HC], [1, HD]])

        def window(unit, p, c, h):
            return spread[0:p, unit, (c * HC + h) * P:(c * HC + h + 1) * P]

        def spread_recips_pool(e, pre, g, h):
            yield
            W(e, pre + "rs", g)
            o = own(h)
            inc(e.tensor_tensor(xn[:, o, :].rearrange("p b (h d) -> p b h d", d=HD),
                                h_rs[:, o, :].unsqueeze(3).broadcast_to([S, HB, NH, HD]),
                                cs("ones", S)[:, 0:1].unsqueeze(2).unsqueeze(3).broadcast_to([S, HB, NH, HD]),
                                ALU.mult), pre + "rx")

        def self_pe(e, pre, it):
            def scores(u):
                b, c = divmod(u, 2)
                W(e, pre + "bd", it, u + 1)
                if u >= 2:
                    W(e, pre + "sub", it, u - 1)
                for i in range(2):
                    o = bank(2 * (u % 2) + i, S, 4 * S)
                    e.matmul(o, qT[:, c, b * S:(b + 1) * S],
                             headbd[:, u % 2, 4 * i:4 * i + 4, :].rearrange("p h n -> p (h n)"),
                             start=True, stop=False)
                    ins = e.matmul(o, identb[0:S, 0:S], causalb[:].rearrange("p h n -> p (h n)"),
                                   start=False, stop=True)
                inc(ins, pre + "s")

            def turn(u):
                W(e, pre + "e", it, u + 1)
                if u >= 1:
                    W(e, pre + "pT", it, u)
                for h in range(HC):
                    ins = e.transpose(ps[0:S, 4 + h // 4, (h % 4) * S:(h % 4 + 1) * S],
                                      probs[:, u % 2, h * S:(h + 1) * S], identS)
                inc(ins, pre + "pTp")

            def values(u):
                b, c = divmod(u, 2)
                W(e, pre + "pT", it, u + 1)
                W(e, pre + "vs", it, b + 1)
                for h in range(HC):
                    ins = e.matmul(ps[:, 6 + c, b * S:(b + 1) * S], window(b % 2, S, c, h),
                                   probsT[0:S, u % 2, h * S:(h + 1) * S], start=(h == 0), stop=(h == HC - 1))
                inc(ins, pre + "av")

            for u in range(2 * NB + 2):
                if u < 2 * NB:
                    scores(u)
                if 1 <= u <= 2 * NB:
                    turn(u - 1)
                if u >= 2:
                    values(u - 2)
        def self_dve(e, pre, it):
            def shift(u):
                W(e, pre + "s", it, u + 1)
                sc = ps[0:S, 2 * (u % 2):2 * (u % 2) + 2, 0:4 * S].rearrange("p a (h n) -> p a h n", h=4)
                nm = h_nm[:, u % 2, 0:HC].rearrange("p (a h) -> p a h", a=2)
                e.tensor_reduce(nm, sc, AX, ALU.max)
                e.drain()
                if u >= 2:
                    W(e, pre + "pTp", it, u - 1)
                for i in range(2):
                    ins = e.tensor_tensor(
                        probs[:, u % 2, i * 4 * S:(i + 1) * 4 * S].rearrange("p (h n) -> p h n", h=4),
                        sc[:, i, :, :], nm[:, i, :].unsqueeze(2).broadcast_to([S, 4, S]), ALU.subtract)
                inc(ins, pre + "sub")

            def total(u):
                b, c = divmod(u, 2)
                W(e, pre + "e", it, u + 1)
                e.tensor_reduce(h_sum[:, b, c * HC:(c + 1) * HC],
                                probs[:, u % 2, :].rearrange("p (h n) -> p h n", h=HC), AX, ALU.add)

            for u in range(2 * NB + 1):
                if u < 2 * NB:
                    shift(u)
                if u >= 1:
                    total(u - 1)
            e.drain()
            inc(e.reciprocal(h_rs, h_sum), pre + "rs")

        def self_act(e, pre, it):
            def expo(u):
                W(e, pre + "sub", it, u + 1)
                inc(e.activation(probs[:, u % 2, :], probs[:, u % 2, :], ACT.Exp), pre + "e")

            def evac(u):
                W(e, pre + "pTp", it, u + 1)
                if u >= 2:
                    W(e, pre + "av", it, u - 1)
                ins = e.activation(probsT[0:S, u % 2, :].rearrange("p (a n) -> p a n", a=2),
                                   ps[0:S, 4:6, 0:4 * S], ACT.Copy)
                inc(ins, pre + "pT")

            for u in range(2 * NB + 1):
                if u < 2 * NB:
                    expo(u)
                if u >= 1:
                    evac(u - 1)

        def self_pool(e, pre, it, vsrc):
            for u in range(2 * NB):
                b, c = divmod(u, 2)
                if u == 0:
                    W(e, pre + "kT", it, 1, 1)
                if u >= 2:
                    W(e, pre + "s", it, u - 1)
                inc(e.tensor_tensor(headbd[:, u % 2],
                                    keysT[:, c, b * S:(b + 1) * S].unsqueeze(1).broadcast_to([P, HC, S]),
                                    cs("head").unsqueeze(2).broadcast_to([P, HC, S]), ALU.mult), pre + "bd")
                if c == 0:
                    if b == 0:
                        W(e, pre + "v", it, 1, 1)
                    if b >= 2:
                        W(e, pre + "av", it, 2 * (b - 1))
                    inc(e.tensor_tensor(diag(b % 2, S), vsrc[:, b, :].rearrange("p (c h d) -> p c h d", c=DC, h=HC),
                                        cs("ones", S)[:, 0:1].unsqueeze(2).unsqueeze(3).broadcast_to([S, DC, HC, HD]),
                                        ALU.mult), pre + "vs")

        def gate_pe(e, pre, g, h, w):
            yield
            W(e, pre + "hT", g, 1, h)
            for i, b in enumerate(seqs(h)):
                for c in range(DC):
                    ins = e.matmul(ps[0:S, 4 * h + 1, i * 8:(i + 1) * 8], hT[:, c, b * S:(b + 1) * S], w[:, c, :],
                                   start=(c == 0), stop=(c == DC - 1))
            inc(ins, pre + "gs")

        def gate_act(e, pre, g, h):
            yield
            W(e, pre + "gm", g, 1, h)
            inc(e.activation(g_e[:, own(h), :], g_e[:, own(h), :], ACT.Exp), pre + "ge")

        def gate_dve(e, pre, g, h, probs_first, out_gates):
            o = own(h)
            s_, e_, m_, r_, k_ = g_s[:, o, :], g_e[:, o, :], g_m[:, o], g_r[:, o], g_rank[:, o, :]
            yield
            W(e, pre + "gs", g, 1, h)
            e.tensor_scalar(s_, ps[0:S, 4 * h + 1, 0:8 * HB].rearrange("p (b n) -> p b n", b=HB), 1.0, None, ALU.mult)
            e.drain()
            e.tensor_reduce(m_, s_, AX, ALU.max)
            e.drain()
            bc = lambda v: v.unsqueeze(2).broadcast_to([S, HB, 8])
            inc(e.tensor_tensor(e_, s_, bc(m_), ALU.subtract), pre + "gm")
            yield
            W(e, pre + "ge", g, 1, h)
            if probs_first:
                e.tensor_reduce(m_, e_, AX, ALU.add)
                e.drain()
                e.reciprocal(r_, m_)
                e.drain()
                e.tensor_tensor(e_, e_, bc(r_), ALU.mult)
                e.drain()
            key = e_ if probs_first else s_
            sh = [S, HB, 8, 8]
            mine = key.unsqueeze(3).broadcast_to(sh)
            other = key.unsqueeze(2).broadcast_to(sh)
            beats = y[:, HB * h, 0:HB * 64].rearrange("p (b e f) -> p b e f", b=HB, e=8)
            ties = y[:, HB * h + 1, 0:HB * 64].rearrange("p (b e f) -> p b e f", b=HB, e=8)
            before = cs("before", S).rearrange("p (e f) -> p e f", e=8).unsqueeze(1).broadcast_to(sh)
            e.tensor_tensor(beats, other, mine, ALU.is_gt)
            e.tensor_tensor(ties, other, mine, ALU.is_equal)
            e.drain()
            e.tensor_tensor(ties, ties, before, ALU.mult)
            e.drain()
            e.tensor_tensor(beats, beats, ties, ALU.add)
            e.drain()
            e.tensor_reduce(k_, beats, AX, ALU.add)
            e.drain()
            e.scalar_tensor_tensor(e_, k_, 1.5, e_, ALU.is_lt, ALU.mult)
            e.drain()
            e.tensor_reduce(m_, e_, AX, ALU.add)
            e.drain()
            if probs_first:
                e.tensor_scalar(m_, m_, 1e-20, None, ALU.add)
                e.drain()
            e.reciprocal(r_, m_)
            e.drain()
            inc(e.tensor_tensor(out_gates, e_, bc(r_), ALU.mult), pre + "g")
            e.drain()

        block = ctx.enter_context(nc.Block())

        @block.sync
        def _(e):
            def load_group(g):
                e.dma_start(xin[:], x_d[g]).then_inc(ld["x"].sem, 16)
                e.dma_start(ctxT[:], ctxT_d[g]).then_inc(ld["ctxT"].sem, 16)
                e.dma_start(ctxk, ctx_d[g]).then_inc(ld["ctxk"].sem, 16)

            e.dma_start(xin[:], x_d[0]).then_inc(ld["x"].sem, 16)
            e.dma_start(cst[:], c_d).then_inc(ld["cst"].sem, 16)
            e.dma_start(wt[:], w_d).then_inc(ld["wt"].sem, 16)
            e.dma_start(rows[:], r_d).then_inc(ld["rows"].sem, 16)
            e.dma_start(ctxT[:], ctxT_d[0]).then_inc(ld["ctxT"].sem, 16)
            e.dma_start(ctxk, ctx_d[0]).then_inc(ld["ctxk"].sem, 16)
            e.dma_start(experts[:, 0:4 * DC * D], wq_d).then_inc(ld["wq"].sem, 16)
            with e.Fori(0, NG - 1) as g:
                W(e, "B_oTp", g, 1, 1)
                load_group(g + 1)
            e.wait_ge(tern_go.sem, 1)
            with e.Fori(0, E0 // 2) as ep:
                for s in range(2):
                    e.wait_ge(m_out.sem, m_out.free(ep, NG * (s + 1)))
                    e.dma_start(experts[:, s * W0:(s + 1) * W0], e0_d[2 * ep + s]).then_inc(ld_e0[s].sem, 16)
            W(e, "B_oTp", NG - 1, 1, 1)
            e.dma_start(ctxT[:], ctxT_d[0]).then_inc(ld["ctxT3"].sem, 16)
            e.wait_ge(m_out.sem, m_out.at(E0 // 2 - 1, 2 * NG))
            e.dma_start(experts[:, 0:E1 * 768], e1_d).then_inc(ld["e1"].sem, 16)
            e.sem_inc(x_free.sem, 1)
            with e.Fori(0, NG - 1) as g:
                W(e, "F_kvp", g, 5 * NB)
                e.dma_start(ctxT[:], ctxT_d[g + 1]).then_inc(ld["ctxT3"].sem, 16)
                W(e, "G_acc", g, E1)
                e.dma_start(out_d[g], x[:]).then_inc(ld["out"].sem, 16)
                e.wait_ge(ld["out"].sem, g * 16 + 16)
                e.sem_inc(x_free.sem, 1)
            W(e, "G_acc", NG - 1, E1)
            e.dma_start(out_d[NG - 1], x[:]).then_inc(ld["out"].sem, 16)
            e.wait_ge(ld["out"].sem, NG * 16)

        @block.tensor
        def _(e):
            e.wait_ge(ld["cst"].sem, 16)
            e.wait_ge(prep_abs.sem, 1)
            inc_ = e.matmul(bank(0, n=4), cs("ones"), wsum, start=True, stop=True)
            inc_.then_inc(prep_sum.sem, 1)
            e.wait_ge(ld["wt"].sem, 16)
            e.wait_ge(prep_b.sem, 1)

            def before_c(g, h):
                b0, t, bs = 4 * h, tok(h), list(enumerate(seqs(h)))
                yield from toT_pe(e, "A_", g, h, "hTp", b0, xn, ("A_xn", 1))
                yield
                W(e, "A_hT", g, 1, h)
                w = wv("A_in", DC)
                for i, b in bs:
                    for c in range(DC):
                        ins = e.matmul(bank(b0 + 1 + i, S, 321), hT[:, c, b * S:(b + 1) * S], w[:, c, :],
                                       start=(c == 0), stop=(c == DC - 1))
                inc(ins, "A_in_p")
                yield
                W(e, "A_shn", g, 1, h)
                for i, b in bs:
                    ins = e.transpose(ps[:, b0, i * S:(i + 1) * S], a_sqw[:, b, :], identS)
                inc(ins, "A_shTp")
                yield
                W(e, "A_shT", g, 1, h)
                inc(e.matmul(bank(b0 + 3, n=HT), wv("A_omega", rows_=SH), a_shT[:, t], start=True, stop=True), "A_angp")
                yield
                W(e, "A_trig", g, 1, h)
                for i, b in bs:
                    ins = e.matmul(bank(b0 + 1 + i, S, 320), a_trig[:, b * S:(b + 1) * S], wv("A_comb", rows_=SH),
                                   start=True, stop=True)
                inc(ins, "A_comb")
                yield
                W(e, "A_phi", g, 1, h)
                for i, b in bs:
                    ins = e.transpose(ps[:, b0, i * S:(i + 1) * S], a_phiw[:, b, :], identS)
                inc(ins, "A_phiTp")
                yield
                W(e, "A_phiT", g, 1, h)
                for i, b in bs:
                    pb = a_phiT[:, b * S:(b + 1) * S]
                    ins = e.matmul(ps[0:S, b0 + 3, i * S:(i + 1) * S], pb, pb, start=True, stop=True)
                inc(ins, "A_lg")
                yield
                W(e, "A_p", g, 1, h)
                for i, b in bs:
                    ins = e.transpose(ps[0:S, b0, i * S:(i + 1) * S], a_lg[:, b, :], identS)
                inc(ins, "A_pTp")
                yield
                W(e, "A_pT", g, 1, h)
                for c in range(DC):
                    for i, b in bs:
                        ins = e.matmul(part(b0 + 1)[:, c, i * S:(i + 1) * S], a_in[:, b, 65 + c * P:65 + (c + 1) * P],
                                       probsT[0:S, 0, b * S:(b + 1) * S], start=True, stop=True)
                inc(ins, "A_oTp")
                yield
                W(e, "A_oT", g, 1, h)
                proj_pe(e, h, wv("A_out", DC), qT, b0 + 2, "A_out")
                yield from toT_pe(e, "B_", g, h, "hTp", b0, xn, ("B_xn", 1))
                yield
                W(e, "B_hT", g, 1, h)
                projT_pe(e, h, wv("B_q", DC), hT, b0 + 1, "B_qTp")
                yield
                W(e, "B_qT", g, 1, h)
                for c in range(DC):
                    ins = e.matmul(bank(b0 + 2, n=HT), wv("B_kT", DC)[:, c, :], qT[:, c, t],
                                   start=(c == 0), stop=(c == DC - 1))
                inc(ins, "B_kqTp")
                for i, b in bs:
                    for c in range(DC):
                        ins = e.matmul(ps[0:S, b0 + 3, i:i + 1], qT[:, c, b * S:(b + 1) * S], wv("B_bk", DC)[:, c, :],
                                       start=(c == 0), stop=(c == DC - 1))
                inc(ins, "B_qbkp")
                yield
                W(e, "B_kqT", g, 1, h)
                e.wait_ge(ld["ctxT"].sem, g * 16 + 16)
                for i, b in bs:
                    ins = e.matmul(bank(b0 + 1 + i, S, LC), hT[:, 0, b * S:(b + 1) * S], ctxT[:, b, 0:LC],
                                   start=True, stop=True)
                inc(ins, "B_s")
                yield
                W(e, "B_p", g, 1, h)
                for i, b in bs:
                    for k in range(KC):
                        ins = e.transpose(ps[0:KW, b0 + 3 * i, k * S:(k + 1) * S], b_e[:, b, k * KW:(k + 1) * KW],
                                          identS)
                inc(ins, "B_pTp")
                yield
                W(e, "B_pT", g, 1, h)
                e.wait_ge(ld["ctxk"].sem, g * 16 + 16)
                for i, b in bs:
                    for k in range(KC):
                        ins = e.matmul(ps[:, b0 + 1, i * S:(i + 1) * S], ctxk[:, b, k, :], b_eT[:, b, k * S:(k + 1) * S],
                                       start=(k == 0), stop=(k == KC - 1))
                inc(ins, "B_oTp")
                yield
                W(e, "B_oT", g, 1, h)
                for i, b in bs:
                    ins = e.matmul(ps[0:S, b0 + 2, i * D:(i + 1) * D], hT[:, 1, b * S:(b + 1) * S],
                                   wv("B_v"), start=True, stop=True)
                inc(ins, "B_out")
                yield from toT_pe(e, "C_", g, h, "hTp", b0, xn, ("C_xn", 1))
                yield
                W(e, "C_hT", g, 1, h)
                proj_pe(e, h, wv("C_v", DC), hT, b0 + 1, "C_vp")
                projT_pe(e, h, wv("C_k", DC), hT, b0 + 2, "C_kTp")
                projT_pe(e, h, wv("C_q", DC), hT, b0 + 3, "C_qTp")

            def after_c(g, h):
                b0 = 4 * h
                yield from toT_pe(e, "C_", g, h, "rTp", b0, xn, ("C_rx", 1))
                yield
                W(e, "C_yT", g, 1, h)
                proj_pe(e, h, wv("C_o", DC), qT, b0 + 1, "C_out")
                yield from toT_pe(e, "D_", g, h, "hTp", b0, xn, ("D_xn", 1))
                yield from gate_pe(e, "D_", g, h, wv("D_gate", DC))

            with e.Fori(0, NG) as g:
                in_turn(before_c(g, 0), before_c(g, 1))
                W(e, "C_v", g, 1, 1)
                W(e, "C_kT", g, 1, 1)
                W(e, "C_qT", g, 1, 1)
                self_pe(e, "C_", g)
                in_turn(after_c(g, 0), after_c(g, 1))
            def product(out, w, rhs_hi, rhs_lo, start, stop):
                wh, wl = w
                e.matmul(out, wh, rhs_hi, start=start, stop=False)
                e.matmul(out, wh, rhs_lo, start=False, stop=False)
                return e.matmul(out, wl, rhs_hi, start=False, stop=stop)

            def weights(slot, o):
                return w_hi[:, slot, o:o + P], w_lo[:, slot, o:o + P]

            def up(ep, s, m):
                slot, gi = divmod(s, NG)
                t = slice(gi * NT, (gi + 1) * NT)
                if gi == 0 and m == 0:
                    e.wait_ge(m_wlo.sem, m_wlo.at(ep, NPIECE * (slot + 1)))
                if slot == 0 and m == 0:
                    e.wait_ge(m_x.sem, gi + 1)
                e.wait_ge(m_hid.sem, m_hid.free(ep, s * MC0 + m + 1))
                for i in range(2):
                    for c in range(DC):
                        ins = product(bank(2 * i + m % 2, n=NT), weights(slot, (i * DC + c) * HID0 + m * P),
                                      x_hi[:, c, t], x_lo[:, c, t], c == 0, c == DC - 1)
                ins.then_inc(m_h.sem, 1)

            def spread_gates(ep, slot):
                if slot == 0:
                    e.wait_ge(m_gr.sem, ep + 1)
                e.wait_ge(m_acc.sem, m_acc.free(ep, NG * slot + 2))
                for q in range(NSEQ):
                    ins = e.matmul(ps[:, 4 + q // NB, (q % NB) * S:(q % NB + 1) * S],
                                   gpair[:, slot, q:q + 1].broadcast_to([S, P]), identS, start=True, stop=True)
                ins.then_inc(m_gp.sem, 1)

            def down(ep, s):
                slot, gi = divmod(s, NG)
                e.wait_ge(m_lo.sem, m_lo.at(ep, MC0 * (s + 1)))
                if gi == 0:
                    e.wait_ge(m_gb.sem, m_gb.at(ep, slot + 1))
                e.wait_ge(m_acc.sem, m_acc.free(ep, s + 1))
                for m in range(DC):
                    for c in range(MC0):
                        ins = product(bank(4 + 2 * (s % 2) + m, n=NT),
                                      weights(slot, 2 * DC * HID0 + c * D + m * P),
                                      hid_hi[:, s % 2, c, :], hid_lo[:, s % 2, c, :], c == 0, c == MC0 - 1)
                ins.then_inc(m_out.sem, 1)

            def experts_pe(ep):
                for s in range(2 * NG):
                    up(ep, s, 0)
                    up(ep, s, 1)
                    if s >= 1:
                        down(ep, s - 1)
                    up(ep, s, 2)
                    up(ep, s, 3)
                    if s % NG == 0:
                        spread_gates(ep, s // NG)
                down(ep, 2 * NG - 1)

            with e.Fori(0, E0 // 2 - 1) as ep:
                experts_pe(ep)
            experts_pe(E0 // 2 - 1)
            e.wait_ge(m_sum.sem, E0 // 2)
            for q in range(NSEQ):
                for c in range(DC):
                    ins = e.transpose(ps[0:S, q // 2, (q % 2) * D + c * P:(q % 2) * D + (c + 1) * P],
                                      hT_all[:, c, q * S:(q + 1) * S], ident)
                if q % 2:
                    ins.then_inc(m_back.sem, 1)
            def ternT_pe(g, h, j):
                yield
                W(e, "E_xq", g, j + 1, h)
                pb = ps[:, 4 * h, :].bitcast(BF16)
                for c in range(DC):
                    for i, b in enumerate(seqs(h)):
                        ins = e.transpose(pb[:, c * HT + i * S:c * HT + (i + 1) * S], xq[:, b, c * P:(c + 1) * P],
                                          identb[0:S, 0:S])
                inc(ins, "E_xqTp")
                yield
                W(e, "E_xqT", g, j + 1, h)

            def before_e(g, h):
                b0 = 4 * h
                for j in range(3):
                    yield from ternT_pe(g, h, j)
                    if j < 2:
                        projT_pe(e, h, wtern[:, j], xqT, b0 + 1, "E_qTp" if j == 0 else "E_kTp")
                        W(e, "E_bc", g, j + 1, h)
                        for i, b in enumerate(seqs(h)):
                            ins = e.matmul(ps[:, b0 + 2, i * S:(i + 1) * S], cs("ones", S), y[:, b, 0:S],
                                           start=True, stop=True)
                        inc(ins, "E_bcp")
                        if j == 0:
                            yield
                            W(e, "E_qT", g, 1, h)
                    else:
                        proj_pe(e, h, wtern[:, j], xqT, b0 + 3, "E_vp")

            def after_e(g, h):
                b0 = 4 * h
                yield from toT_pe(e, "E_", g, h, "rTp", b0, xn, ("E_rx", 1))
                yield
                W(e, "E_yT", g, 1, h)
                for i, b in enumerate(seqs(h)):
                    for c in range(DC):
                        ins = e.transpose(ps[0:S, b0 + 1, i * D + c * P:i * D + (c + 1) * P],
                                          qT[:, c, b * S:(b + 1) * S], ident)
                inc(ins, "E_ytp")
                yield from ternT_pe(g, h, 3)
                proj_pe(e, h, wtern[:, 3], xqT, b0 + 1, "E_out")
                yield from toT_pe(e, "F_", g, h, "hTp", b0, xn, ("F_xn", 1))
                yield
                W(e, "F_hT", g, 1, h)
                projT_pe(e, h, wv("F_q", DC), hT, b0 + 1, "F_qTp")

            def after_f(g, h):
                b0 = 4 * h
                yield from toT_pe(e, "F_", g, h, "rTp", b0, xn, ("F_rx", 1))
                yield
                W(e, "F_yT", g, 1, h)
                proj_pe(e, h, wv("F_o", DC), qT, b0 + 1, "F_out")
                yield from toT_pe(e, "G_", g, h, "hTp", b0, xn, ("G_xn", 1))
                yield from gate_pe(e, "G_", g, h, wv("G_gate", DC))

            with e.Fori(0, NG) as g:
                in_turn(before_e(g, 0), before_e(g, 1))
                W(e, "E_kT", g, 1, 1)
                W(e, "E_v", g, 1, 1)
                self_pe(e, "E_", g)
                in_turn(after_e(g, 0), after_e(g, 1))
                e.wait_ge(ld["ctxT3"].sem, g * 16 + 16)

                def kv(b, i):
                    n = 5 * b + i
                    if n >= 1:
                        W(e, "F_kv", g, n)
                    if i < DC:
                        ins = e.matmul(bank(7, n=LC), wv("F_k")[:, i * P:(i + 1) * P], ctxT[:, b, 0:LC],
                                       start=True, stop=True)
                    else:
                        k = i - DC
                        ins = e.matmul(bank(7, KW, D), ctxT[:, b, k * KW:(k + 1) * KW], wv("F_v"),
                                       start=True, stop=True)
                    inc(ins, "F_kvp")

                def f_scores(b, v):
                    n, c = 8 * b + v, v // 4
                    W(e, "F_bd", g, 2 * b + c + 1)
                    if v == 0:
                        W(e, "F_kv", g, 5 * b + 2)
                    if n >= 2:
                        W(e, "F_e", g, n - 1)
                    for i in range(2):
                        ins = e.matmul(bank(2 * (n % 2) + i, S, LC), headbd[:, c, 2 * (v % 4) + i, :],
                                       kT[:, b % 2, c * LC:(c + 1) * LC], start=True, stop=True)
                    inc(ins, "F_s")

                def f_turn(b, v):
                    n = 8 * b + v
                    W(e, "F_e", g, n + 1)
                    if n >= 1:
                        W(e, "F_pT", g, n)
                    for i in range(2):
                        for k in range(KC):
                            ins = e.transpose(ps[0:KW, 4 + i, k * S:(k + 1) * S],
                                              f_e[:, n % 2, i, k * KW:(k + 1) * KW], identS)
                    inc(ins, "F_pTp")

                def f_values(b, v):
                    n, c = 8 * b + v, v // 4
                    W(e, "F_pT", g, n + 1)
                    if v == 0:
                        W(e, "F_kv", g, 5 * b + 5)
                        if b >= 1:
                            W(e, "F_o", g, b)
                    for i in range(2):
                        h = 2 * (v % 4) + i
                        for k in range(KC):
                            ins = e.matmul(ps[:, 6, (2 * (b % 2) + c) * S:(2 * (b % 2) + c + 1) * S],
                                           window(3 * (b % 2) + k, KW, c, h), f_eT[:, n % 2, i, k * S:(k + 1) * S],
                                           start=(h == 0 and k == 0), stop=(h == HC - 1 and k == KC - 1))
                    inc(ins, "F_av")

                W(e, "F_qT", g, 1, 1)
                for i in range(5):
                    kv(0, i)
                units = [(b, v) for b in range(NB) for v in range(8)]
                for n in range(len(units) + 2):
                    if n < len(units):
                        b, v = units[n]
                        f_scores(b, v)
                    if 1 <= n <= len(units):
                        f_turn(*units[n - 1])
                    if n >= 2:
                        f_values(*units[n - 2])
                    if n < len(units) and b + 1 < NB and 3 <= v < 8:
                        kv(b + 1, v - 3)
                in_turn(after_f(g, 0), after_f(g, 1))
                e.wait_ge(ld["e1"].sem, 16)
                W(e, "G_gm", g, 1, 1)

                def up1(j):
                    if j >= 2:
                        W(e, "G_hid", g, j - 1)
                    for i in range(2):
                        w = experts[:, j * 768 + i * 256:j * 768 + (i + 1) * 256].rearrange("p (c n) -> p c n", c=DC)
                        for c in range(DC):
                            ins = e.matmul(bank(2 * i + j % 2, n=NT), w[:, c, :], hT[:, c, :],
                                           start=(c == 0), stop=(c == DC - 1))
                    inc(ins, "G_h")

                def down1(j):
                    W(e, "G_hid", g, j + 1)
                    if j >= 2:
                        W(e, "G_acc", g, j - 1)
                    for b in range(NB):
                        ins = e.matmul(ps[0:S, 4 + 2 * (j % 2) + b // 2, (b % 2) * D:(b % 2 + 1) * D],
                                       g_hid[:, j % 2, b * S:(b + 1) * S], experts[:, j * 768 + 512:(j + 1) * 768],
                                       start=True, stop=True)
                    inc(ins, "G_o")

                for j in range(E1 + 1):
                    if j < E1:
                        up1(j)
                    if j >= 1:
                        down1(j - 1)


        @block.scalar
        def _(e):
            e.wait_ge(ld["cst"].sem, 16)
            e.activation(identb[:], ident, ACT.Copy)
            for b in range(NB):
                ins = e.activation(causalb[:, b, :], cs("causal", S), ACT.Copy)
            ins.then_inc(prep_b.sem, 1)
            e.wait_ge(prep_t.sem, 1)
            e.activation(tempc[:, 1:2], tempc[:, 0:1], ACT.Exp, scale=-1.0)
            e.drain()
            e.activation(tempc[:, 1:2], tempc[:, 1:2], ACT.Ln, bias=1.0).then_inc(prep_e.sem, 1)

            def before_c(g, h):
                b0, t, o = 4 * h, tok(h), own(h)
                yield from toT_act(e, "A_", g, h, "hTp", "hT", b0, hT)
                yield
                W(e, "A_in", g, 1, h)
                inc(e.activation(a_q[:, o], a_in[:, o, SH], ACT.Tanh), "A_q")
                yield
                W(e, "A_shTp", g, 1, h)
                inc(e.activation(a_shT[:, t], bank(b0, SH, HT), ACT.Copy), "A_shT")
                yield
                W(e, "A_ang", g, 1, h)
                inc(e.activation(a_trig[:, t], a_ang[:, t], ACT.Sin), "A_trig")
                yield
                W(e, "A_phiTp", g, 1, h)
                inc(e.activation(a_phiT[:, t], bank(b0, SH, HT), ACT.Copy), "A_phiT")
                yield
                W(e, "A_nm", g, 1, h)
                for b in seqs(h):
                    ins = e.activation(a_lg[:, b, :], a_lg[:, b, :], ACT.Exp, bias=a_nm[:, b:b + 1],
                                       accum_out=a_sum[:, b:b + 1])
                inc(ins, "A_e")
                yield
                W(e, "A_pTp", g, 1, h)
                inc(e.activation(probsT[0:S, 0, t], bank(b0, S, HT), ACT.Copy), "A_pT")
                yield
                W(e, "A_oTp", g, 1, h)
                inc(e.activation(qT[:, :, t], part(b0 + 1), ACT.Copy), "A_oT")
                yield from toT_act(e, "B_", g, h, "hTp", "hT", b0, hT)
                yield
                W(e, "B_qTp", g, 1, h)
                for m in range(DC):
                    ins = e.activation(qT[:, m, t], part(b0 + 1)[:, m, :], ACT.Identity, bias=col("B_bq", m))
                inc(ins, "B_qT")
                yield
                W(e, "B_kqTp", g, 1, h)
                inc(e.activation(hT[:, 0, t], bank(b0 + 2, n=HT), ACT.Copy), "B_kqT")
                yield
                W(e, "B_nm", g, 1, h)
                for i, b in enumerate(seqs(h)):
                    ins = e.activation(b_e[:, b, 0:LC], bank(b0 + 1 + i, S, LC), ACT.Exp, bias=b_nm[:, b:b + 1],
                                       accum_out=b_sum[:, b:b + 1])
                inc(ins, "B_e")
                yield
                W(e, "B_pTp", g, 1, h)
                for i, b in enumerate(seqs(h)):
                    ins = e.activation(b_eT[:, b, :], bank(b0 + 3 * i, KW, KC * S), ACT.Copy)
                inc(ins, "B_pT")
                yield
                W(e, "B_oTp", g, 1, h)
                inc(e.activation(hT[:, 1, t], bank(b0 + 1, n=HT), ACT.Copy), "B_oT")
                yield from toT_act(e, "C_", g, h, "hTp", "hT", b0, hT, "C_s", "C_b")
                yield
                W(e, "C_kTp", g, 1, h)
                inc(e.activation(keysT[:, :, t], part(b0 + 2), ACT.Copy), "C_kT")
                yield
                W(e, "C_qTp", g, 1, h)
                inc(e.activation(qT[:, :, t], part(b0 + 3), ACT.Copy, scale=HD ** -0.5), "C_qT")

            def after_c(g, h):
                yield from toT_act(e, "C_", g, h, "rTp", "rT", 4 * h, hT)
                yield from toT_act(e, "D_", g, h, "hTp", "hT", 4 * h, hT, "D_s", "D_b")
                yield from gate_act(e, "D_", g, h)

            with e.Fori(0, NG) as g:
                in_turn(before_c(g, 0), before_c(g, 1))
                self_act(e, "C_", g)
                in_turn(after_c(g, 0), after_c(g, 1))
            def split_hi(slot, k):
                e.activation(w_hi[:, slot, k * WP:(k + 1) * WP], experts[:, slot * W0 + k * WP:slot * W0 + (k + 1) * WP],
                             ACT.Copy).then_inc(m_whi.sem, 1)

            def experts_act(ep, last=False):
                for n in range(2 * NG * MC0):
                    slot, k = divmod(n, NG * MC0)
                    e.wait_ge(m_h.sem, m_h.at(ep, n + 1))
                    e.wait_ge(m_hid.sem, m_hid.free(ep, n + 1))
                    e.activation(silu[:, n % 2, :], bank(n % 2, n=NT), ACT.Silu).then_inc(m_act.sem, 1)
                    if k == MC0:
                        e.wait_ge(m_gp.sem, m_gp.at(ep, slot + 1))
                        e.activation(gate_b[:, slot], ps[:, 4:8, 0:NT], ACT.Copy).then_inc(m_gb.sem, 1)
                    k -= NG * MC0 - NPIECE
                    if k >= 0 and not (last and slot == 1):
                        if k == 0:
                            e.wait_ge(ld_e0[1 - slot].sem, (ep + slot) * 16 + 16)
                        split_hi(1 - slot, k)

            W(e, "D_g", NG - 1, 1, 1)
            e.wait_ge(ld_e0[0].sem, 16)
            for k in range(NPIECE):
                split_hi(0, k)
            with e.Fori(0, E0 // 2 - 1) as ep:
                experts_act(ep)
            experts_act(E0 // 2 - 1, True)
            def tern_act(g, h, j):
                yield
                W(e, "E_xqTp", g, j + 1, h)
                inc(e.activation(xqT[:, :, tok(h)],
                                 ps[:, 4 * h, :].bitcast(BF16)[:, 0:DC * HT].rearrange("p (c n) -> p c n", c=DC),
                                 ACT.Copy), "E_xqT")

            def before_e(g, h):
                for j in range(3):
                    yield from tern_act(g, h, j)
                    if j < 2:
                        yield
                        W(e, "E_bcp", g, j + 1, h)
                        inc(e.activation(hT[:, j, tok(h)], bank(4 * h + 2, n=HT), ACT.Copy,
                                         scale=wscale[:, j:j + 1]), "E_sc")

            def after_e(g, h):
                yield from toT_act(e, "E_", g, h, "rTp", "rT", 4 * h, hT)
                yield from tern_act(g, h, 3)
                yield from toT_act(e, "F_", g, h, "hTp", "hT", 4 * h, hT)
                yield
                W(e, "F_qTp", g, 1, h)
                for m in range(DC):
                    ins = e.activation(qT[:, m, tok(h)], part(4 * h + 1)[:, m, :], ACT.Identity, scale=HD ** -0.5,
                                       bias=bq4[:, m:m + 1])
                inc(ins, "F_qT")

            def after_f(g, h):
                yield from toT_act(e, "F_", g, h, "rTp", "rT", 4 * h, keysT)
                yield from toT_act(e, "G_", g, h, "hTp", "hT", 4 * h, hT)
                yield from gate_act(e, "G_", g, h)

            with e.Fori(0, NG) as g:
                in_turn(before_e(g, 0), before_e(g, 1))
                self_act(e, "E_", g)
                in_turn(after_e(g, 0), after_e(g, 1))

                def key_evac(b, i):
                    W(e, "F_kvp", g, 5 * b + i + 1)
                    inc(e.activation(kT[:, b % 2, i * LC:(i + 1) * LC], bank(7, n=LC), ACT.Identity,
                                     bias=col("F_bk", i)), "F_kv")

                for i in range(DC):
                    key_evac(0, i)
                for n in range(8 * NB):
                    b, v = divmod(n, 8)
                    W(e, "F_nm", g, n + 1)
                    if n >= 2:
                        W(e, "F_pTp", g, n - 1)
                    for i in range(2):
                        h = 2 * v + i
                        ins = e.activation(f_e[:, n % 2, i, 0:LC], bank(2 * (n % 2) + i, S, LC), ACT.Exp,
                                           bias=h_nm[:, n % 2, i:i + 1], accum_out=h_sum[:, b, h:h + 1])
                    inc(ins, "F_e")
                    if v == 1 and b >= 1:
                        W(e, "F_av", g, 8 * b)
                        inc(e.activation(hT[:, :, (b - 1) * S:b * S],
                                         ps[:, 6, 2 * ((b - 1) % 2) * S:2 * ((b - 1) % 2) * S + 2 * S].rearrange(
                                             "p (c n) -> p c n", c=DC), ACT.Copy), "F_o")
                    if b + 1 < NB and v in (3, 4):
                        key_evac(b + 1, v - 3)
                W(e, "F_av", g, 8 * NB)
                inc(e.activation(hT[:, :, (NB - 1) * S:NB * S],
                                 ps[:, 6, 2 * S:4 * S].rearrange("p (c n) -> p c n", c=DC), ACT.Copy), "F_o")
                in_turn(after_f(g, 0), after_f(g, 1))
                for j in range(E1):
                    W(e, "G_h", g, j + 1)
                    if j >= 2:
                        W(e, "G_hid", g, j - 1)
                    inc(e.activation(g_act[:, j % 2, :], bank(j % 2, n=NT), ACT.Gelu), "G_act")

        @block.gpsimd
        def _(e):
            e.memset(spread[:, 0:2, :], 0.0)
            e.wait_ge(ld["cst"].sem, 16)
            e.wait_ge(ld["rows"].sem, 16)
            e.drain()
            bcast = lambda name: row(name).unsqueeze(1).broadcast_to([S, HB, D])

            def add_bias(dst, src, name, h):
                return e.tensor_tensor(dst[:, own(h), :], src[:, own(h), :], bcast(name), ALU.add)

            def before_c(g, h):
                yield from norm_pool(e, "A_", g, h)
                inc(add_bias(x, xin, "A_out", h), "A_xb")
                yield
                W(e, "A_ss", g, 1, h)
                inc(e.tensor_tensor(a_rn[:, own(h)], a_ss[:, own(h)], cs("mhalf", S)[:, 0:HB], ALU.pow), "A_rn")
                yield from norm_pool(e, "B_", g, h)
                yield
                W(e, "B_xn", g, 1, h)
                inc(add_bias(x, x, "B_v", h), "B_xb")
                yield from norm_pool(e, "C_", g, h, eps2=EPS)
                yield
                W(e, "C_xn", g, 1, h)
                inc(add_bias(y, y, "C_o", h), "C_xb")

            def after_c(g, h):
                yield from spread_recips_pool(e, "C_", g, h)
                yield from norm_pool(e, "D_", g, h)

            with e.Fori(0, NG) as g:
                in_turn(before_c(g, 0), before_c(g, 1))
                self_pool(e, "C_", g, c_v)
                in_turn(after_c(g, 0), after_c(g, 1))
            def split_lo(ep, slot, k, n):
                raw = experts[:, slot * W0 + k * WP:slot * W0 + (k + 1) * WP]
                e.wait_ge(m_whi.sem, m_whi.at(ep, n))
                e.tensor_tensor(w_lo[:, slot, k * WP:(k + 1) * WP], raw, w_hi[:, slot, k * WP:(k + 1) * WP],
                                ALU.subtract).then_inc(m_wlo.sem, 1)

            def experts_pool(ep, last=False):
                for n in range(2 * NG * MC0):
                    s, m = divmod(n, MC0)
                    slot, k = divmod(n, NG * MC0)
                    e.wait_ge(m_hid.sem, m_hid.at(ep, n + 1))
                    e.tensor_tensor(hid_lo[:, s % 2, m, :], hid[:, n % 2, :], hid_hi[:, s % 2, m, :],
                                    ALU.subtract).then_inc(m_lo.sem, 1)
                    k -= NG * MC0 - NPIECE
                    if k >= 0 and not (last and slot == 1):
                        split_lo(ep, 1 - slot, k, NPIECE * (slot + 1) + k + 1)

            for k in range(NPIECE):
                split_lo(0, 0, k, k + 1)
            with e.Fori(0, E0 // 2 - 1) as ep:
                experts_pool(ep)
            experts_pool(E0 // 2 - 1, True)
            e.wait_ge(m_acc.sem, m_acc.at(E0 // 2 - 1, 2 * NG))
            for u in range(NVU):
                e.memset(spread[:, u, :], 0.0)
            e.drain()

            def before_e(g, h):
                yield from norm_pool(e, "E_", g, h, eps2=EPS_RMS, fold=True)

            def after_e(g, h):
                yield from spread_recips_pool(e, "E_", g, h)
                yield
                W(e, "E_ssr", g, 1, h)
                inc(e.tensor_tensor(r2[:, own(h)], t1[:, own(h)], cs("mhalf", S)[:, 0:HB], ALU.pow), "E_sso")
                yield from norm_pool(e, "F_", g, h)
                yield
                W(e, "F_xn", g, 1, h)
                inc(add_bias(x, x, "F_o", h), "F_xb")

            def after_f(g, h):
                yield from spread_recips_pool(e, "F_", g, h)
                yield from norm_pool(e, "G_", g, h)

            with e.Fori(0, NG) as g:
                in_turn(before_e(g, 0), before_e(g, 1))
                self_pool(e, "E_", g, y)
                in_turn(after_e(g, 0), after_e(g, 1))
                e.memset(f_e[:, :, :, LC:LP], 0.0)
                e.drain()
                W(e, "F_qT", g, 1, 1)
                for b in range(NB):
                    for c in range(DC):
                        if b >= 1:
                            W(e, "F_s", g, 8 * (b - 1) + 4 * (c + 1))
                        inc(e.tensor_tensor(headbd[:, c],
                                            qT[:, c, b * S:(b + 1) * S].unsqueeze(1).broadcast_to([P, HC, S]),
                                            cs("head").unsqueeze(2).broadcast_to([P, HC, S]), ALU.mult), "F_bd")
                in_turn(after_f(g, 0), after_f(g, 1))

        @block.vector
        def _(e):
            e.sem_inc(m_hid.sem, m_hid.base)
            e.sem_inc(m_acc.sem, m_acc.base)
            e.sem_inc(m_out.sem, m_out.base)
            e.wait_ge(ld["wq"].sem, 16)
            e.wait_ge(ld["wt"].sem, 16)
            e.wait_ge(ld["cst"].sem, 16)
            e.wait_ge(ld["rows"].sem, 16)
            wq4 = experts[:, 0:4 * DC * D].rearrange("p (j n) -> p j n", j=4)
            e.tensor_reduce(wsum, wq4, AX, ALU.add, apply_absolute_value=True).then_inc(prep_abs.sem, 1)
            lt = col("log_temp")
            e.tensor_scalar(tempc[:, 0:1], lt, -1.0, None, ALU.mult)
            e.drain()
            e.tensor_tensor(tempc[:, 0:1], tempc[:, 0:1], lt, ALU.max).then_inc(prep_t.sem, 1)
            e.tensor_scalar(bq4, wt[:, WOFF["cols"][0] + COLS["F_bq"]:WOFF["cols"][0] + COLS["F_bq"] + 2],
                            HD ** -0.5, None, ALU.mult)
            e.memset(b_e[:, :, LC:LP], 0.0)
            e.memset(a_sqw[:, :, SH:P], 0.0)
            e.memset(a_phiw[:, :, SH:P], 0.0)
            e.wait_ge(prep_sum.sem, 1)
            e.tensor_scalar(wscale, bank(0, n=4), 1.0 / (D * D), 1e-5, ALU.mult, ALU.max)
            e.drain()
            e.reciprocal(wrecip, wscale)
            e.drain()
            for j in range(4):
                e.tensor_scalar(wq4[:, j, :], wq4[:, j, :], wrecip[:, j:j + 1], MAGIC, ALU.mult, ALU.add)
            e.tensor_scalar(wscale[:, 0:1], wscale[:, 0:1], HD ** -0.5, None, ALU.mult)
            e.drain()
            e.tensor_scalar(wq4, wq4, MAGIC, 1.0, ALU.subtract, ALU.min)
            e.drain()
            e.tensor_scalar(wtern[:].rearrange("p j c n -> p j (c n)"), wq4, -1.0, None, ALU.max
                            ).then_inc(tern_go.sem, 1)
            e.wait_ge(prep_e.sem, 1)
            e.tensor_scalar(tempc[:, 2:3], lt, 0.0, None, ALU.max)
            e.drain()
            e.tensor_tensor(tempc[:, 2:3], tempc[:, 2:3], tempc[:, 1:2], ALU.add)
            e.drain()
            e.tensor_scalar(tempc[:, 2:3], tempc[:, 2:3], 0.1, None, ALU.add)
            e.drain()
            e.reciprocal(tempc[:, 3:4], tempc[:, 2:3])
            e.drain()
            e.tensor_scalar(decay, cs("decay", S), tempc[0:S, 3:4], None, ALU.mult)

            def add_out(dst, b0, h):
                e.tensor_tensor(dst[:, own(h), :], tokens(b0), dst[:, own(h), :], ALU.add)
                e.drain()

            def before_c(g, h):
                b0, t, o = 4 * h, tok(h), own(h)
                if h == 0:
                    e.wait_ge(ld["x"].sem, g * 16 + 16)
                inc((yield from norm_dve(e, "A_", g, h, xin, xn)), "A_xn")
                yield
                W(e, "A_in_p", g, 1, h)
                inc(e.tensor_tensor(a_in[:, o, :], ps[0:S, b0 + 1:b0 + 3, 0:321],
                                    row("A_in").unsqueeze(1).broadcast_to([S, HB, 321]), ALU.add), "A_in")
                e.drain()
                e.tensor_tensor(a_sq[:, o, :], a_in[:, o, 0:SH], a_in[:, o, 0:SH], ALU.mult)
                e.drain()
                e.tensor_reduce(a_ss[:, o], a_sq[:, o, :], AX, ALU.add)
                e.drain()
                inc(e.tensor_scalar(a_ss[:, o], a_ss[:, o], 1e-24, None, ALU.max), "A_ss")
                yield
                W(e, "A_rn", g, 1, h)
                inc(e.tensor_tensor(a_sq[:, o, :], a_in[:, o, 0:SH],
                                    a_rn[:, o].unsqueeze(2).broadcast_to([S, HB, SH]), ALU.mult), "A_shn")
                yield
                W(e, "A_angp", g, 1, h)
                ang, turns = a_ang[:, t], a_k[:, t]
                e.tensor_scalar(ang, bank(b0 + 3, SH, HT), col("rb", 0, SH), col("half_pi", 0, SH), ALU.add, ALU.add)
                e.drain()
                e.tensor_scalar(turns, ang, 1.0 / (2 * math.pi), MAGIC, ALU.mult, ALU.add)
                e.drain()
                e.tensor_scalar(turns, turns, MAGIC, -1.0, ALU.subtract, ALU.mult)
                e.drain()
                e.scalar_tensor_tensor(ang, turns, TWO_PI_HI, ang, ALU.mult, ALU.add)
                e.drain()
                e.scalar_tensor_tensor(ang, turns, TWO_PI_LO, ang, ALU.mult, ALU.add)
                e.drain()
                inc(e.tensor_scalar(ang, ang, 3.1415925, -3.1415925, ALU.min, ALU.max), "A_ang")
                yield
                W(e, "A_comb", g, 1, h)
                W(e, "A_q", g, 1, h)
                phi = a_phi[:, o, :]
                qb = a_q[:, o].unsqueeze(2).broadcast_to([S, HB, SH])
                pm = lambda m: ps[0:S, b0 + 1:b0 + 3, m * SH:(m + 1) * SH]
                e.tensor_scalar(phi, pm(ORD - 1), MAGS[ORD - 1] / MAGS[ORD - 2], None, ALU.mult)
                e.drain()
                for m in range(ORD - 2, -1, -1):
                    if m == ORD - 2:
                        e.tensor_tensor(phi, phi, qb, ALU.mult)
                    else:
                        e.scalar_tensor_tensor(phi, phi, MAGS[m + 1] / MAGS[m], qb, ALU.mult, ALU.mult)
                    e.drain()
                    ins = e.tensor_tensor(phi, phi, pm(m), ALU.add)
                    if m:
                        e.drain()
                inc(ins, "A_phi")
                yield
                W(e, "A_lg", g, 1, h)
                lg = a_lg[:, o, :]
                e.tensor_tensor(lg, ps[0:S, b0 + 3, 0:HT].rearrange("p (b n) -> p b n", b=HB),
                                decay.unsqueeze(1).broadcast_to([S, HB, S]), ALU.mult)
                e.drain()
                e.tensor_tensor(lg, lg, cs("causal", S).unsqueeze(1).broadcast_to([S, HB, S]), ALU.add)
                e.drain()
                inc(e.tensor_reduce(a_nm[:, o], lg, AX, ALU.max, negate=True), "A_nm")
                yield
                W(e, "A_e", g, 1, h)
                e.reciprocal(a_rs[:, o], a_sum[:, o])
                e.drain()
                inc(e.tensor_tensor(lg, lg, a_rs[:, o].unsqueeze(2).broadcast_to([S, HB, S]), ALU.mult), "A_p")
                yield
                W(e, "A_out", g, 1, h)
                W(e, "A_xb", g, 1, h)
                add_out(x, b0 + 2, h)
                inc((yield from norm_dve(e, "B_", g, h, x, xn)), "B_xn")
                yield
                W(e, "B_qbkp", g, 1, h)
                e.tensor_scalar(b_qbk[:, o], bank(b0 + 3, S, HB), 1.0, None, ALU.mult)
                yield
                W(e, "B_s", g, 1, h)
                e.tensor_reduce(b_mx[:, o], ps[0:S, b0 + 1:b0 + 3, 0:LC], AX, ALU.max)
                e.drain()
                e.tensor_tensor(b_mx[:, o], b_mx[:, o], b_qbk[:, o], ALU.add)
                e.drain()
                inc(e.tensor_tensor(b_nm[:, o], b_qbk[:, o], b_mx[:, o], ALU.subtract), "B_nm")
                yield
                W(e, "B_e", g, 1, h)
                e.reciprocal(b_rs[:, o], b_sum[:, o])
                e.drain()
                for b in seqs(h):
                    ins = e.tensor_scalar(b_e[:, b, 0:LC], b_e[:, b, 0:LC], b_rs[:, b:b + 1], None, ALU.mult)
                inc(ins, "B_p")
                yield
                W(e, "B_out", g, 1, h)
                W(e, "B_xb", g, 1, h)
                add_out(x, b0 + 2, h)
                yield from norm_dve(e, "C_", g, h, x, y)
                e.drain()
                for b in seqs(h):
                    ins = e.tensor_scalar(xn[:, b, :], y[:, b, :], r2[:, b:b + 1], None, ALU.mult)
                inc(ins, "C_xn")
                yield
                W(e, "C_vp", g, 1, h)
                inc(e.tensor_scalar(c_v[:, o, :], tokens(b0 + 1), 1.0, None, ALU.mult), "C_v")

            def after_c(g, h):
                b0, t, o = 4 * h, tok(h), own(h)
                yield
                W(e, "C_rT", g, 1, h)
                inc(e.tensor_tensor(qT[:, :, t], ps[:, 6:8, t], hT[:, :, t], ALU.mult), "C_yT")
                yield
                W(e, "C_out", g, 1, h)
                W(e, "C_xb", g, 1, h)
                add_out(y, b0 + 1, h)
                inc((yield from norm_dve(e, "D_", g, h, y, xn)), "D_xn")
                e.tensor_tensor(xall[:, bass.ds(g * NB + HB * h, HB), :], x[:, o, :], y[:, o, :], ALU.add)
                e.drain()
                yield
                W(e, "D_hT", g, 1, h)
                for c in range(DC):
                    e.tensor_scalar(hT_all[:, c, bass.ds(g * NT + HT * h, HT)], hT[:, c, t], 1.0, None, ALU.mult)
                yield from gate_dve(e, "D_", g, h, False, gates_all[:, bass.ds(g * NB + HB * h, HB), :])

            with e.Fori(0, NG) as g:
                in_turn(before_c(g, 0), before_c(g, 1))
                self_dve(e, "C_", g)
                in_turn(after_c(g, 0), after_c(g, 1))
            for gi in range(NG):
                t = slice(gi * NT, (gi + 1) * NT)
                e.tensor_scalar(x_hi[:, :, t], hT_all[:, :, t], 1.0, None, ALU.mult)
                e.drain()
                e.tensor_tensor(x_lo[:, :, t], hT_all[:, :, t], x_hi[:, :, t], ALU.subtract).then_inc(m_x.sem, 1)
            e.drain()
            e.memset(hT_all[:], 0.0)

            def acc(ep, s):
                slot, gi = divmod(s, NG)
                total = hT_all[:, :, gi * NT:(gi + 1) * NT]
                e.wait_ge(m_out.sem, m_out.at(ep, s + 1))
                e.tensor_tensor(gated[:], ps[:, 4 + 2 * (s % 2):6 + 2 * (s % 2), 0:NT],
                                gate_b[:, slot, gi, :].unsqueeze(1).broadcast_to([P, DC, NT]),
                                ALU.mult).then_inc(m_acc.sem, 1)
                e.drain()
                ins = e.tensor_tensor(total, total, gated[:], ALU.add)
                if s == 2 * NG - 1:
                    ins.then_inc(m_sum.sem, 1)

            def experts_dve(ep):
                for slot in range(2):
                    ins = e.tensor_scalar(gpair[:, slot, :], gates_all[:, :, bass.ds(2 * ep + slot, 1)].rearrange(
                        "p q o -> p (q o)"), 1.0, None, ALU.mult)
                ins.then_inc(m_gr.sem, 1)
                for s in range(2 * NG):
                    for m in range(MC0):
                        n = s * MC0 + m
                        e.wait_ge(m_act.sem, m_act.at(ep, n + 1))
                        if m == 0:
                            e.wait_ge(m_out.sem, m_out.at(ep, s - 1))
                        if n >= 2:
                            e.wait_ge(m_lo.sem, m_lo.at(ep, n - 1))
                        e.tensor_tensor(hid[:, n % 2, :], bank(2 + n % 2, n=NT), silu[:, n % 2, :], ALU.mult)
                        e.tensor_tensor(hid_hi[:, s % 2, m, :], bank(2 + n % 2, n=NT), silu[:, n % 2, :],
                                        ALU.mult).then_inc(m_hid.sem, 1)
                        if m == 1 and s >= 1:
                            acc(ep, s - 1)
                acc(ep, 2 * NG - 1)
                e.drain()

            with e.Fori(0, E0 // 2 - 1) as ep:
                experts_dve(ep)
            experts_dve(E0 // 2 - 1)
            for i in range(NSEQ // 2):
                e.wait_ge(m_back.sem, i + 1)
                e.tensor_tensor(xall[:, 2 * i:2 * i + 2, :], ps[0:S, i, :].rearrange("p (b n) -> p b n", b=2),
                                xall[:, 2 * i:2 * i + 2, :], ALU.add)
            e.drain()
            tq = xin

            def quantise(j, g, h):
                o = own(h)
                am, sc = q_am[:, o], q_sc[:, o]
                e.drain()
                e.tensor_reduce(am, tq[:, o, :], AX, ALU.max, apply_absolute_value=True)
                e.drain()
                e.tensor_scalar(am, am, 1e-5, None, ALU.max)
                e.drain()
                e.reciprocal(sc, am)
                e.tensor_scalar(q_isc[:, min(j, 2), o], am, 1.0 / 127.0, None, ALU.mult)
                e.drain()
                e.tensor_scalar(sc, sc, 127.0, None, ALU.mult)
                e.drain()
                for b in seqs(h):
                    e.tensor_scalar(tq[:, b, :], tq[:, b, :], q_sc[:, b:b + 1], MAGIC, ALU.mult, ALU.add)
                e.drain()
                if j >= 1:
                    W(e, "E_xqTp", g, j, h)
                inc(e.tensor_scalar(xq[:, o, :], tq[:, o, :], MAGIC, 127.0, ALU.subtract, ALU.min), "E_xq")

            def before_e(g, h):
                b0, t, o = 4 * h, tok(h), own(h)
                if h == 0:
                    e.wait_ge(x_free.sem, g + 1)
                e.tensor_scalar(x[:, o, :], xall[:, bass.ds(g * NB + HB * h, HB), :], 1.0, None, ALU.mult)
                e.drain()
                yield from norm_dve(e, "E_", g, h, x, xn)
                e.drain()
                for j, gain in enumerate(("gq", "gk", "gv")):
                    e.tensor_tensor(tq[:, o, :], xn[:, o, :], row(gain).unsqueeze(1).broadcast_to([S, HB, D]), ALU.mult)
                    quantise(j, g, h)
                    if j < 2:
                        if j == 1:
                            W(e, "E_bcp", g, 1, h)
                        for b in seqs(h):
                            ins = e.tensor_scalar(y[:, b, 0:S], identS, q_isc[:, j, b:b + 1], None, ALU.mult)
                        inc(ins, "E_bc")
                        yield
                        W(e, "E_sc", g, j + 1, h)
                        W(e, "E_qTp" if j == 0 else "E_kTp", g, 1, h)
                        inc(e.tensor_tensor((qT if j == 0 else keysT)[:, :, t], part(b0 + 1),
                                            hT[:, j, t].unsqueeze(1).broadcast_to([P, DC, HT]), ALU.mult),
                            "E_qT" if j == 0 else "E_kT")
                yield
                W(e, "E_vp", g, 1, h)
                for i, b in enumerate(seqs(h)):
                    ins = e.tensor_scalar(y[:, b, :], ps[0:S, b0 + 3, i * D:(i + 1) * D],
                                          q_isc[:, 2, b:b + 1], wscale[0:S, 2:3], ALU.mult, ALU.mult)
                inc(ins, "E_v")

            def after_e(g, h):
                b0, t, o = 4 * h, tok(h), own(h)
                yield
                W(e, "E_rT", g, 1, h)
                inc(e.tensor_tensor(qT[:, :, t], ps[:, 6:8, t], hT[:, :, t], ALU.mult), "E_yT")
                yield
                W(e, "E_ytp", g, 1, h)
                e.tensor_scalar(y[:, o, :], tokens(b0 + 1), 1.0, None, ALU.mult)
                e.drain()
                e.tensor_tensor(tq[:, o, :], y[:, o, :], y[:, o, :], ALU.mult)
                e.drain()
                e.tensor_reduce(q_am[:, o], tq[:, o, :], AX, ALU.add)
                e.drain()
                inc(e.tensor_scalar(t1[:, o], q_am[:, o], 1.0 / D, EPS_RMS, ALU.mult, ALU.add), "E_ssr")
                yield
                W(e, "E_sso", g, 1, h)
                for b in seqs(h):
                    e.scalar_tensor_tensor(tq[:, b, :], y[:, b, :], r2[:, b:b + 1], row("go"), ALU.mult, ALU.mult)
                quantise(3, g, h)
                e.tensor_scalar(q_isc[:, 2, o], q_isc[:, 2, o], wscale[0:S, 3:4], None, ALU.mult)
                e.drain()
                yield
                W(e, "E_out", g, 1, h)
                for i, b in enumerate(seqs(h)):
                    e.scalar_tensor_tensor(x[:, b, :], ps[0:S, b0 + 1, i * D:(i + 1) * D],
                                           q_isc[:, 2, b:b + 1], x[:, b, :], ALU.mult, ALU.add)
                e.drain()
                inc((yield from norm_dve(e, "F_", g, h, x, xn)), "F_xn")

            def after_f(g, h):
                b0, t, o = 4 * h, tok(h), own(h)
                yield
                W(e, "F_rT", g, 1, h)
                W(e, "F_o", g, NB)
                inc(e.tensor_tensor(qT[:, :, t], hT[:, :, t], keysT[:, :, t], ALU.mult), "F_yT")
                yield
                W(e, "F_out", g, 1, h)
                W(e, "F_xb", g, 1, h)
                add_out(x, b0 + 1, h)
                inc((yield from norm_dve(e, "G_", g, h, x, xn)), "G_xn")
                yield from gate_dve(e, "G_", g, h, True, gates_all[:, HB * h:HB * (h + 1), :])

            with e.Fori(0, NG) as g:
                in_turn(before_e(g, 0), before_e(g, 1))
                self_dve(e, "E_", g)
                in_turn(after_e(g, 0), after_e(g, 1))

                def value_evac(b, k):
                    W(e, "F_kvp", g, 5 * b + DC + k + 1)
                    inc(e.tensor_tensor(diag(3 * (b % 2) + k, KW),
                                        bank(7, KW, D).rearrange("p (c h d) -> p c h d", c=DC, h=HC),
                                        row("F_v", KW).rearrange("p (c h d) -> p c h d", c=DC, h=HC), ALU.add), "F_kv")

                for k in range(KC):
                    value_evac(0, k)
                for n in range(8 * NB + 1):
                    b, v = divmod(n, 8)
                    if n < 8 * NB:
                        W(e, "F_s", g, n + 1)
                        if n >= 2:
                            W(e, "F_e", g, n - 1)
                        inc(e.tensor_reduce(h_nm[:, n % 2, 0:2], ps[0:S, 2 * (n % 2):2 * (n % 2) + 2, 0:LC], AX,
                                            ALU.max, negate=True), "F_nm")
                    if n >= 1:
                        W(e, "F_pTp", g, n)
                        if n >= 3:
                            W(e, "F_av", g, n - 2)
                        inc(e.tensor_scalar(f_eT[:, (n - 1) % 2], ps[0:KW, 4:6, 0:KC * S], 1.0, None, ALU.mult), "F_pT")
                    if n < 8 * NB and b + 1 < NB and v >= 5:
                        value_evac(b + 1, v - 5)
                W(e, "F_e", g, 8 * NB)
                inc(e.reciprocal(h_rs, h_sum), "F_rs")
                in_turn(after_f(g, 0), after_f(g, 1))

                def acc1(j):
                    W(e, "G_o", g, j + 1)
                    b0 = 4 + 2 * (j % 2)
                    if j == E1 - 1:
                        ins = e.tensor_tensor(x[:], pair(b0), x[:], ALU.add)
                    else:
                        for b in range(NB):
                            ins = e.scalar_tensor_tensor(
                                x[:, b, :], ps[0:S, b0 + b // 2, (b % 2) * D:(b % 2 + 1) * D],
                                gates_all[:, b, j:j + 1], x[:, b, :], ALU.mult, ALU.add)
                    inc(ins, "G_acc")
                    e.drain()

                for j in range(E1 + 1):
                    if j < E1:
                        W(e, "G_act", g, j + 1)
                        if j >= 2:
                            W(e, "G_o", g, j - 1)
                        inc(e.tensor_tensor(g_hid[:, j % 2, :], bank(2 + j % 2, n=NT), g_act[:, j % 2, :],
                                            ALU.mult), "G_hid")
                    if j >= 1:
                        acc1(j - 1)


def kernel(**inputs):
    import concourse.bacc as bacc
    from concourse.bass_utils import run_bass_kernel_spmd

    a = {k: np.asarray(v) for k, v in inputs.items()}
    f32 = np.float32

    def chunks(w):
        return np.ascontiguousarray(w.reshape(-1, P, w.shape[1]).transpose(1, 0, 2)).reshape(P, -1)

    wt = np.zeros((P, NW), f32)

    def put(name, v):
        o, n = WOFF[name]
        wt[:v.shape[0], o:o + n] = v

    put("A_in", chunks(np.concatenate([a["L0_attn_W_shell"].T, a["L0_attn_W_charge"].T, a["L0_attn_W_v"].T], 1)))
    put("A_omega", np.concatenate([a["L0_attn_omega"].T] * 2 + [np.zeros((SH, 2 * RF), f32)], 1))
    put("A_comb", a["L0_attn_W_combine"].reshape(SH, ORD, 2 * RF).transpose(2, 1, 0).reshape(2 * RF, ORD * SH))
    put("A_out", chunks(a["L0_attn_W_out"].T))
    put("B_q", chunks(a["L0_xattn_Wq"]))
    put("B_kT", chunks(a["L0_xattn_Wk"].T))
    put("B_bk", chunks(a["L0_xattn_bk"][:, None]))
    put("B_v", a["L0_xattn_Wv"])
    put("C_q", chunks(a["L0_ffn_wq"]))
    put("C_k", chunks(a["L0_ffn_wk"]))
    put("C_v", chunks(a["L0_ffn_wv"]))
    put("C_o", chunks(a["L0_ffn_wo"]))
    put("D_gate", chunks(a["L0_ffn_gate_w"]))
    put("F_q", chunks(a["L1_xattn_Wq"]))
    put("F_k", a["L1_xattn_Wk"])
    put("F_v", a["L1_xattn_Wv"])
    put("F_o", chunks(a["L1_xattn_Wo"]))
    put("G_gate", chunks(a["L1_ffn_gate_w"].T))

    def putcol(name, v):
        o = WOFF["cols"][0] + COLS[name]
        wt[:v.shape[0], o:o + v.shape[1]] = v

    putcol("rb", np.concatenate([a["L0_attn_rff_bias"]] * 2)[:, None])
    putcol("half_pi", np.full((RF, 1), math.pi / 2, f32))
    for name, key in (("B_bq", "L0_xattn_bq"), ("C_s", "L0_ffn_ln1_scale"), ("C_b", "L0_ffn_ln1_shift"),
                      ("D_s", "L0_ffn_ln2_scale"), ("D_b", "L0_ffn_ln2_shift"), ("F_bq", "L1_xattn_bq"),
                      ("F_bk", "L1_xattn_bk")):
        putcol(name, a[key].reshape(DC, P).T)
    putcol("log_temp", np.broadcast_to(a["L0_attn_log_temp"].reshape(1, 1), (P, 1)))

    rv = {"A_in": np.concatenate([a["L0_attn_b_shell"], a["L0_attn_b_charge"], a["L0_attn_b_v"]]),
          "A_out": a["L0_attn_b_out"], "B_v": a["L0_xattn_bv"], "C_o": a["L0_ffn_bo"], "F_v": a["L1_xattn_bv"],
          "F_o": a["L1_xattn_bo"], "gq": a["L1_attn_gq"], "gk": a["L1_attn_gk"], "gv": a["L1_attn_gv"],
          "go": a["L1_attn_go"]}
    rows = np.ascontiguousarray(np.broadcast_to(np.concatenate([rv[n] for n, _ in RCOLS])[None], (P, NR)))

    cst = np.zeros((P, NCST), f32)

    def putc(name, v):
        o, n = COFF[name]
        cst[:v.shape[0], o:o + n] = v

    i = np.arange(S)
    putc("ident", np.eye(P, dtype=f32))
    putc("ones", np.ones((P, P), f32))
    putc("decay", (np.exp(-0.03 * np.abs(i[:, None] - i[None, :])) * PHI_SCALE2).astype(f32))
    putc("causal", np.where(i[:, None] >= i[None, :], 0.0, NEG).astype(f32))
    putc("head", (np.arange(P)[:, None] // HD == np.arange(HC)[None, :]).astype(f32))
    putc("before", np.broadcast_to((np.arange(8)[None, :] < np.arange(8)[:, None]).astype(f32).reshape(1, 64), (P, 64)))
    putc("mhalf", np.full((P, 8), -0.5, f32))
    putc("eps", np.full((P, 4), EPS, f32))

    c = a["ctx_512"].reshape(NG, NB, LC, DX)
    cpad = np.concatenate([c, np.zeros((NG, NB, LP - LC, DX), f32)], 2)
    arrays = {
        "x_d": np.ascontiguousarray(a["x"].reshape(NG, NB, S, D).transpose(0, 2, 1, 3)),
        "ctxT_d": np.ascontiguousarray(cpad.transpose(0, 3, 1, 2)),
        "ctx_d": np.ascontiguousarray(cpad.reshape(NG, NB, KC, KW, DX).transpose(0, 3, 1, 2, 4)),
        "w_d": wt, "r_d": rows, "c_d": cst,
        "wq_d": np.concatenate([chunks(a["L1_attn_" + n].T) for n in ("wq", "wk", "wv", "wo")], 1),
        "e0_d": np.stack([np.concatenate([chunks(a["L0_ffn_w1"][e]), chunks(a["L0_ffn_w2"][e]),
                                          chunks(a["L0_ffn_w3"][e])], 1) for e in range(E0)]),
        "e1_d": np.concatenate(
            [np.concatenate([chunks(a["L1_ffn_Wg"][e]), chunks(a["L1_ffn_Wu"][e]), a["L1_ffn_Wd"][e]], 1)
             for e in range(E1 - 1)]
            + [chunks(a["L1_ffn_sWg"]), chunks(a["L1_ffn_sWu"]), a["L1_ffn_sWd"]], 1),
    }
    nc = bacc.Bacc("TRN2", target_bir_lowering=False, num_devices=1)
    aps = [nc.dram_tensor(n, v.shape, F32, kind="ExternalInput").ap() for n, v in arrays.items()]
    out = nc.dram_tensor("out_0", (NG, S, NB, D), F32, kind="ExternalOutput").ap()
    decoder(nc, *aps, out)
    r = run_bass_kernel_spmd(nc, [arrays], core_ids=[0])
    return np.ascontiguousarray(r.results[0]["out_0"].reshape(NG, S, NB, D).transpose(0, 2, 1, 3)).reshape(NSEQ, S, D)
```

```python
import math
from contextlib import ExitStack

import numpy as np

import concourse.bass as bass
from concourse import mybir

ACT = mybir.ActivationFunctionType
ALU = mybir.AluOpType
F32 = mybir.dt.float32
F32R = mybir.dt.float32r
BF16 = mybir.dt.bfloat16
AX = mybir.AxisListType.X

NSEQ, S, D = 16, 100, 256
NB = 4
NG = NSEQ // NB
NT = NB * S
HB, HT = NB // 2, NB * S // 2
P = 128
DC = D // P
LC, DX = 361, 128
KC = 3
KW = 121
LP = KC * KW
LE = LC + 1
NH, HD = 16, 16
HC = NH // DC
SH, RF, ORD = 64, 32, 5
E0, HID0 = 8, 512
E1, HID1 = 9, 128
MC0 = HID0 // P
W0 = DC * HID0 * 2 + MC0 * D
W1 = DC * HID1 * 2 + D
NPIECE = 3 * MC0
WP = W0 // NPIECE
EPS = 1e-5
EPS_RMS = 1e-6
MAGIC = 12582912.0
TWO_PI_HI = 6.28125
TWO_PI_LO = 2 * math.pi - TWO_PI_HI
NEG = -1e30
MAGS = [math.sqrt(abs((-1.0) ** m / math.factorial(m)) + 1e-10) for m in range(ORD)]
RFF_SCALE = math.sqrt(2.0 / (2 * RF)) * math.sqrt(math.exp(-0.5))
PHI_SCALE2 = (MAGS[0] * RFF_SCALE) ** 2

WCOLS = [("A_in", DC * 321), ("A_omega", P), ("A_comb", 320), ("A_out", DC * D),
         ("B_q", DC * D), ("B_kT", DC * DX), ("B_bk", DC), ("B_v", D),
         ("C_q", DC * D), ("C_k", DC * D), ("C_v", DC * D), ("C_o", DC * D), ("D_gate", DC * 8),
         ("F_q", DC * D), ("F_k", D), ("F_v", D), ("F_o", DC * D), ("G_gate", DC * 8),
         ("cols", 24)]
WOFF, _o = {}, 0
for _n, _w in WCOLS:
    WOFF[_n] = (_o, _w)
    _o += _w
NW = _o
COLS = {"rb": 0, "half_pi": 1, "B_bq": 2, "C_s": 4, "C_b": 6, "D_s": 8, "D_b": 10, "F_bq": 12, "F_bk": 14}
RCOLS = [("A_in", 321), ("A_out", D), ("B_v", D), ("C_o", D), ("F_v", D), ("F_o", D),
         ("gq", D), ("gk", D), ("gv", D), ("go", D)]
ROFF, _o = {}, 0
for _n, _w in RCOLS:
    ROFF[_n] = (_o, _w)
    _o += _w
NR = _o
CCOLS = [("ident", P), ("ones", P), ("decay", S), ("causal", S), ("head", HC), ("before", 64), ("mhalf", 8), ("eps", 4),
         ("log_temp", 1)]
COFF, _o = {}, 0
for _n, _w in CCOLS:
    COFF[_n] = (_o, _w)
    _o += _w
NCST = _o
VU = 2 * HC * P
NVU = 6


class Signal:

    def __init__(self, sem, stride, base=0, turns=1):
        self.sem, self.stride, self.base, self.turns = sem, stride, base, turns

    def at(self, it, k=1, half=0):
        return it * self.stride + (self.base + self.turns * (k - 1) + half + 1)

    def free(self, it, k=1):
        return it * self.stride + k


def in_turn(*streams):
    streams = list(streams)
    while streams:
        for st in list(streams):
            if next(st, "over") == "over":
                streams.remove(st)


def late(stream):
    yield
    yield from stream


def decoder(nc, x_d, ctxT_d, ctx_d, w_d, r_d, c_d, wq_d, e0_d, e1_d, out_d):
    with ExitStack() as ctx:
        def sb(name, shape, dt=F32):
            return ctx.enter_context(nc.sbuf_tensor(name, shape, dt))

        def sig(name, stride=1, base=0):
            return Signal(ctx.enter_context(nc.semaphore(name)), stride, base)

        ps = ctx.enter_context(nc.psum_tensor("ps", [P, 8, 512], F32))

        wt = sb("wt", [P, NW])
        rows = sb("rows", [P, NR])
        cst = sb("cst", [P, NCST])
        wtern = sb("wtern", [P, 4, DC, D], BF16)
        experts_start = -(-nc.sbuf_base // 32) * 32
        experts = sb("experts", [P, max(2 * W0, E1 * W1)])
        xall = sb("xall", [S, NSEQ, D])
        hT_all_start = -(-nc.sbuf_base // 32) * 32
        hT_all = sb("hT_all", [P, DC, NG * NT])
        gates_all = sb("gates_all", [S, NSEQ, 8])
        identb = sb("identb", [P, P], BF16)
        causalb = sb("causalb", [S, NB, S], BF16)
        small = sb("small", [P, 832])
        ctxT = sb("ctxT", [P, NB, LP])
        work_start = -(-nc.sbuf_base // 32) * 32
        spread = sb("spread", [P, NVU, VU])
        probs = sb("probs", [S, 2, 800])
        probsT = sb("probsT", [P, 2, 800])
        headbd_start = -(-nc.sbuf_base // 32) * 32
        headbd = sb("headbd", [P, 2, HC, S])
        xin_start = -(-nc.sbuf_base // 32) * 32
        xin = sb("xin", [S, NB, D])
        x = sb("x", [S, NB, D])
        y_start = -(-nc.sbuf_base // 32) * 32
        y = sb("y", [S, NB, D])
        xn = sb("xn", [S, NB, D])
        hT = sb("hT", [P, DC, NT])
        qT = sb("qT", [P, DC, NT])
        kT_start = -(-nc.sbuf_base // 32) * 32
        kT = sb("kT", [P, 2, DC * LC + 80])
        xqT = sb("xqT", [P, DC, NT], BF16)
        xq = sb("xq", [S, NB, D], BF16)
        k_hi = nc.alloc_sbuf_tensor_at("k_hi", [P, 2, DC, LE], F32R, offset=kT_start)
        k_lo = nc.alloc_sbuf_tensor_at("k_lo", [P, 2, DC, LE], F32R, offset=hT_all_start)
        bd_hi = nc.alloc_sbuf_tensor_at("bd_hi", [P, 2, HC, S], F32R, offset=headbd_start)
        bd_lo = nc.alloc_sbuf_tensor_at("bd_lo", [P, 2, HC, S], F32R, offset=hT_all_start + 4 * 2 * DC * LE)
        q_hi = nc.alloc_sbuf_tensor_at("q_hi", [P, DC, NT], F32R, offset=xin_start)
        q_lo = nc.alloc_sbuf_tensor_at("q_lo", [P, DC, NT], F32R, offset=y_start)
        place = [work_start]

        def over(name, shape, dt):
            t = nc.alloc_sbuf_tensor_at(name, shape, dt, offset=place[0])
            place[0] += 4 * int(np.prod(shape[1:]))
            assert place[0] <= nc.sbuf_base
            return t

        x_hi = over("x_hi", [P, DC, NG * NT], F32R)
        x_lo = over("x_lo", [P, DC, NG * NT], F32R)
        w_hi = over("w_hi", [P, 2, W0], F32R)
        hid_hi = over("hid_hi", [P, 2, MC0, NT], F32R)
        hid_lo = over("hid_lo", [P, 2, MC0, NT], F32R)
        hid = over("hid", [P, 2, NT], F32)
        silu = over("silu", [P, 2, NT], F32)
        gate_b = over("gate_b", [P, 2, NG, NT], F32)
        gated = over("gated", [P, DC, NT], F32)
        w_lo = nc.alloc_sbuf_tensor_at("w_lo", [P, 2, W0], F32R, offset=experts_start)

        keysT = kT[:].rearrange("p s n -> p (s n)")[:, 0:DC * NT].rearrange("p (c n) -> p c n", c=DC)
        def wv(name, chunks=None, rows_=P):
            o, n = WOFF[name]
            v = wt[0:rows_, o:o + n]
            return v.rearrange("p (c n) -> p c n", c=chunks) if chunks else v

        def col(name, c=0, p=P):
            o = WOFF["cols"][0] + COLS[name] + c
            return wt[0:p, o:o + 1]

        def row(name, p=S):
            o, n = ROFF[name]
            return rows[0:p, o:o + n]

        def cs(name, p=P):
            o, n = COFF[name]
            return cst[0:p, o:o + n]

        ident = cs("ident")
        identS = ident[0:S, 0:S]
        scr = spread[:, 2:6, :].rearrange("p u n -> p (u n)")
        a_in = scr[0:S, 0:NB * 321].rearrange("p (b n) -> p b n", b=NB)
        a_sqw = scr[0:S, 1300:1300 + NB * P].rearrange("p (b n) -> p b n", b=NB)
        a_sq = a_sqw[:, :, 0:SH]
        a_shT = scr[0:SH, 1900:2300]
        a_ang = scr[0:SH, 2300:2700]
        a_lg = scr[0:S, 2300:2700].rearrange("p (b n) -> p b n", b=NB)
        a_k = scr[0:SH, 2700:3100]
        a_trig = scr[0:SH, 3100:3500]
        a_phiw = scr[0:S, 3500:3500 + NB * P].rearrange("p (b n) -> p b n", b=NB)
        a_phi = a_phiw[:, :, 0:SH]
        a_phiT = scr[0:SH, 7460:7860]
        ctxk = scr[0:KW, 4300:4300 + NB * KC * DX].rearrange("p (b c n) -> p b c n", b=NB, c=KC)
        b_e = scr[0:S, 5900:5900 + NB * LP].rearrange("p (b n) -> p b n", b=NB)
        b_eT = scr[0:KW, 0:NB * KC * S].rearrange("p (b n) -> p b n", b=NB)
        decay = scr[0:S, 7360:7460]
        c_v = scr[0:S, 0:NB * D].rearrange("p (b n) -> p b n", b=NB)
        f_e = probs[:].rearrange("p s n -> p (s n)")[:, 0:4 * LP].rearrange("p (s i n) -> p s i n", s=2, i=2)
        f_eT = probsT[0:KW].rearrange("p s n -> p (s n)")[:, 0:4 * KC * S].rearrange(
            "p (s i n) -> p s i n", s=2, i=2)
        scales = headbd[:, :, 0:4, :].rearrange("p j h n -> p j (h n)")
        g_hid, g_act = probsT[:, :, 0:NT], probsT[:, :, NT:2 * NT]
        sm_o = [0]

        def smt(n, p=S, shape=None):
            v = small[0:p, sm_o[0]:sm_o[0] + n]
            sm_o[0] += n
            return v.rearrange("p (b n) -> p b n", b=shape) if shape else v

        stats = smt(NB * 6, shape=NB)
        mv = smt(NB * 2, shape=NB)
        var_e, r1, r2, t1 = smt(4), smt(4), smt(4), smt(4)
        a_ss, a_rn, a_q, a_nm, a_sum, a_rs = smt(4), smt(4), smt(4), smt(4), smt(4), smt(4)
        b_qbk, b_mx, b_nm, b_sum, b_rs = smt(4), smt(4), smt(4), smt(4), smt(4)
        h_nm = smt(32, shape=2)
        h_sum = smt(64, shape=NB)
        h_rs = smt(64, shape=NB)
        g_s, g_e, g_rank = smt(NSEQ * 8, shape=NSEQ), smt(NSEQ * 8, shape=NSEQ), smt(NSEQ * 8, shape=NSEQ)
        g_m, g_r = smt(NSEQ), smt(NSEQ)
        gpair = smt(2 * NSEQ, shape=2)
        wsum, wscale, wrecip = smt(4, P), smt(4, P), smt(4, P)
        tempc = smt(4, P)
        q_am, q_sc, q_isc = smt(4), smt(4), smt(12, shape=3)
        bq4 = smt(2, P)
        assert sm_o[0] <= 832

        ld = {n: sig("ld_" + n) for n in ("wt", "rows", "cst", "wq", "x", "ctxT", "ctxk", "ctxT3", "e1", "out")}
        ld_e0 = [sig(f"ld_e0_{i}") for i in range(2)]
        prep_abs = sig("prep_abs")
        prep_sum = sig("prep_sum")
        prep_b = sig("prep_b")
        prep_t = sig("prep_t")
        prep_e = sig("prep_e")
        x_free = sig("x_free")
        g0_shifted, g0_e = sig("g0_shifted"), sig("g0_e")
        g1_shifted, g1_e = sig("g1_shifted"), sig("g1_e")
        tern_go = sig("tern_go")
        names = {}

        def stage(prefix, table):
            for n, per in table.items():
                names[prefix + n] = sig(prefix + n, per)

        def halves(name, per, phase1, phase3=""):
            sem = ctx.enter_context(nc.semaphore(name))
            base = 0
            for stages in (phase1, phase3):
                for i, p in enumerate(stages):
                    names[f"{p}_{name}"] = Signal(sem, 2 * per * len(stages), base + 2 * per * i, 2)
                base += 2 * per * NG * len(stages)

        def shared(name, per, phase1, phase3):
            sem = ctx.enter_context(nc.semaphore(name))
            names[f"{phase1}_{name}"] = Signal(sem, per)
            names[f"{phase3}_{name}"] = Signal(sem, per, per * NG)

        for n, stages1, stages3 in (("mv", "ABCD", "EFG"), ("rstd", "ABCD", "EFG"), ("xn", "ABCD", "FG"),
                                    ("hTp", "ABCD", "FG"), ("hT", "ABCD", "FG"),
                                    ("out", "ABC", "EF"), ("xb", "ABC", "F"),
                                    ("qTp", "BC", "F"), ("qT", "BC", "F"),
                                    ("kTp", "C", ""), ("kT", "C", ""), ("vp", "C", ""), ("v", "C", ""),
                                    ("rx", "C", "EF"), ("rTp", "C", "EF"), ("rT", "C", "EF"), ("yT", "C", "EF"),
                                    ("gs", "D", "G"), ("gc", "D", "G")):
            halves(n, 1, stages1, stages3)
        for n in ("in_p", "in", "ss", "rn", "q", "shn", "shTp", "shT", "angp", "ang", "trig", "comb", "phi",
                  "phiTp", "phiT", "lg", "nm", "e", "p", "pTp", "pT", "oTp", "oT"):
            sem_name = "A" + n
            halves(sem_name, 1, "A")
            names["A_" + n] = names.pop("A_" + sem_name)
        for n in ("kqTp", "kqT", "qbkp", "s", "nm", "e", "p", "pTp", "pT", "oTp", "oT"):
            sem_name = "B" + n
            halves(sem_name, 1, "B")
            names["B_" + n] = names.pop("B_" + sem_name)
        for n, per in (("xq", 4), ("xqTp", 4), ("xqT", 4), ("pp", 3), ("p", 3), ("ytp", 1), ("ssr", 1),
                       ("sso", 1)):
            halves(n, per, "", "E")
        names["E_kT"] = Signal(names["E_p"].sem, 6, 2, 2)
        names["E_v"] = Signal(names["E_p"].sem, 6, 4, 2)
        for n, per in {"bd": 8, "vs": 4, "s": 8, "sub": 8, "e": 8, "pTp": 8, "pT": 8, "av": 8, "rs": 1}.items():
            shared(n, per, "C", "E")
        stage("F_", {"ql": 2, "bl": 2, "kh": 8, "kvp": 20, "kv": 20, "bd": 8, "s": 32, "nm": 32, "e": 32, "pTp": 32,
                     "pT": 32, "av": 32, "o": 4, "rs": 1})
        stage("G_", {"h": 9, "act": 9, "hid": 9, "o": 9, "acc": 9})
        m_x = sig("m_x")
        m_whi = sig("m_whi", 2 * NPIECE)
        m_wlo = sig("m_wlo", 2 * NPIECE)
        m_gr = sig("m_gr")
        m_gp = sig("m_gp", 2)
        m_gb = sig("m_gb", 2)
        m_h = sig("m_h", 2 * NG * MC0)
        m_act = sig("m_act", 2 * NG * MC0)
        m_hid = sig("m_hid", 2 * NG * MC0, 2)
        m_lo = sig("m_lo", 2 * NG * MC0)
        m_out = sig("m_out", 2 * NG, 2 * NG)
        m_acc = sig("m_acc", 2 * NG, 2)
        m_sum = sig("m_sum")
        m_back = sig("m_back")

        def W(e, name, it, k=1, half=0):
            e.wait_ge(names[name].sem, names[name].at(it, k, half))

        def inc(ins, name):
            ins.then_inc(names[name].sem, 1)

        def bank(b, p=P, n=512, lo=0):
            return ps[0:p, b, lo:lo + n]

        def seqs(h):
            return range(HB * h, HB * (h + 1))

        def own(h):
            return slice(HB * h, HB * (h + 1))

        def tok(h):
            return slice(HT * h, HT * (h + 1))

        def norm_dve(e, pre, g, h, src, xn_out):
            for b in seqs(h):
                e.bn_stats(stats[:, b, :], src[:, b, :])
            e.drain()
            for b in seqs(h):
                ins = e.bn_aggr(mv[:, b, :], stats[:, b, :])
            inc(ins, pre + "mv")
            e.drain()
            yield
            W(e, pre + "rstd", g, 1, h)
            for b in seqs(h):
                ins = e.tensor_scalar(xn_out[:, b, :], src[:, b, :], mv[:, b, 0:1], r1[:, b:b + 1],
                                      ALU.subtract, ALU.mult)
            return ins

        def norm_pool(e, pre, g, h, eps2=None, fold=False):
            o = own(h)
            yield
            W(e, pre + "mv", g, 1, h)
            e.tensor_tensor(var_e[:, o], mv[:, o, 1], cs("eps", S)[:, 0:HB], ALU.add)
            e.drain()
            ins = e.tensor_tensor(r1[:, o], var_e[:, o], cs("mhalf", S)[:, 0:HB], ALU.pow)
            if eps2 is not None:
                e.drain()
                e.tensor_tensor(t1[:, o], r1[:, o], r1[:, o], ALU.mult)
                e.drain()
                e.tensor_tensor(t1[:, o], t1[:, o], mv[:, o, 1], ALU.mult)
                e.drain()
                e.tensor_scalar(t1[:, o], t1[:, o], eps2, None, ALU.add)
                e.drain()
                ins = e.tensor_tensor(r2[:, o], t1[:, o], cs("mhalf", S)[:, 0:HB], ALU.pow)
                if fold:
                    e.drain()
                    ins = e.tensor_tensor(r1[:, o], r1[:, o], r2[:, o], ALU.mult)
            inc(ins, pre + "rstd")

        def part(b0, n=HT, p=P, chunks=DC):
            return ps[0:p, b0, 0:chunks * n].rearrange("p (c n) -> p c n", c=chunks)

        def toT_pe(e, pre, g, h, name, b0, src, ready):
            yield
            W(e, ready[0], g, ready[1], h)
            for c in range(DC):
                for i, b in enumerate(seqs(h)):
                    ins = e.transpose(part(b0)[:, c, i * S:(i + 1) * S], src[:, b, c * P:(c + 1) * P], identS)
            inc(ins, pre + name)

        def toT_act(e, pre, g, h, pname, name, b0, dst, scale=None, bias=None):
            yield
            W(e, pre + pname, g, 1, h)
            if scale:
                for c in range(DC):
                    ins = e.activation(dst[:, c, tok(h)], part(b0)[:, c, :], ACT.Identity,
                                       scale=col(scale, c), bias=col(bias, c))
            else:
                ins = e.activation(dst[:, :, tok(h)], part(b0), ACT.Copy)
            inc(ins, pre + name)

        def projT_pe(e, h, w, src, b0, name):
            for m in range(DC):
                for c in range(DC):
                    ins = e.matmul(part(b0)[:, m, :], w[:, c, m * P:(m + 1) * P], src[:, c, tok(h)],
                                   start=(c == 0), stop=(c == DC - 1))
            inc(ins, name)

        def proj_pe(e, h, w, srcT, b0, name):
            for i, b in enumerate(seqs(h)):
                for c in range(DC):
                    ins = e.matmul(ps[0:S, b0, i * D:(i + 1) * D], srcT[:, c, b * S:(b + 1) * S], w[:, c, :],
                                   start=(c == 0), stop=(c == DC - 1))
            inc(ins, name)

        def tokens(b0, p=S):
            return ps[0:p, b0, 0:HB * D].rearrange("p (b n) -> p b n", b=HB)

        def pair(b0, p=S):
            return ps[0:p, b0:b0 + 2, :].rearrange("p a (b n) -> p (a b) n", b=2)

        def diag(unit, p):
            base = spread[0:p, unit, :]
            return bass.AP(tensor=base.tensor, offset=base.offset,
                           ap=[list(base.ap[0]), [HC * P, DC], [P + HD, HC], [1, HD]])

        def window(unit, p, c, h):
            return spread[0:p, unit, (c * HC + h) * P:(c * HC + h + 1) * P]

        def spread_recips_pool(e, pre, g, h):
            yield
            W(e, pre + "rs", g)
            o = own(h)
            inc(e.tensor_tensor(xn[:, o, :].rearrange("p b (h d) -> p b h d", d=HD),
                                h_rs[:, o, :].unsqueeze(3).broadcast_to([S, HB, NH, HD]),
                                cs("ones", S)[:, 0:1].unsqueeze(2).unsqueeze(3).broadcast_to([S, HB, NH, HD]),
                                ALU.mult), pre + "rx")

        def self_pe(e, pre, it):
            def scores(u):
                b, c = divmod(u, 2)
                W(e, pre + "bd", it, u + 1)
                if u >= 2:
                    W(e, pre + "sub", it, u - 1)
                for i in range(2):
                    o = bank(2 * (u % 2) + i, S, 4 * S)
                    e.matmul(o, qT[:, c, b * S:(b + 1) * S],
                             headbd[:, u % 2, 4 * i:4 * i + 4, :].rearrange("p h n -> p (h n)"),
                             start=True, stop=False)
                    ins = e.matmul(o, identb[0:S, 0:S], causalb[:].rearrange("p h n -> p (h n)"),
                                   start=False, stop=True)
                inc(ins, pre + "s")

            def turn(u):
                W(e, pre + "e", it, u + 1)
                if u >= 1:
                    W(e, pre + "pT", it, u)
                for h in range(HC):
                    ins = e.transpose(ps[0:S, 4 + h // 4, (h % 4) * S:(h % 4 + 1) * S],
                                      probs[:, u % 2, h * S:(h + 1) * S], identS)
                inc(ins, pre + "pTp")

            def values(u):
                b, c = divmod(u, 2)
                W(e, pre + "pT", it, u + 1)
                W(e, pre + "vs", it, b + 1)
                for h in range(HC):
                    ins = e.matmul(ps[:, 6 + c, b * S:(b + 1) * S], window(b % 2, S, c, h),
                                   probsT[0:S, u % 2, h * S:(h + 1) * S], start=(h == 0), stop=(h == HC - 1))
                inc(ins, pre + "av")

            for u in range(2 * NB + 2):
                if u < 2 * NB:
                    scores(u)
                if 1 <= u <= 2 * NB:
                    turn(u - 1)
                if u >= 2:
                    values(u - 2)
        def self_dve(e, pre, it):
            def shift(u):
                W(e, pre + "s", it, u + 1)
                sc = ps[0:S, 2 * (u % 2):2 * (u % 2) + 2, 0:4 * S].rearrange("p a (h n) -> p a h n", h=4)
                nm = h_nm[:, u % 2, 0:HC].rearrange("p (a h) -> p a h", a=2)
                e.tensor_reduce(nm, sc, AX, ALU.max)
                e.drain()
                if u >= 2:
                    W(e, pre + "pTp", it, u - 1)
                for i in range(2):
                    ins = e.tensor_tensor(
                        probs[:, u % 2, i * 4 * S:(i + 1) * 4 * S].rearrange("p (h n) -> p h n", h=4),
                        sc[:, i, :, :], nm[:, i, :].unsqueeze(2).broadcast_to([S, 4, S]), ALU.subtract)
                inc(ins, pre + "sub")

            def total(u):
                b, c = divmod(u, 2)
                W(e, pre + "e", it, u + 1)
                e.tensor_reduce(h_sum[:, b, c * HC:(c + 1) * HC],
                                probs[:, u % 2, :].rearrange("p (h n) -> p h n", h=HC), AX, ALU.add)

            for u in range(2 * NB + 1):
                if u < 2 * NB:
                    shift(u)
                if u >= 1:
                    total(u - 1)
            e.drain()
            inc(e.reciprocal(h_rs, h_sum), pre + "rs")

        def self_act(e, pre, it):
            def expo(u):
                W(e, pre + "sub", it, u + 1)
                inc(e.activation(probs[:, u % 2, :], probs[:, u % 2, :], ACT.Exp), pre + "e")

            def evac(u):
                W(e, pre + "pTp", it, u + 1)
                if u >= 2:
                    W(e, pre + "av", it, u - 1)
                ins = e.activation(probsT[0:S, u % 2, :].rearrange("p (a n) -> p a n", a=2),
                                   ps[0:S, 4:6, 0:4 * S], ACT.Copy)
                inc(ins, pre + "pT")

            for u in range(2 * NB + 1):
                if u < 2 * NB:
                    expo(u)
                if u >= 1:
                    evac(u - 1)

        def self_pool(e, pre, it, vsrc):
            for u in range(2 * NB):
                b, c = divmod(u, 2)
                if u == 0:
                    W(e, pre + "kT", it, 1, 1)
                if u >= 2:
                    W(e, pre + "s", it, u - 1)
                inc(e.tensor_tensor(headbd[:, u % 2],
                                    keysT[:, c, b * S:(b + 1) * S].unsqueeze(1).broadcast_to([P, HC, S]),
                                    cs("head").unsqueeze(2).broadcast_to([P, HC, S]), ALU.mult), pre + "bd")
                if c == 0:
                    if b == 0:
                        W(e, pre + "v", it, 1, 1)
                    if b >= 2:
                        W(e, pre + "av", it, 2 * (b - 1))
                    inc(e.tensor_tensor(diag(b % 2, S), vsrc[:, b, :].rearrange("p (c h d) -> p c h d", c=DC, h=HC),
                                        cs("ones", S)[:, 0:1].unsqueeze(2).unsqueeze(3).broadcast_to([S, DC, HC, HD]),
                                        ALU.mult), pre + "vs")

        def over_heads(e, dst, q, b, c):
            return e.tensor_tensor(dst[:, c], q[:, c, b * S:(b + 1) * S].unsqueeze(1).broadcast_to([P, HC, S]),
                                   cs("head").unsqueeze(2).broadcast_to([P, HC, S]), ALU.mult)

        def gate_pe(e, pre, g, h, w):
            yield
            W(e, pre + "hT", g, 1, h)
            for i, b in enumerate(seqs(h)):
                for c in range(DC):
                    ins = e.matmul(ps[0:S, 4 * h + 1, i * 8:(i + 1) * 8], hT[:, c, b * S:(b + 1) * S], w[:, c, :],
                                   start=(c == 0), stop=(c == DC - 1))
            inc(ins, pre + "gs")

        def gate_copy_dve(e, pre, g, h, dst):
            yield
            W(e, pre + "gs", g, 1, h)
            inc(e.tensor_scalar(dst, ps[0:S, 4 * h + 1, 0:8 * HB].rearrange("p (b n) -> p b n", b=HB), 1.0, None,
                                ALU.mult), pre + "gc")

        def gate_shift_dve(e, n, g_shifted, it):
            e.tensor_reduce(g_m[:, 0:n], g_s[:, 0:n, :], AX, ALU.max)
            e.drain()
            e.tensor_tensor(g_e[:, 0:n, :], g_s[:, 0:n, :], g_m[:, 0:n].unsqueeze(2).broadcast_to([S, n, 8]),
                            ALU.subtract).then_inc(g_shifted.sem, 1)

        def gate_top_dve(e, n, probs_first, out_gates, beats, ties):
            s_, e_, m_, r_, k_ = g_s[:, 0:n, :], g_e[:, 0:n, :], g_m[:, 0:n], g_r[:, 0:n], g_rank[:, 0:n, :]
            bc = lambda v: v.unsqueeze(2).broadcast_to([S, n, 8])
            if probs_first:
                e.tensor_reduce(m_, e_, AX, ALU.add)
                e.drain()
                e.reciprocal(r_, m_)
                e.drain()
                e.tensor_tensor(e_, e_, bc(r_), ALU.mult)
                e.drain()
            key = e_ if probs_first else s_
            sh = [S, n, 8, 8]
            mine = key.unsqueeze(3).broadcast_to(sh)
            other = key.unsqueeze(2).broadcast_to(sh)
            beats, ties = (t.rearrange("p (b e f) -> p b e f", b=n, e=8) for t in (beats, ties))
            before = cs("before", S).rearrange("p (e f) -> p e f", e=8).unsqueeze(1).broadcast_to(sh)
            e.tensor_tensor(beats, other, mine, ALU.is_gt)
            e.tensor_tensor(ties, other, mine, ALU.is_equal)
            e.drain()
            e.tensor_tensor(ties, ties, before, ALU.mult)
            e.drain()
            e.tensor_tensor(beats, beats, ties, ALU.add)
            e.drain()
            e.tensor_reduce(k_, beats, AX, ALU.add)
            e.drain()
            e.scalar_tensor_tensor(e_, k_, 1.5, e_, ALU.is_lt, ALU.mult)
            e.drain()
            e.tensor_reduce(m_, e_, AX, ALU.add)
            e.drain()
            if probs_first:
                e.tensor_scalar(m_, m_, 1e-20, None, ALU.add)
                e.drain()
            e.reciprocal(r_, m_)
            e.drain()
            e.tensor_tensor(out_gates, e_, bc(r_), ALU.mult)
            e.drain()

        block = ctx.enter_context(nc.Block())

        @block.sync
        def _(e):
            def load_group(g):
                e.dma_start(xin[:], x_d[g]).then_inc(ld["x"].sem, 16)
                e.dma_start(ctxT[:], ctxT_d[g]).then_inc(ld["ctxT"].sem, 16)
                e.dma_start(ctxk, ctx_d[g]).then_inc(ld["ctxk"].sem, 16)

            e.dma_start(xin[:], x_d[0]).then_inc(ld["x"].sem, 16)
            e.dma_start(cst[:], c_d).then_inc(ld["cst"].sem, 16)
            e.dma_start(experts[:, 0:4 * DC * D], wq_d).then_inc(ld["wq"].sem, 16)
            e.dma_start(wt[:], w_d).then_inc(ld["wt"].sem, 16)
            e.dma_start(rows[:], r_d).then_inc(ld["rows"].sem, 16)
            e.dma_start(ctxT[:], ctxT_d[0]).then_inc(ld["ctxT"].sem, 16)
            e.dma_start(ctxk, ctx_d[0]).then_inc(ld["ctxk"].sem, 16)
            with e.Fori(0, NG - 1) as g:
                W(e, "B_oTp", g, 1, 1)
                load_group(g + 1)
            e.wait_ge(tern_go.sem, 1)
            with e.Fori(0, E0 // 2) as ep:
                for s in range(2):
                    e.wait_ge(m_out.sem, m_out.free(ep, NG * (s + 1)))
                    e.dma_start(experts[:, s * W0:(s + 1) * W0], e0_d[2 * ep + s]).then_inc(ld_e0[s].sem, 16)
            W(e, "B_oTp", NG - 1, 1, 1)
            e.dma_start(ctxT[:], ctxT_d[0]).then_inc(ld["ctxT3"].sem, 16)
            e.wait_ge(m_out.sem, m_out.at(E0 // 2 - 1, 2 * NG))
            e.dma_start(experts[:, 0:E1 * W1], e1_d).then_inc(ld["e1"].sem, 16)
            e.sem_inc(x_free.sem, 1)
            with e.Fori(0, NG - 1) as g:
                W(e, "F_kvp", g, 5 * NB)
                e.dma_start(ctxT[:], ctxT_d[g + 1]).then_inc(ld["ctxT3"].sem, 16)
                W(e, "G_acc", g, E1)
                e.dma_start(out_d[g], x[:]).then_inc(ld["out"].sem, 16)
                e.wait_ge(ld["out"].sem, g * 16 + 16)
                e.sem_inc(x_free.sem, 1)
            W(e, "G_acc", NG - 1, E1)
            e.dma_start(out_d[NG - 1], x[:]).then_inc(ld["out"].sem, 16)
            e.wait_ge(ld["out"].sem, NG * 16)

        @block.tensor
        def _(e):
            e.wait_ge(ld["cst"].sem, 16)
            e.wait_ge(prep_abs.sem, 1)
            inc_ = e.matmul(bank(0, n=4), cs("ones"), wsum, start=True, stop=True)
            inc_.then_inc(prep_sum.sem, 1)
            e.wait_ge(ld["wt"].sem, 16)
            e.wait_ge(prep_b.sem, 1)

            def before_c(g, h):
                b0, t, bs = 4 * h, tok(h), list(enumerate(seqs(h)))
                yield from toT_pe(e, "A_", g, h, "hTp", b0, xn, ("A_xn", 1))
                yield
                W(e, "A_hT", g, 1, h)
                w = wv("A_in", DC)
                for i, b in bs:
                    for c in range(DC):
                        ins = e.matmul(bank(b0 + 1 + i, S, 321), hT[:, c, b * S:(b + 1) * S], w[:, c, :],
                                       start=(c == 0), stop=(c == DC - 1))
                inc(ins, "A_in_p")
                yield
                W(e, "A_shn", g, 1, h)
                for i, b in bs:
                    ins = e.transpose(ps[:, b0, i * S:(i + 1) * S], a_sqw[:, b, :], identS)
                inc(ins, "A_shTp")
                yield
                W(e, "A_shT", g, 1, h)
                inc(e.matmul(bank(b0 + 3, n=HT), wv("A_omega", rows_=SH), a_shT[:, t], start=True, stop=True), "A_angp")
                yield
                W(e, "A_trig", g, 1, h)
                for i, b in bs:
                    ins = e.matmul(bank(b0 + 1 + i, S, 320), a_trig[:, b * S:(b + 1) * S], wv("A_comb", rows_=SH),
                                   start=True, stop=True)
                inc(ins, "A_comb")
                yield
                W(e, "A_phi", g, 1, h)
                for i, b in bs:
                    ins = e.transpose(ps[:, b0, i * S:(i + 1) * S], a_phiw[:, b, :], identS)
                inc(ins, "A_phiTp")
                yield
                W(e, "A_phiT", g, 1, h)
                for i, b in bs:
                    pb = a_phiT[:, b * S:(b + 1) * S]
                    ins = e.matmul(ps[0:S, b0 + 3, i * S:(i + 1) * S], pb, pb, start=True, stop=True)
                inc(ins, "A_lg")
                yield
                W(e, "A_p", g, 1, h)
                for i, b in bs:
                    ins = e.transpose(ps[0:S, b0, i * S:(i + 1) * S], a_lg[:, b, :], identS)
                inc(ins, "A_pTp")
                yield
                W(e, "A_pT", g, 1, h)
                for c in range(DC):
                    for i, b in bs:
                        ins = e.matmul(part(b0 + 1)[:, c, i * S:(i + 1) * S], a_in[:, b, 65 + c * P:65 + (c + 1) * P],
                                       probsT[0:S, 0, b * S:(b + 1) * S], start=True, stop=True)
                inc(ins, "A_oTp")
                yield
                W(e, "A_oT", g, 1, h)
                proj_pe(e, h, wv("A_out", DC), qT, b0 + 2, "A_out")
                yield from toT_pe(e, "B_", g, h, "hTp", b0, xn, ("B_xn", 1))
                yield
                W(e, "B_hT", g, 1, h)
                projT_pe(e, h, wv("B_q", DC), hT, b0 + 1, "B_qTp")
                yield
                W(e, "B_qT", g, 1, h)
                for c in range(DC):
                    ins = e.matmul(bank(b0 + 2, n=HT), wv("B_kT", DC)[:, c, :], qT[:, c, t],
                                   start=(c == 0), stop=(c == DC - 1))
                inc(ins, "B_kqTp")
                for i, b in bs:
                    for c in range(DC):
                        ins = e.matmul(ps[0:S, b0 + 3, i:i + 1], qT[:, c, b * S:(b + 1) * S], wv("B_bk", DC)[:, c, :],
                                       start=(c == 0), stop=(c == DC - 1))
                inc(ins, "B_qbkp")
                yield
                W(e, "B_kqT", g, 1, h)
                e.wait_ge(ld["ctxT"].sem, g * 16 + 16)
                for i, b in bs:
                    ins = e.matmul(bank(b0 + 1 + i, S, LC), hT[:, 0, b * S:(b + 1) * S], ctxT[:, b, 0:LC],
                                   start=True, stop=True)
                inc(ins, "B_s")
                yield
                W(e, "B_p", g, 1, h)
                for i, b in bs:
                    for k in range(KC):
                        ins = e.transpose(ps[0:KW, b0 + 3 * i, k * S:(k + 1) * S], b_e[:, b, k * KW:(k + 1) * KW],
                                          identS)
                inc(ins, "B_pTp")
                yield
                W(e, "B_pT", g, 1, h)
                e.wait_ge(ld["ctxk"].sem, g * 16 + 16)
                for i, b in bs:
                    for k in range(KC):
                        ins = e.matmul(ps[:, b0 + 1, i * S:(i + 1) * S], ctxk[:, b, k, :], b_eT[:, b, k * S:(k + 1) * S],
                                       start=(k == 0), stop=(k == KC - 1))
                inc(ins, "B_oTp")
                yield
                W(e, "B_oT", g, 1, h)
                for i, b in bs:
                    ins = e.matmul(ps[0:S, b0 + 2, i * D:(i + 1) * D], hT[:, 1, b * S:(b + 1) * S],
                                   wv("B_v"), start=True, stop=True)
                inc(ins, "B_out")
                yield from toT_pe(e, "C_", g, h, "hTp", b0, xn, ("C_xn", 1))
                yield
                W(e, "C_hT", g, 1, h)
                proj_pe(e, h, wv("C_v", DC), hT, b0 + 1, "C_vp")
                projT_pe(e, h, wv("C_k", DC), hT, b0 + 2, "C_kTp")
                projT_pe(e, h, wv("C_q", DC), hT, b0 + 3, "C_qTp")

            def after_c(g, h):
                b0 = 4 * h
                yield from toT_pe(e, "C_", g, h, "rTp", b0, xn, ("C_rx", 1))
                yield
                W(e, "C_yT", g, 1, h)
                proj_pe(e, h, wv("C_o", DC), qT, b0 + 1, "C_out")
                yield from toT_pe(e, "D_", g, h, "hTp", b0, xn, ("D_xn", 1))
                yield from gate_pe(e, "D_", g, h, wv("D_gate", DC))

            with e.Fori(0, NG) as g:
                in_turn(before_c(g, 0), before_c(g, 1))
                W(e, "C_v", g, 1, 1)
                W(e, "C_kT", g, 1, 1)
                W(e, "C_qT", g, 1, 1)
                self_pe(e, "C_", g)
                in_turn(after_c(g, 0), after_c(g, 1))
            def product(out, w, rhs_hi, rhs_lo, start, stop):
                wh, wl = w
                e.matmul(out, wh, rhs_hi, start=start, stop=False)
                e.matmul(out, wh, rhs_lo, start=False, stop=False)
                return e.matmul(out, wl, rhs_hi, start=False, stop=stop)

            def weights(slot, o):
                return w_hi[:, slot, o:o + P], w_lo[:, slot, o:o + P]

            def up(ep, s, m):
                slot, gi = divmod(s, NG)
                t = slice(gi * NT, (gi + 1) * NT)
                if gi == 0 and m == 0:
                    e.wait_ge(m_wlo.sem, m_wlo.at(ep, NPIECE * slot + 2 * DC * HID0 // WP))
                if slot == 0 and m == 0:
                    e.wait_ge(m_x.sem, gi + 1)
                e.wait_ge(m_hid.sem, m_hid.free(ep, s * MC0 + m + 1))
                for i in range(2):
                    for c in range(DC):
                        ins = product(bank(2 * i + m % 2, n=NT), weights(slot, (i * DC + c) * HID0 + m * P),
                                      x_hi[:, c, t], x_lo[:, c, t], c == 0, c == DC - 1)
                ins.then_inc(m_h.sem, 1)

            def spread_gates(ep, slot):
                if slot == 0:
                    e.wait_ge(m_gr.sem, ep + 1)
                e.wait_ge(m_acc.sem, m_acc.free(ep, NG * slot + 2))
                for q in range(NSEQ):
                    ins = e.matmul(ps[:, 4 + q // NB, (q % NB) * S:(q % NB + 1) * S],
                                   gpair[:, slot, q:q + 1].broadcast_to([S, P]), identS, start=True, stop=True)
                ins.then_inc(m_gp.sem, 1)

            def down(ep, s):
                slot, gi = s // NG % 2, s % NG
                e.wait_ge(m_lo.sem, m_lo.at(ep, MC0 * (s + 1)))
                if gi == 0:
                    e.wait_ge(m_wlo.sem, m_wlo.at(ep, NPIECE * (slot + 1)))
                    e.wait_ge(m_gb.sem, m_gb.at(ep, slot + 1))
                e.wait_ge(m_acc.sem, m_acc.free(ep, s + 1))
                for m in range(DC):
                    for c in range(MC0):
                        ins = product(bank(4 + 2 * (s % 2) + m, n=NT),
                                      weights(slot, 2 * DC * HID0 + c * D + m * P),
                                      hid_hi[:, s % 2, c, :], hid_lo[:, s % 2, c, :], c == 0, c == MC0 - 1)
                ins.then_inc(m_out.sem, 1)

            def experts_pe(ep, first=False):
                for s in range(2 * NG):
                    up(ep, s, 0)
                    up(ep, s, 1)
                    if s >= 1 or not first:
                        down(ep, s - 1)
                    up(ep, s, 2)
                    up(ep, s, 3)
                    if s % NG == 0:
                        spread_gates(ep, s // NG)

            experts_pe(0, True)
            with e.Fori(1, E0 // 2) as ep:
                experts_pe(ep)
            down(E0 // 2, -1)
            e.wait_ge(m_sum.sem, 1)
            for q in range(NSEQ):
                for c in range(DC):
                    ins = e.transpose(ps[0:S, q // 2, (q % 2) * D + c * P:(q % 2) * D + (c + 1) * P],
                                      hT_all[:, c, q * S:(q + 1) * S], ident)
                if q % 2:
                    ins.then_inc(m_back.sem, 1)
            def ternT_pe(g, h, j, b0):
                W(e, "E_xq", g, j + 1, h)
                pb = ps[:, b0, :].bitcast(BF16)
                for c in range(DC):
                    for i, b in enumerate(seqs(h)):
                        ins = e.transpose(pb[:, c * HT + i * S:c * HT + (i + 1) * S], xq[:, b, c * P:(c + 1) * P],
                                          identb[0:S, 0:S])
                return ins

            def before_e(g, h):
                yield
                yield
                for j in range(3):
                    if h == 1:
                        W(e, "E_xqT", g, j + 1, 0)
                    elif j:
                        W(e, "E_xqT", g, j, 1)
                    ins = ternT_pe(g, h, j, 6)
                    if j < 2:
                        for i, b in enumerate(seqs(h)):
                            ins = e.matmul(ps[:, 6, 256 + i * S:256 + (i + 1) * S], cs("ones", S), y[:, b, 0:S],
                                           start=True, stop=True)
                    inc(ins, "E_xqTp")
                    yield
                    W(e, "E_xqT", g, j + 1, h)
                    if h == 1:
                        W(e, "E_p", g, j + 1, 0)
                    elif j:
                        W(e, "E_p", g, j, 1)
                    if j < 2:
                        projT_pe(e, h, wtern[:, j], xqT, 7, "E_pp")
                    else:
                        proj_pe(e, h, wtern[:, j], xqT, 7, "E_pp")
                    yield

            def kv(g, b, i):
                n = 5 * b + i
                if n >= 1:
                    W(e, "F_kv", g, n)
                if i < DC:
                    ins = e.matmul(bank(7, n=LE), wv("F_k")[:, i * P:(i + 1) * P], ctxT[:, b, 0:LE],
                                   start=True, stop=True)
                else:
                    k = i - DC
                    ins = e.matmul(bank(7, KW, D), ctxT[:, b, k * KW:(k + 1) * KW], wv("F_v"),
                                   start=True, stop=True)
                inc(ins, "F_kvp")

            def after_e(g, h):
                b0 = 4 * h
                yield from toT_pe(e, "E_", g, h, "rTp", b0, xn, ("E_rx", 1))
                yield
                W(e, "E_yT", g, 1, h)
                for i, b in enumerate(seqs(h)):
                    for c in range(DC):
                        ins = e.transpose(ps[0:S, b0 + 1, i * D + c * P:i * D + (c + 1) * P],
                                          qT[:, c, b * S:(b + 1) * S], ident)
                inc(ins, "E_ytp")
                if h == 1:
                    e.wait_ge(ld["ctxT3"].sem, g * 16 + 16)
                    for i in range(3):
                        kv(g, 0, i)
                yield
                inc(ternT_pe(g, h, 3, b0), "E_xqTp")
                if h == 1:
                    kv(g, 0, 3)
                yield
                W(e, "E_xqT", g, 4, h)
                proj_pe(e, h, wtern[:, 3], xqT, b0 + 1, "E_out")
                if h == 1:
                    kv(g, 0, 4)
                yield from toT_pe(e, "F_", g, h, "hTp", b0, xn, ("F_xn", 1))
                yield
                W(e, "F_hT", g, 1, h)
                projT_pe(e, h, wv("F_q", DC), hT, b0 + 1, "F_qTp")

            def after_f(g, h):
                b0 = 4 * h
                yield from toT_pe(e, "F_", g, h, "rTp", b0, xn, ("F_rx", 1))
                yield
                W(e, "F_yT", g, 1, h)
                proj_pe(e, h, wv("F_o", DC), qT, b0 + 1, "F_out")
                yield from toT_pe(e, "G_", g, h, "hTp", b0, xn, ("G_xn", 1))
                yield from gate_pe(e, "G_", g, h, wv("G_gate", DC))

            in_turn(late(before_e(0, 1)), before_e(0, 0))

            def group_pe(g, last=False):
                W(e, "E_kT", g, 1, 1)
                W(e, "E_v", g, 1, 1)
                self_pe(e, "E_", g)
                in_turn(after_e(g, 0), after_e(g, 1))

                def f_scores(b, v):
                    n, c = 8 * b + v, v // 4
                    W(e, "F_bd", g, 2 * b + c + 1)
                    if b == 0:
                        W(e, "F_bl", g, c + 1)
                    if v == 0:
                        W(e, "F_kv", g, 5 * b + 2)
                    if n >= 2:
                        W(e, "F_e", g, n - 1)
                    for i in range(2):
                        h = 2 * (v % 4) + i
                        ins = product(bank(2 * (n % 2) + i, S, LE), (bd_hi[:, c, h, :], bd_lo[:, c, h, :]),
                                      k_hi[:, b % 2, c, :], k_lo[:, b % 2, c, :], True, True)
                    inc(ins, "F_s")

                def f_turn(b, v):
                    n = 8 * b + v
                    W(e, "F_e", g, n + 1)
                    if n == 0:
                        W(e, "F_qT", g, 1, 1)
                    else:
                        W(e, "F_pT", g, n)
                    for i in range(2):
                        for k in range(KC):
                            ins = e.transpose(ps[0:KW, 4 + i, k * S:(k + 1) * S],
                                              f_e[:, n % 2, i, k * KW:(k + 1) * KW], identS)
                    inc(ins, "F_pTp")

                def f_values(b, v):
                    n, c = 8 * b + v, v // 4
                    W(e, "F_pT", g, n + 1)
                    if v == 0:
                        W(e, "F_kv", g, 5 * b + 5)
                        if b >= 1:
                            W(e, "F_o", g, b)
                    for i in range(2):
                        h = 2 * (v % 4) + i
                        for k in range(KC):
                            ins = e.matmul(ps[:, 6, (2 * (b % 2) + c) * S:(2 * (b % 2) + c + 1) * S],
                                           window(3 * (b % 2) + k, KW, c, h), f_eT[:, n % 2, i, k * S:(k + 1) * S],
                                           start=(h == 0 and k == 0), stop=(h == HC - 1 and k == KC - 1))
                    inc(ins, "F_av")

                W(e, "F_qT", g, 1, 0)
                units = [(b, v) for b in range(NB) for v in range(8)]
                for n in range(len(units) + 2):
                    if n < len(units):
                        b, v = units[n]
                        f_scores(b, v)
                    if 1 <= n <= len(units):
                        f_turn(*units[n - 1])
                    if n >= 2:
                        f_values(*units[n - 2])
                    if n < len(units) and b + 1 < NB and 3 <= v < 8:
                        kv(g, b + 1, v - 3)
                in_turn(after_f(g, 0), after_f(g, 1))
                e.wait_ge(ld["e1"].sem, 16)
                W(e, "G_gc", g, 1, 1)
                if last:
                    in_turn(experts_g(g))
                else:
                    in_turn(late(before_e(g + 1, 1)), before_e(g + 1, 0), experts_g(g))

            def experts_g(g):
                for j in range(E1 + 1):
                    if j < E1:
                        if j >= 2:
                            W(e, "G_hid", g, j - 1)
                        for i in range(2):
                            o = j * W1 + i * DC * HID1
                            w = experts[:, o:o + DC * HID1].rearrange("p (c n) -> p c n", c=DC)
                            for c in range(DC):
                                ins = e.matmul(bank(2 * i + j % 2, n=NT), w[:, c, :], hT[:, c, :],
                                               start=(c == 0), stop=(c == DC - 1))
                        inc(ins, "G_h")
                    if j >= 1:
                        W(e, "G_hid", g, j)
                        if j >= 2:
                            W(e, "G_acc", g, j - 1)
                        for b in range(NB):
                            ins = e.matmul(ps[0:S, 4 + b // 2, (b % 2) * D:(b % 2 + 1) * D],
                                           g_hid[:, (j - 1) % 2, b * S:(b + 1) * S],
                                           experts[:, j * W1 - D:j * W1], start=True, stop=True)
                        inc(ins, "G_o")
                    yield

            with e.Fori(0, NG - 1) as g:
                group_pe(g)
            group_pe(NG - 1, True)

        @block.scalar
        def _(e):
            e.wait_ge(ld["cst"].sem, 16)
            e.activation(identb[:], ident, ACT.Copy)
            for b in range(NB):
                ins = e.activation(causalb[:, b, :], cs("causal", S), ACT.Copy)
            ins.then_inc(prep_b.sem, 1)
            e.wait_ge(prep_t.sem, 1)
            e.activation(tempc[:, 1:2], tempc[:, 0:1], ACT.Exp, scale=-1.0)
            e.drain()
            e.activation(tempc[:, 1:2], tempc[:, 1:2], ACT.Ln, bias=1.0).then_inc(prep_e.sem, 1)

            def before_c(g, h):
                b0, t, o = 4 * h, tok(h), own(h)
                yield from toT_act(e, "A_", g, h, "hTp", "hT", b0, hT)
                yield
                W(e, "A_in", g, 1, h)
                inc(e.activation(a_q[:, o], a_in[:, o, SH], ACT.Tanh), "A_q")
                yield
                W(e, "A_shTp", g, 1, h)
                inc(e.activation(a_shT[:, t], bank(b0, SH, HT), ACT.Copy), "A_shT")
                yield
                W(e, "A_ang", g, 1, h)
                inc(e.activation(a_trig[:, t], a_ang[:, t], ACT.Sin), "A_trig")
                yield
                W(e, "A_phiTp", g, 1, h)
                inc(e.activation(a_phiT[:, t], bank(b0, SH, HT), ACT.Copy), "A_phiT")
                yield
                W(e, "A_nm", g, 1, h)
                for b in seqs(h):
                    ins = e.activation(a_lg[:, b, :], a_lg[:, b, :], ACT.Exp, bias=a_nm[:, b:b + 1],
                                       accum_out=a_sum[:, b:b + 1])
                inc(ins, "A_e")
                yield
                W(e, "A_pTp", g, 1, h)
                inc(e.activation(probsT[0:S, 0, t], bank(b0, S, HT), ACT.Copy), "A_pT")
                yield
                W(e, "A_oTp", g, 1, h)
                inc(e.activation(qT[:, :, t], part(b0 + 1), ACT.Copy), "A_oT")
                yield from toT_act(e, "B_", g, h, "hTp", "hT", b0, hT)
                yield
                W(e, "B_qTp", g, 1, h)
                for m in range(DC):
                    ins = e.activation(qT[:, m, t], part(b0 + 1)[:, m, :], ACT.Identity, bias=col("B_bq", m))
                inc(ins, "B_qT")
                yield
                W(e, "B_kqTp", g, 1, h)
                inc(e.activation(hT[:, 0, t], bank(b0 + 2, n=HT), ACT.Copy), "B_kqT")
                yield
                W(e, "B_nm", g, 1, h)
                for i, b in enumerate(seqs(h)):
                    ins = e.activation(b_e[:, b, 0:LC], bank(b0 + 1 + i, S, LC), ACT.Exp, bias=b_nm[:, b:b + 1],
                                       accum_out=b_sum[:, b:b + 1])
                inc(ins, "B_e")
                yield
                W(e, "B_pTp", g, 1, h)
                for i, b in enumerate(seqs(h)):
                    ins = e.activation(b_eT[:, b, :], bank(b0 + 3 * i, KW, KC * S), ACT.Copy)
                inc(ins, "B_pT")
                yield
                W(e, "B_oTp", g, 1, h)
                inc(e.activation(hT[:, 1, t], bank(b0 + 1, n=HT), ACT.Copy), "B_oT")
                yield from toT_act(e, "C_", g, h, "hTp", "hT", b0, hT, "C_s", "C_b")
                yield
                W(e, "C_kTp", g, 1, h)
                inc(e.activation(keysT[:, :, t], part(b0 + 2), ACT.Copy), "C_kT")
                yield
                W(e, "C_qTp", g, 1, h)
                inc(e.activation(qT[:, :, t], part(b0 + 3), ACT.Copy, scale=HD ** -0.5), "C_qT")

            def after_c(g, h):
                yield from toT_act(e, "C_", g, h, "rTp", "rT", 4 * h, hT)
                yield from toT_act(e, "D_", g, h, "hTp", "hT", 4 * h, hT, "D_s", "D_b")

            with e.Fori(0, NG) as g:
                in_turn(before_c(g, 0), before_c(g, 1))
                self_act(e, "C_", g)
                in_turn(after_c(g, 0), after_c(g, 1))
            def split_hi(slot, k):
                e.activation(w_hi[:, slot, k * WP:(k + 1) * WP], experts[:, slot * W0 + k * WP:slot * W0 + (k + 1) * WP],
                             ACT.Copy).then_inc(m_whi.sem, 1)

            def experts_act(ep, last=False):
                for n in range(2 * NG * MC0):
                    slot, k = divmod(n, NG * MC0)
                    e.wait_ge(m_h.sem, m_h.at(ep, n + 1))
                    e.wait_ge(m_hid.sem, m_hid.free(ep, n + 1))
                    e.activation(silu[:, n % 2, :], bank(n % 2, n=NT), ACT.Silu).then_inc(m_act.sem, 1)
                    if k == MC0:
                        e.wait_ge(m_gp.sem, m_gp.at(ep, slot + 1))
                        e.activation(gate_b[:, slot], ps[:, 4:8, 0:NT], ACT.Copy).then_inc(m_gb.sem, 1)
                    if 6 <= k < 6 + NPIECE // 2 and not (last and slot == 1):
                        if k == 6:
                            e.wait_ge(ld_e0[1 - slot].sem, (ep + slot) * 16 + 16)
                        split_hi(1 - slot, 2 * (k - 6))
                        split_hi(1 - slot, 2 * (k - 6) + 1)

            e.wait_ge(ld_e0[0].sem, 16)
            for k in range(NPIECE):
                split_hi(0, k)
            e.wait_ge(g0_shifted.sem, 1)
            e.activation(g_e, g_e, ACT.Exp).then_inc(g0_e.sem, 1)
            with e.Fori(0, E0 // 2 - 1) as ep:
                experts_act(ep)
            experts_act(E0 // 2 - 1, True)
            def tern_act(g, h, j, b0):
                W(e, "E_xqTp", g, j + 1, h)
                return e.activation(xqT[:, :, tok(h)],
                                    ps[:, b0, :].bitcast(BF16)[:, 0:DC * HT].rearrange("p (c n) -> p c n", c=DC),
                                    ACT.Copy)

            def before_e(g, h):
                yield
                yield
                for j in range(3):
                    ins = tern_act(g, h, j, 6)
                    if j < 2:
                        ins = e.activation(scales[:, j, tok(h)], bank(6, n=HT, lo=256), ACT.Copy,
                                           scale=wscale[:, j:j + 1])
                    inc(ins, "E_xqT")
                    yield
                    yield

            def key_evac(g, b, i):
                W(e, "F_kvp", g, 5 * b + i + 1)
                inc(e.activation(k_hi[:, b % 2, i, :], bank(7, n=LE), ACT.Identity, bias=col("F_bk", i)), "F_kh")

            def after_e(g, h):
                yield from toT_act(e, "E_", g, h, "rTp", "rT", 4 * h, hT)
                if h == 1:
                    key_evac(g, 0, 0)
                    key_evac(g, 0, 1)
                yield
                inc(tern_act(g, h, 3, 4 * h), "E_xqT")
                yield from toT_act(e, "F_", g, h, "hTp", "hT", 4 * h, hT)
                yield
                W(e, "F_qTp", g, 1, h)
                for dst in (qT, q_hi):
                    for m in range(DC):
                        ins = e.activation(dst[:, m, tok(h)], part(4 * h + 1)[:, m, :], ACT.Identity,
                                           scale=HD ** -0.5, bias=bq4[:, m:m + 1])
                inc(ins, "F_qT")

            def after_f(g, h):
                yield from toT_act(e, "F_", g, h, "rTp", "rT", 4 * h, keysT)
                yield from toT_act(e, "G_", g, h, "hTp", "hT", 4 * h, hT)

            in_turn(late(before_e(0, 1)), before_e(0, 0))

            def group_act(g, last=False):
                self_act(e, "E_", g)
                in_turn(after_e(g, 0), after_e(g, 1))

                for n in range(8 * NB):
                    b, v = divmod(n, 8)
                    W(e, "F_nm", g, n + 1)
                    if n >= 2:
                        W(e, "F_pTp", g, n - 1)
                    for i in range(2):
                        h = 2 * v + i
                        ins = e.activation(f_e[:, n % 2, i, 0:LC], bank(2 * (n % 2) + i, S, LC), ACT.Exp,
                                           bias=h_nm[:, n % 2, i:i + 1], accum_out=h_sum[:, b, h:h + 1])
                    inc(ins, "F_e")
                    if v == 1 and b >= 1:
                        W(e, "F_av", g, 8 * b)
                        inc(e.activation(hT[:, :, (b - 1) * S:b * S],
                                         ps[:, 6, 2 * ((b - 1) % 2) * S:2 * ((b - 1) % 2) * S + 2 * S].rearrange(
                                             "p (c n) -> p c n", c=DC), ACT.Copy), "F_o")
                    if b + 1 < NB and v in (3, 4):
                        key_evac(g, b + 1, v - 3)
                W(e, "F_av", g, 8 * NB)
                inc(e.activation(hT[:, :, (NB - 1) * S:NB * S],
                                 ps[:, 6, 2 * S:4 * S].rearrange("p (c n) -> p c n", c=DC), ACT.Copy), "F_o")
                in_turn(after_f(g, 0), after_f(g, 1))
                if last:
                    in_turn(experts_g(g))
                else:
                    in_turn(late(before_e(g + 1, 1)), before_e(g + 1, 0), experts_g(g))

            def experts_g(g):
                e.wait_ge(g1_shifted.sem, g1_shifted.at(g))
                e.activation(g_e[:, 0:NB, :], g_e[:, 0:NB, :], ACT.Exp).then_inc(g1_e.sem, 1)
                for j in range(E1):
                    W(e, "G_h", g, j + 1)
                    if j >= 2:
                        W(e, "G_hid", g, j - 1)
                    inc(e.activation(g_act[:, j % 2, :], bank(j % 2, n=NT), ACT.Gelu), "G_act")
                    yield

            with e.Fori(0, NG - 1) as g:
                group_act(g)
            group_act(NG - 1, True)

        @block.gpsimd
        def _(e):
            e.memset(spread[:, 0:2, :], 0.0)
            e.wait_ge(ld["cst"].sem, 16)
            e.drain()
            bcast = lambda name: row(name).unsqueeze(1).broadcast_to([S, HB, D])

            def add_bias(dst, src, name, h):
                return e.tensor_tensor(dst[:, own(h), :], src[:, own(h), :], bcast(name), ALU.add)

            def before_c(g, h):
                yield from norm_pool(e, "A_", g, h)
                if h == 0:
                    e.wait_ge(ld["rows"].sem, 16)
                inc(add_bias(x, xin, "A_out", h), "A_xb")
                yield
                W(e, "A_ss", g, 1, h)
                inc(e.tensor_tensor(a_rn[:, own(h)], a_ss[:, own(h)], cs("mhalf", S)[:, 0:HB], ALU.pow), "A_rn")
                yield from norm_pool(e, "B_", g, h)
                yield
                W(e, "B_xn", g, 1, h)
                inc(add_bias(x, x, "B_v", h), "B_xb")
                yield from norm_pool(e, "C_", g, h, eps2=EPS)
                yield
                W(e, "C_xn", g, 1, h)
                inc(add_bias(y, y, "C_o", h), "C_xb")

            def after_c(g, h):
                yield from spread_recips_pool(e, "C_", g, h)
                yield from norm_pool(e, "D_", g, h)

            with e.Fori(0, NG) as g:
                in_turn(before_c(g, 0), before_c(g, 1))
                self_pool(e, "C_", g, c_v)
                in_turn(after_c(g, 0), after_c(g, 1))
            def split_lo(ep, slot, k, n):
                raw = experts[:, slot * W0 + k * WP:slot * W0 + (k + 1) * WP]
                e.wait_ge(m_whi.sem, m_whi.at(ep, n))
                e.tensor_tensor(w_lo[:, slot, k * WP:(k + 1) * WP], raw, w_hi[:, slot, k * WP:(k + 1) * WP],
                                ALU.subtract).then_inc(m_wlo.sem, 1)

            def experts_pool(ep, last=False):
                for n in range(2 * NG * MC0):
                    s, m = divmod(n, MC0)
                    slot, k = divmod(n, NG * MC0)
                    e.wait_ge(m_hid.sem, m_hid.at(ep, n + 1))
                    e.tensor_tensor(hid_lo[:, s % 2, m, :], hid[:, n % 2, :], hid_hi[:, s % 2, m, :],
                                    ALU.subtract).then_inc(m_lo.sem, 1)
                    if 6 <= k < 6 + NPIECE // 2 and not (last and slot == 1):
                        for p in (2 * (k - 6), 2 * (k - 6) + 1):
                            split_lo(ep, 1 - slot, p, NPIECE * (slot + 1) + p + 1)

            for k in range(NPIECE):
                split_lo(0, 0, k, k + 1)
            with e.Fori(0, E0 // 2 - 1) as ep:
                experts_pool(ep)
            experts_pool(E0 // 2 - 1, True)
            e.wait_ge(m_acc.sem, m_acc.at(E0 // 2 - 1, 2 * NG))
            def before_e(g, h):
                yield from norm_pool(e, "E_", g, h, eps2=EPS_RMS, fold=True)

            def after_e(g, h):
                yield from spread_recips_pool(e, "E_", g, h)
                yield
                W(e, "E_ssr", g, 1, h)
                inc(e.tensor_tensor(r2[:, own(h)], t1[:, own(h)], cs("mhalf", S)[:, 0:HB], ALU.pow), "E_sso")
                yield from norm_pool(e, "F_", g, h)
                yield
                W(e, "F_xn", g, 1, h)
                inc(add_bias(x, x, "F_o", h), "F_xb")

            def after_f(g, h):
                yield from spread_recips_pool(e, "F_", g, h)
                yield from norm_pool(e, "G_", g, h)

            in_turn(late(before_e(0, 1)), before_e(0, 0))
            for u in range(NVU):
                e.memset(spread[:, u, :], 0.0)
            e.drain()

            def group_pool(g, last=False):
                self_pool(e, "E_", g, y)
                in_turn(after_e(g, 0), after_e(g, 1))
                e.memset(f_e[:, :, :, LC:LP], 0.0)
                e.drain()
                for b in range(NB):
                    own_q = slice(b * S, (b + 1) * S)
                    if b % HB == 0:
                        W(e, "F_qT", g, 1, b // HB)
                    if b:
                        W(e, "F_ql", g, b // HB + 1)
                    for c in range(DC):
                        if b >= 1:
                            W(e, "F_s", g, 8 * (b - 1) + 4 * (c + 1))
                        for dst, q in ((bd_hi, q_hi), (bd_lo, q_lo))[:2 if b else 1]:
                            ins = over_heads(e, dst, q, b, c)
                        inc(ins, "F_bd")
                in_turn(after_f(g, 0), after_f(g, 1))
                if not last:
                    in_turn(late(before_e(g + 1, 1)), before_e(g + 1, 0))

            with e.Fori(0, NG - 1) as g:
                group_pool(g)
            group_pool(NG - 1, True)

        @block.vector
        def _(e):
            e.sem_inc(m_hid.sem, m_hid.base)
            e.sem_inc(m_acc.sem, m_acc.base)
            e.sem_inc(m_out.sem, m_out.base)
            e.wait_ge(ld["cst"].sem, 16)
            lt = cs("log_temp")
            e.tensor_scalar(tempc[:, 0:1], lt, -1.0, None, ALU.mult)
            e.drain()
            e.tensor_tensor(tempc[:, 0:1], tempc[:, 0:1], lt, ALU.max).then_inc(prep_t.sem, 1)
            e.wait_ge(prep_e.sem, 1)
            e.tensor_scalar(tempc[:, 2:3], lt, 0.0, None, ALU.max)
            e.drain()
            e.tensor_tensor(tempc[:, 2:3], tempc[:, 2:3], tempc[:, 1:2], ALU.add)
            e.drain()
            e.tensor_scalar(tempc[:, 2:3], tempc[:, 2:3], 0.1, None, ALU.add)
            e.drain()
            e.reciprocal(tempc[:, 3:4], tempc[:, 2:3])
            e.drain()
            e.tensor_scalar(decay, cs("decay", S), tempc[0:S, 3:4], None, ALU.mult)
            e.wait_ge(ld["wq"].sem, 16)
            wq4 = experts[:, 0:4 * DC * D].rearrange("p (j n) -> p j n", j=4)
            e.tensor_reduce(wsum, wq4, AX, ALU.add, apply_absolute_value=True).then_inc(prep_abs.sem, 1)
            e.memset(b_e[:, :, LC:LP], 0.0)
            e.memset(a_sqw[:, :, SH:P], 0.0)
            e.memset(a_phiw[:, :, SH:P], 0.0)
            e.wait_ge(prep_sum.sem, 1)
            e.tensor_scalar(wscale, bank(0, n=4), 1.0 / (D * D), 1e-5, ALU.mult, ALU.max)
            e.drain()
            e.reciprocal(wrecip, wscale)
            e.drain()
            for j in range(4):
                e.tensor_scalar(wq4[:, j, :], wq4[:, j, :], wrecip[:, j:j + 1], MAGIC, ALU.mult, ALU.add)
            e.tensor_scalar(wscale[:, 0:1], wscale[:, 0:1], HD ** -0.5, None, ALU.mult)
            e.drain()
            e.tensor_scalar(wq4, wq4, MAGIC, 1.0, ALU.subtract, ALU.min)
            e.drain()
            e.tensor_scalar(wtern[:].rearrange("p j c n -> p j (c n)"), wq4, -1.0, None, ALU.max
                            ).then_inc(tern_go.sem, 1)
            e.wait_ge(ld["wt"].sem, 16)
            e.tensor_scalar(bq4, wt[:, WOFF["cols"][0] + COLS["F_bq"]:WOFF["cols"][0] + COLS["F_bq"] + 2],
                            HD ** -0.5, None, ALU.mult)

            def add_out(dst, b0, h):
                e.tensor_tensor(dst[:, own(h), :], tokens(b0), dst[:, own(h), :], ALU.add)
                e.drain()

            def before_c(g, h):
                b0, t, o = 4 * h, tok(h), own(h)
                if h == 0:
                    e.wait_ge(ld["x"].sem, g * 16 + 16)
                inc((yield from norm_dve(e, "A_", g, h, xin, xn)), "A_xn")
                yield
                W(e, "A_in_p", g, 1, h)
                if h == 0:
                    e.wait_ge(ld["rows"].sem, 16)
                inc(e.tensor_tensor(a_in[:, o, :], ps[0:S, b0 + 1:b0 + 3, 0:321],
                                    row("A_in").unsqueeze(1).broadcast_to([S, HB, 321]), ALU.add), "A_in")
                e.drain()
                e.tensor_tensor(a_sq[:, o, :], a_in[:, o, 0:SH], a_in[:, o, 0:SH], ALU.mult)
                e.drain()
                e.tensor_reduce(a_ss[:, o], a_sq[:, o, :], AX, ALU.add)
                e.drain()
                inc(e.tensor_scalar(a_ss[:, o], a_ss[:, o], 1e-24, None, ALU.max), "A_ss")
                yield
                W(e, "A_rn", g, 1, h)
                inc(e.tensor_tensor(a_sq[:, o, :], a_in[:, o, 0:SH],
                                    a_rn[:, o].unsqueeze(2).broadcast_to([S, HB, SH]), ALU.mult), "A_shn")
                yield
                W(e, "A_angp", g, 1, h)
                ang, turns = a_ang[:, t], a_k[:, t]
                e.tensor_scalar(ang, bank(b0 + 3, SH, HT), col("rb", 0, SH), col("half_pi", 0, SH), ALU.add, ALU.add)
                e.drain()
                e.tensor_scalar(turns, ang, 1.0 / (2 * math.pi), MAGIC, ALU.mult, ALU.add)
                e.drain()
                e.tensor_scalar(turns, turns, MAGIC, -1.0, ALU.subtract, ALU.mult)
                e.drain()
                e.scalar_tensor_tensor(ang, turns, TWO_PI_HI, ang, ALU.mult, ALU.add)
                e.drain()
                e.scalar_tensor_tensor(ang, turns, TWO_PI_LO, ang, ALU.mult, ALU.add)
                e.drain()
                inc(e.tensor_scalar(ang, ang, 3.1415925, -3.1415925, ALU.min, ALU.max), "A_ang")
                yield
                W(e, "A_comb", g, 1, h)
                W(e, "A_q", g, 1, h)
                phi = a_phi[:, o, :]
                qb = a_q[:, o].unsqueeze(2).broadcast_to([S, HB, SH])
                pm = lambda m: ps[0:S, b0 + 1:b0 + 3, m * SH:(m + 1) * SH]
                e.tensor_scalar(phi, pm(ORD - 1), MAGS[ORD - 1] / MAGS[ORD - 2], None, ALU.mult)
                e.drain()
                for m in range(ORD - 2, -1, -1):
                    if m == ORD - 2:
                        e.tensor_tensor(phi, phi, qb, ALU.mult)
                    else:
                        e.scalar_tensor_tensor(phi, phi, MAGS[m + 1] / MAGS[m], qb, ALU.mult, ALU.mult)
                    e.drain()
                    ins = e.tensor_tensor(phi, phi, pm(m), ALU.add)
                    if m:
                        e.drain()
                inc(ins, "A_phi")
                yield
                W(e, "A_lg", g, 1, h)
                lg = a_lg[:, o, :]
                e.tensor_tensor(lg, ps[0:S, b0 + 3, 0:HT].rearrange("p (b n) -> p b n", b=HB),
                                decay.unsqueeze(1).broadcast_to([S, HB, S]), ALU.mult)
                e.drain()
                e.tensor_tensor(lg, lg, cs("causal", S).unsqueeze(1).broadcast_to([S, HB, S]), ALU.add)
                e.drain()
                inc(e.tensor_reduce(a_nm[:, o], lg, AX, ALU.max, negate=True), "A_nm")
                yield
                W(e, "A_e", g, 1, h)
                e.reciprocal(a_rs[:, o], a_sum[:, o])
                e.drain()
                inc(e.tensor_tensor(lg, lg, a_rs[:, o].unsqueeze(2).broadcast_to([S, HB, S]), ALU.mult), "A_p")
                yield
                W(e, "A_out", g, 1, h)
                W(e, "A_xb", g, 1, h)
                add_out(x, b0 + 2, h)
                inc((yield from norm_dve(e, "B_", g, h, x, xn)), "B_xn")
                yield
                W(e, "B_qbkp", g, 1, h)
                e.tensor_scalar(b_qbk[:, o], bank(b0 + 3, S, HB), 1.0, None, ALU.mult)
                yield
                W(e, "B_s", g, 1, h)
                e.tensor_reduce(b_mx[:, o], ps[0:S, b0 + 1:b0 + 3, 0:LC], AX, ALU.max)
                e.drain()
                e.tensor_tensor(b_mx[:, o], b_mx[:, o], b_qbk[:, o], ALU.add)
                e.drain()
                inc(e.tensor_tensor(b_nm[:, o], b_qbk[:, o], b_mx[:, o], ALU.subtract), "B_nm")
                yield
                W(e, "B_e", g, 1, h)
                e.reciprocal(b_rs[:, o], b_sum[:, o])
                e.drain()
                for b in seqs(h):
                    ins = e.tensor_scalar(b_e[:, b, 0:LC], b_e[:, b, 0:LC], b_rs[:, b:b + 1], None, ALU.mult)
                inc(ins, "B_p")
                yield
                W(e, "B_out", g, 1, h)
                W(e, "B_xb", g, 1, h)
                add_out(x, b0 + 2, h)
                yield from norm_dve(e, "C_", g, h, x, y)
                e.drain()
                for b in seqs(h):
                    ins = e.tensor_scalar(xn[:, b, :], y[:, b, :], r2[:, b:b + 1], None, ALU.mult)
                inc(ins, "C_xn")
                yield
                W(e, "C_vp", g, 1, h)
                inc(e.tensor_scalar(c_v[:, o, :], tokens(b0 + 1), 1.0, None, ALU.mult), "C_v")

            def after_c(g, h):
                b0, t, o = 4 * h, tok(h), own(h)
                yield
                W(e, "C_rT", g, 1, h)
                inc(e.tensor_tensor(qT[:, :, t], ps[:, 6:8, t], hT[:, :, t], ALU.mult), "C_yT")
                yield
                W(e, "C_out", g, 1, h)
                W(e, "C_xb", g, 1, h)
                add_out(y, b0 + 1, h)
                inc((yield from norm_dve(e, "D_", g, h, y, xn)), "D_xn")
                e.tensor_tensor(xall[:, bass.ds(g * NB + HB * h, HB), :], x[:, o, :], y[:, o, :], ALU.add)
                e.drain()
                yield
                W(e, "D_hT", g, 1, h)
                for c in range(DC):
                    e.tensor_scalar(hT_all[:, c, bass.ds(g * NT + HT * h, HT)], hT[:, c, t], 1.0, None, ALU.mult)
                yield from gate_copy_dve(e, "D_", g, h, g_s[:, bass.ds(g * NB + HB * h, HB), :])

            with e.Fori(0, NG) as g:
                in_turn(before_c(g, 0), before_c(g, 1))
                self_dve(e, "C_", g)
                in_turn(after_c(g, 0), after_c(g, 1))
            e.drain()
            gate_shift_dve(e, NSEQ, g0_shifted, 0)
            for gi in range(NG):
                t = slice(gi * NT, (gi + 1) * NT)
                e.tensor_scalar(x_hi[:, :, t], hT_all[:, :, t], 1.0, None, ALU.mult)
                e.drain()
                e.tensor_tensor(x_lo[:, :, t], hT_all[:, :, t], x_hi[:, :, t], ALU.subtract).then_inc(m_x.sem, 1)
            e.drain()
            e.memset(hT_all[:], 0.0)

            def first_gates():
                scratch = gate_b[0:S].rearrange("p s g n -> p (s g n)")
                e.wait_ge(g0_e.sem, 1)
                gate_top_dve(e, NSEQ, False, gates_all[:], scratch[:, 0:64 * NSEQ], scratch[:, 64 * NSEQ:128 * NSEQ])

            def acc(ep, s, last=False):
                slot, gi = s // NG % 2, s % NG
                total = hT_all[:, :, gi * NT:(gi + 1) * NT]
                e.wait_ge(m_out.sem, m_out.at(ep, s + 1))
                e.tensor_tensor(gated[:], ps[:, 4 + 2 * (s % 2):6 + 2 * (s % 2), 0:NT],
                                gate_b[:, slot, gi, :].unsqueeze(1).broadcast_to([P, DC, NT]),
                                ALU.mult).then_inc(m_acc.sem, 1)
                e.drain()
                ins = e.tensor_tensor(total, total, gated[:], ALU.add)
                if last:
                    ins.then_inc(m_sum.sem, 1)

            def pair_gates(ep):
                for slot in range(2):
                    ins = e.tensor_scalar(gpair[:, slot, :], gates_all[:, :, bass.ds(2 * ep + slot, 1)].rearrange(
                        "p q o -> p (q o)"), 1.0, None, ALU.mult)
                ins.then_inc(m_gr.sem, 1)

            def experts_dve(ep, first=False):
                if not first:
                    pair_gates(ep)
                for s in range(2 * NG):
                    for m in range(MC0):
                        n = s * MC0 + m
                        e.wait_ge(m_act.sem, m_act.at(ep, n + 1))
                        if m == 0:
                            e.wait_ge(m_out.sem, m_out.at(ep, s - 1))
                        if n >= 2 or not first:
                            e.wait_ge(m_lo.sem, m_lo.at(ep, n - 1))
                        e.tensor_tensor(hid[:, n % 2, :], bank(2 + n % 2, n=NT), silu[:, n % 2, :], ALU.mult)
                        e.tensor_tensor(hid_hi[:, s % 2, m, :], bank(2 + n % 2, n=NT), silu[:, n % 2, :],
                                        ALU.mult).then_inc(m_hid.sem, 1)
                        if n == 1 and first:
                            first_gates()
                            pair_gates(ep)
                        if m == 1 and (s >= 1 or not first):
                            acc(ep, s - 1)

            experts_dve(0, True)
            with e.Fori(1, E0 // 2) as ep:
                experts_dve(ep)
            acc(E0 // 2, -1, True)
            def add_sum(pairs):
                for i in pairs:
                    e.wait_ge(m_back.sem, i + 1)
                    e.tensor_tensor(xall[:, 2 * i:2 * i + 2, :], ps[0:S, i, :].rearrange("p (b n) -> p b n", b=2),
                                    xall[:, 2 * i:2 * i + 2, :], ALU.add)
                    yield

            list(add_sum(range(HB)))
            e.drain()
            tq = xin

            def quantise(j, g, h):
                o = own(h)
                am, sc = q_am[:, o], q_sc[:, o]
                e.drain()
                e.tensor_reduce(am, tq[:, o, :], AX, ALU.max, apply_absolute_value=True)
                e.drain()
                e.tensor_scalar(am, am, 1e-5, None, ALU.max)
                e.drain()
                e.reciprocal(sc, am)
                e.tensor_scalar(q_isc[:, min(j, 2), o], am, 1.0 / 127.0, None, ALU.mult)
                e.drain()
                e.tensor_scalar(sc, sc, 127.0, None, ALU.mult)
                e.drain()
                for b in seqs(h):
                    e.tensor_scalar(tq[:, b, :], tq[:, b, :], q_sc[:, b:b + 1], MAGIC, ALU.mult, ALU.add)
                e.drain()
                if j >= 1:
                    W(e, "E_xqTp", g, j, h)
                ins = e.tensor_scalar(xq[:, o, :], tq[:, o, :], MAGIC, 127.0, ALU.subtract, ALU.min)
                if j < 2:
                    for b in seqs(h):
                        ins = e.tensor_scalar(y[:, b, 0:S], identS, q_isc[:, j, b:b + 1], None, ALU.mult)
                inc(ins, "E_xq")

            def before_e(g, h):
                t, o = tok(h), own(h)
                group = xall[:, bass.ds(g * NB, NB), :]

                def to_integers(j):
                    gain = ("gq", "gk", "gv")[j]
                    e.tensor_tensor(tq[:, o, :], xn[:, o, :], row(gain).unsqueeze(1).broadcast_to([S, HB, D]), ALU.mult)
                    quantise(j, g, h)

                def scale_back(j):
                    W(e, "E_pp", g, j + 1, h)
                    if j < 2:
                        ins = e.tensor_tensor((qT[:], keysT)[j][:, :, t], part(7),
                                              scales[:, j, t].unsqueeze(1).broadcast_to([P, DC, HT]), ALU.mult)
                    else:
                        for i, b in enumerate(seqs(h)):
                            ins = e.tensor_scalar(y[:, b, :], ps[0:S, 7, i * D:(i + 1) * D],
                                                  q_isc[:, 2, b:b + 1], wscale[0:S, 2:3], ALU.mult, ALU.mult)
                    inc(ins, "E_p")

                yield from norm_dve(e, "E_", g, h, group, xn)
                e.drain()
                to_integers(0)
                yield
                to_integers(1)
                yield
                scale_back(0)
                yield
                to_integers(2)
                yield
                scale_back(1)
                yield
                yield
                scale_back(2)

            def key_lo(g, b, i):
                W(e, "F_kh", g, 2 * b + i + 1)
                inc(e.scalar_tensor_tensor(k_lo[:, b % 2, i, :], bank(7, n=LE), col("F_bk", i), k_hi[:, b % 2, i, :],
                                           ALU.add, ALU.subtract), "F_kv")

            def value_evac(g, b, k):
                W(e, "F_kvp", g, 5 * b + DC + k + 1)
                inc(e.tensor_tensor(diag(3 * (b % 2) + k, KW),
                                    bank(7, KW, D).rearrange("p (c h d) -> p c h d", c=DC, h=HC),
                                    row("F_v", KW).rearrange("p (c h d) -> p c h d", c=DC, h=HC), ALU.add), "F_kv")

            def after_e(g, h):
                b0, t, o = 4 * h, tok(h), own(h)
                yield
                W(e, "E_rT", g, 1, h)
                inc(e.tensor_tensor(qT[:, :, t], ps[:, 6:8, t], hT[:, :, t], ALU.mult), "E_yT")
                yield
                W(e, "E_ytp", g, 1, h)
                e.tensor_scalar(y[:, o, :], tokens(b0 + 1), 1.0, None, ALU.mult)
                e.drain()
                e.tensor_tensor(tq[:, o, :], y[:, o, :], y[:, o, :], ALU.mult)
                e.drain()
                e.tensor_reduce(q_am[:, o], tq[:, o, :], AX, ALU.add)
                e.drain()
                inc(e.tensor_scalar(t1[:, o], q_am[:, o], 1.0 / D, EPS_RMS, ALU.mult, ALU.add), "E_ssr")
                if h == 1:
                    key_lo(g, 0, 0)
                    key_lo(g, 0, 1)
                yield
                W(e, "E_sso", g, 1, h)
                for b in seqs(h):
                    e.scalar_tensor_tensor(tq[:, b, :], y[:, b, :], r2[:, b:b + 1], row("go"), ALU.mult, ALU.mult)
                quantise(3, g, h)
                if h == 1:
                    value_evac(g, 0, 0)
                    value_evac(g, 0, 1)
                e.tensor_scalar(q_isc[:, 2, o], q_isc[:, 2, o], wscale[0:S, 3:4], None, ALU.mult)
                e.drain()
                yield
                W(e, "E_out", g, 1, h)
                if h == 0:
                    e.wait_ge(x_free.sem, g + 1)
                group = xall[:, bass.ds(g * NB, NB), :]
                for i, b in enumerate(seqs(h)):
                    e.scalar_tensor_tensor(x[:, b, :], ps[0:S, b0 + 1, i * D:(i + 1) * D],
                                           q_isc[:, 2, b:b + 1], group[:, b, :], ALU.mult, ALU.add)
                e.drain()
                if h == 1:
                    value_evac(g, 0, 2)
                inc((yield from norm_dve(e, "F_", g, h, x, xn)), "F_xn")

            def after_f(g, h):
                b0, t, o = 4 * h, tok(h), own(h)
                yield
                W(e, "F_rT", g, 1, h)
                W(e, "F_o", g, NB)
                inc(e.tensor_tensor(qT[:, :, t], hT[:, :, t], keysT[:, :, t], ALU.mult), "F_yT")
                yield
                W(e, "F_out", g, 1, h)
                W(e, "F_xb", g, 1, h)
                add_out(x, b0 + 1, h)
                inc((yield from norm_dve(e, "G_", g, h, x, xn)), "G_xn")
                yield from gate_copy_dve(e, "G_", g, h, g_s[:, own(h), :])

            in_turn(late(before_e(0, 1)), before_e(0, 0), add_sum([6, 7, 2, 3, 4, 5]))

            def group_dve(g, last=False):
                self_dve(e, "E_", g)
                in_turn(after_e(g, 0), after_e(g, 1))

                def query_lo(h):
                    W(e, "F_qT", g, 1, h)
                    inc(e.tensor_tensor(q_lo[:, :, tok(h)], qT[:, :, tok(h)], q_hi[:, :, tok(h)], ALU.subtract), "F_ql")

                query_lo(0)
                e.drain()
                inc(over_heads(e, bd_lo, q_lo, 0, 0), "F_bl")
                query_lo(1)
                inc(over_heads(e, bd_lo, q_lo, 0, 1), "F_bl")
                for n in range(8 * NB + 1):
                    b, v = divmod(n, 8)
                    if n < 8 * NB:
                        W(e, "F_s", g, n + 1)
                        if n >= 2:
                            W(e, "F_e", g, n - 1)
                        inc(e.tensor_reduce(h_nm[:, n % 2, 0:2], ps[0:S, 2 * (n % 2):2 * (n % 2) + 2, 0:LC], AX,
                                            ALU.max, negate=True), "F_nm")
                        if b + 1 < NB and v in (4, 5):
                            key_lo(g, b + 1, v - 4)
                    if n >= 1:
                        W(e, "F_pTp", g, n)
                        if n >= 3:
                            W(e, "F_av", g, n - 2)
                        inc(e.tensor_scalar(f_eT[:, (n - 1) % 2], ps[0:KW, 4:6, 0:KC * S], 1.0, None, ALU.mult), "F_pT")
                    if n < 8 * NB and b + 1 < NB and v >= 5:
                        value_evac(g, b + 1, v - 5)
                W(e, "F_e", g, 8 * NB)
                inc(e.reciprocal(h_rs, h_sum), "F_rs")
                in_turn(after_f(g, 0), after_f(g, 1))
                e.drain()
                if last:
                    in_turn(experts_g(g))
                else:
                    in_turn(late(before_e(g + 1, 1)), before_e(g + 1, 0), experts_g(g))

            def experts_g(g):
                gate_shift_dve(e, NB, g1_shifted, g)
                for j in range(E1 + 1):
                    if j == 1:
                        e.wait_ge(g1_e.sem, g1_e.at(g))
                        gate_top_dve(e, NB, True, gates_all[:, 0:NB, :], probs[:, 0, 0:NB * 64], probs[:, 1, 0:NB * 64])
                    if j < E1:
                        W(e, "G_act", g, j + 1)
                        if j >= 2:
                            W(e, "G_o", g, j - 1)
                        inc(e.tensor_tensor(g_hid[:, j % 2, :], bank(2 + j % 2, n=NT), g_act[:, j % 2, :],
                                            ALU.mult), "G_hid")
                    if j >= 1:
                        W(e, "G_o", g, j)
                        if j == E1:
                            ins = e.tensor_tensor(x[:], pair(4), x[:], ALU.add)
                        else:
                            for b in range(NB):
                                ins = e.scalar_tensor_tensor(
                                    x[:, b, :], ps[0:S, 4 + b // 2, (b % 2) * D:(b % 2 + 1) * D],
                                    gates_all[:, b, j - 1:j], x[:, b, :], ALU.mult, ALU.add)
                        inc(ins, "G_acc")
                        e.drain()
                    yield

            with e.Fori(0, NG - 1) as g:
                group_dve(g)
            group_dve(NG - 1, True)


def kernel(**inputs):
    import concourse.bacc as bacc
    from concourse.bass_utils import run_bass_kernel_spmd

    a = {k: np.asarray(v) for k, v in inputs.items()}
    f32 = np.float32

    def chunks(w):
        return np.ascontiguousarray(w.reshape(-1, P, w.shape[1]).transpose(1, 0, 2)).reshape(P, -1)

    wt = np.zeros((P, NW), f32)

    def put(name, v):
        o, n = WOFF[name]
        wt[:v.shape[0], o:o + n] = v

    put("A_in", chunks(np.concatenate([a["L0_attn_W_shell"].T, a["L0_attn_W_charge"].T, a["L0_attn_W_v"].T], 1)))
    put("A_omega", np.concatenate([a["L0_attn_omega"].T] * 2 + [np.zeros((SH, 2 * RF), f32)], 1))
    put("A_comb", a["L0_attn_W_combine"].reshape(SH, ORD, 2 * RF).transpose(2, 1, 0).reshape(2 * RF, ORD * SH))
    put("A_out", chunks(a["L0_attn_W_out"].T))
    put("B_q", chunks(a["L0_xattn_Wq"]))
    put("B_kT", chunks(a["L0_xattn_Wk"].T))
    put("B_bk", chunks(a["L0_xattn_bk"][:, None]))
    put("B_v", a["L0_xattn_Wv"])
    put("C_q", chunks(a["L0_ffn_wq"]))
    put("C_k", chunks(a["L0_ffn_wk"]))
    put("C_v", chunks(a["L0_ffn_wv"]))
    put("C_o", chunks(a["L0_ffn_wo"]))
    put("D_gate", chunks(a["L0_ffn_gate_w"]))
    put("F_q", chunks(a["L1_xattn_Wq"]))
    put("F_k", a["L1_xattn_Wk"])
    put("F_v", a["L1_xattn_Wv"])
    put("F_o", chunks(a["L1_xattn_Wo"]))
    put("G_gate", chunks(a["L1_ffn_gate_w"].T))

    def putcol(name, v):
        o = WOFF["cols"][0] + COLS[name]
        wt[:v.shape[0], o:o + v.shape[1]] = v

    putcol("rb", np.concatenate([a["L0_attn_rff_bias"]] * 2)[:, None])
    putcol("half_pi", np.full((RF, 1), math.pi / 2, f32))
    for name, key in (("B_bq", "L0_xattn_bq"), ("C_s", "L0_ffn_ln1_scale"), ("C_b", "L0_ffn_ln1_shift"),
                      ("D_s", "L0_ffn_ln2_scale"), ("D_b", "L0_ffn_ln2_shift"), ("F_bq", "L1_xattn_bq"),
                      ("F_bk", "L1_xattn_bk")):
        putcol(name, a[key].reshape(DC, P).T)
    rv = {"A_in": np.concatenate([a["L0_attn_b_shell"], a["L0_attn_b_charge"], a["L0_attn_b_v"]]),
          "A_out": a["L0_attn_b_out"], "B_v": a["L0_xattn_bv"], "C_o": a["L0_ffn_bo"], "F_v": a["L1_xattn_bv"],
          "F_o": a["L1_xattn_bo"], "gq": a["L1_attn_gq"], "gk": a["L1_attn_gk"], "gv": a["L1_attn_gv"],
          "go": a["L1_attn_go"]}
    rows = np.ascontiguousarray(np.broadcast_to(np.concatenate([rv[n] for n, _ in RCOLS])[None], (P, NR)))

    cst = np.zeros((P, NCST), f32)

    def putc(name, v):
        o, n = COFF[name]
        cst[:v.shape[0], o:o + n] = v

    i = np.arange(S)
    putc("ident", np.eye(P, dtype=f32))
    putc("ones", np.ones((P, P), f32))
    putc("decay", (np.exp(-0.03 * np.abs(i[:, None] - i[None, :])) * PHI_SCALE2).astype(f32))
    putc("causal", np.where(i[:, None] >= i[None, :], 0.0, NEG).astype(f32))
    putc("head", (np.arange(P)[:, None] // HD == np.arange(HC)[None, :]).astype(f32))
    putc("before", np.broadcast_to((np.arange(8)[None, :] < np.arange(8)[:, None]).astype(f32).reshape(1, 64), (P, 64)))
    putc("mhalf", np.full((P, 8), -0.5, f32))
    putc("eps", np.full((P, 4), EPS, f32))
    putc("log_temp", np.broadcast_to(a["L0_attn_log_temp"].reshape(1, 1), (P, 1)))

    c = a["ctx_512"].reshape(NG, NB, LC, DX)
    cpad = np.concatenate([c, np.zeros((NG, NB, LP - LC, DX), f32)], 2)
    arrays = {
        "x_d": np.ascontiguousarray(a["x"].reshape(NG, NB, S, D).transpose(0, 2, 1, 3)),
        "ctxT_d": np.ascontiguousarray(cpad.transpose(0, 3, 1, 2)),
        "ctx_d": np.ascontiguousarray(cpad.reshape(NG, NB, KC, KW, DX).transpose(0, 3, 1, 2, 4)),
        "w_d": wt, "r_d": rows, "c_d": cst,
        "wq_d": np.concatenate([chunks(a["L1_attn_" + n].T) for n in ("wq", "wk", "wv", "wo")], 1),
        "e0_d": np.stack([np.concatenate([chunks(a["L0_ffn_w1"][e]), chunks(a["L0_ffn_w2"][e]),
                                          chunks(a["L0_ffn_w3"][e])], 1) for e in range(E0)]),
        "e1_d": np.concatenate(
            [np.concatenate([chunks(a["L1_ffn_Wg"][e]), chunks(a["L1_ffn_Wu"][e]), a["L1_ffn_Wd"][e]], 1)
             for e in range(E1 - 1)]
            + [chunks(a["L1_ffn_sWg"]), chunks(a["L1_ffn_sWu"]), a["L1_ffn_sWd"]], 1),
    }
    nc = bacc.Bacc("TRN2", target_bir_lowering=False, num_devices=1)
    aps = [nc.dram_tensor(n, v.shape, F32, kind="ExternalInput").ap() for n, v in arrays.items()]
    out = nc.dram_tensor("out_0", (NG, S, NB, D), F32, kind="ExternalOutput").ap()
    decoder(nc, *aps, out)
    r = run_bass_kernel_spmd(nc, [arrays], core_ids=[0])
    return np.ascontiguousarray(r.results[0]["out_0"].reshape(NG, S, NB, D).transpose(0, 2, 1, 3)).reshape(NSEQ, S, D)
```
